# Optimizing a Trainium2 kernel written in Bass

```python
import numpy as np
import jax
import jax.numpy as jnp

def _softmax(x, axis=-1):
    return jax.nn.softmax(x, axis=axis)

def _gelu(x):
    return jax.nn.gelu(x, approximate=True)

def _silu(x):
    return jax.nn.silu(x)

def _sigmoid(x):
    return jax.nn.sigmoid(x)

def _layernorm(x, axis=-1, eps=1e-05):
    m = jnp.mean(x, axis=axis, keepdims=True)
    v = jnp.var(x, axis=axis, keepdims=True)
    return (x - m) / jnp.sqrt(v + eps)

def _scatter_add(tgt, idx, src, axis=0):
    return tgt.at[idx].add(src)

def _segment_sum(src, seg, n):
    return jax.ops.segment_sum(src, seg, n)
kernel_name = 'mk_cond_seq_d2_seqx_r2_14f5c3'

def setup_inputs(seed: int=0):
    np.random.seed(seed)
    _w = jnp.asarray

    def _rec_inputs():
        import jax
        import jax.numpy as jnp
        _rk = jax.random.key(seed)
        x = -0.0003929 + 0.9999 * jax.random.normal(jax.random.fold_in(_rk, 1), (2, 2048, 512), jnp.float32)
        _lenS = 2048 - jax.random.randint(jax.random.fold_in(_rk, 7), (2,), 0, max(1, 2048 // 4) + 1, jnp.int32)
        _lenS2 = 2048 - jax.random.randint(jax.random.fold_in(_rk, 8), (2,), 0, max(1, 2048 // 4) + 1, jnp.int32)
        cond_1024 = 0.0061147 + 1.02565 * jax.random.normal(jax.random.fold_in(_rk, 11), (2, 512), jnp.float32)
        return (x, cond_1024)
    x, cond_1024 = _rec_inputs()

    def _L0_cond_setup():
        import jax, jax.numpy as jnp
        import numpy as np
        B, S, D = (4, 2048, 512)
        H, K = (16, 64)
        DV = 512
        FINAL = H * K
        EPS_ATT = 1e-30
        EPS_LN = 1e-06
        key = jax.random.key(seed)
        ks = jax.random.split(key, 12)
        s = 0.02
        return {'inputs': jax.random.normal(ks[0], (B, S, D), jnp.float32), 'vector': jax.random.normal(ks[1], (B, DV), jnp.float32), 'attention_weights': jax.random.normal(ks[2], (D, H), jnp.float32) * s, 'temperature': jnp.ones((1, 1, H), jnp.float32), 'values': jax.random.normal(ks[3], (D, H, K), jnp.float32) * s, 'operator': jax.random.normal(ks[4], (FINAL, DV), jnp.float32) * s, 'ff1': jax.random.normal(ks[5], (DV + D, D), jnp.float32) * s, 'ff1_bias': jnp.zeros((1, 1, D), jnp.float32), 'ff2': jax.random.normal(ks[6], (D, D), jnp.float32) * s, 'ff2_bias': jnp.zeros((1, 1, D), jnp.float32), 'ln_gamma': jnp.ones((D,), jnp.float32), 'ln_beta': jnp.zeros((D,), jnp.float32)}
    _L0_cond_all = _L0_cond_setup()
    _L0_cond_in = {k: v for k, v in _L0_cond_all.items() if k in ('attention_weights', 'temperature', 'values', 'operator', 'ff1', 'ff1_bias', 'ff2', 'ff2_bias', 'ln_gamma', 'ln_beta')}
    del _L0_cond_all

    def _L1_cond_setup():
        import jax, jax.numpy as jnp
        import numpy as np
        D_MODEL = 512
        NHEAD = 16
        HEAD_DIM = D_MODEL // NHEAD
        D_FF = 2048
        EPS = 1e-05

        def _layernorm(x):
            mu = jnp.mean(x, axis=-1, keepdims=True)
            var = jnp.var(x, axis=-1, keepdims=True)
            return (x - mu) * jax.lax.rsqrt(var + EPS)
        key = jax.random.key(seed)
        ks = jax.random.split(key, 16)
        B, N = (4, 1024)
        s = 0.02
        inp = {'x': jax.random.normal(ks[0], (B, N, D_MODEL), jnp.float32), 'c': jax.random.normal(ks[1], (B, D_MODEL), jnp.float32), 'W_ada': jax.random.normal(ks[2], (D_MODEL, 6 * D_MODEL), jnp.float32) * s, 'b_ada': jnp.zeros((6 * D_MODEL,), jnp.float32), 'Wq': jax.random.normal(ks[3], (D_MODEL, D_MODEL), jnp.float32) * s, 'bq': jnp.zeros((D_MODEL,), jnp.float32), 'Wk': jax.random.normal(ks[4], (D_MODEL, D_MODEL), jnp.float32) * s, 'bk': jnp.zeros((D_MODEL,), jnp.float32), 'Wv': jax.random.normal(ks[5], (D_MODEL, D_MODEL), jnp.float32) * s, 'bv': jnp.zeros((D_MODEL,), jnp.float32), 'Wo': jax.random.normal(ks[6], (D_MODEL, D_MODEL), jnp.float32) * s, 'bo': jnp.zeros((D_MODEL,), jnp.float32), 'W1': jax.random.normal(ks[7], (D_MODEL, D_FF), jnp.float32) * s, 'b1': jnp.zeros((D_FF,), jnp.float32), 'W2': jax.random.normal(ks[8], (D_FF, D_MODEL), jnp.float32) * s, 'b2': jnp.zeros((D_MODEL,), jnp.float32)}
        return inp
    _L1_cond_all = _L1_cond_setup()
    _L1_cond_in = {k: v for k, v in _L1_cond_all.items() if k in ('W_ada', 'b_ada', 'Wq', 'bq', 'Wk', 'bk', 'Wv', 'bv', 'Wo', 'bo', 'W1', 'b1', 'W2', 'b2')}
    del _L1_cond_all
    return {'x': x, 'cond_1024': cond_1024, 'L0_cond_attention_weights': _L0_cond_in['attention_weights'], 'L0_cond_temperature': _L0_cond_in['temperature'], 'L0_cond_values': _L0_cond_in['values'], 'L0_cond_operator': _L0_cond_in['operator'], 'L0_cond_ff1': _L0_cond_in['ff1'], 'L0_cond_ff1_bias': _L0_cond_in['ff1_bias'], 'L0_cond_ff2': _L0_cond_in['ff2'], 'L0_cond_ff2_bias': _L0_cond_in['ff2_bias'], 'L0_cond_ln_gamma': _L0_cond_in['ln_gamma'], 'L0_cond_ln_beta': _L0_cond_in['ln_beta'], 'L1_cond_W_ada': _L1_cond_in['W_ada'], 'L1_cond_b_ada': _L1_cond_in['b_ada'], 'L1_cond_Wq': _L1_cond_in['Wq'], 'L1_cond_bq': _L1_cond_in['bq'], 'L1_cond_Wk': _L1_cond_in['Wk'], 'L1_cond_bk': _L1_cond_in['bk'], 'L1_cond_Wv': _L1_cond_in['Wv'], 'L1_cond_bv': _L1_cond_in['bv'], 'L1_cond_Wo': _L1_cond_in['Wo'], 'L1_cond_bo': _L1_cond_in['bo'], 'L1_cond_W1': _L1_cond_in['W1'], 'L1_cond_b1': _L1_cond_in['b1'], 'L1_cond_W2': _L1_cond_in['W2'], 'L1_cond_b2': _L1_cond_in['b2']}

def reference(x, cond_1024, L0_cond_attention_weights, L0_cond_temperature, L0_cond_values, L0_cond_operator, L0_cond_ff1, L0_cond_ff1_bias, L0_cond_ff2, L0_cond_ff2_bias, L0_cond_ln_gamma, L0_cond_ln_beta, L1_cond_W_ada, L1_cond_b_ada, L1_cond_Wq, L1_cond_bq, L1_cond_Wk, L1_cond_bk, L1_cond_Wv, L1_cond_bv, L1_cond_Wo, L1_cond_bo, L1_cond_W1, L1_cond_b1, L1_cond_W2, L1_cond_b2):
    import jax
    import jax.numpy as jnp

    def _L0_cond_ref(inputs, vector, attention_weights, temperature, values, operator, ff1, ff1_bias, ff2, ff2_bias, ln_gamma, ln_beta):
        import jax, jax.numpy as jnp
        import numpy as np
        B, S, D = (4, 2048, 512)
        H, K = (16, 64)
        DV = 512
        FINAL = H * K
        EPS_ATT = 1e-30
        EPS_LN = 1e-06
        att = inputs @ attention_weights
        att = att - jnp.max(att, axis=1, keepdims=True)
        att = jnp.exp(att * temperature)
        v = jnp.einsum('bsi,ihk->bshk', inputs, values)
        cumv = jnp.cumsum(v, axis=1)
        counts = jnp.arange(1, S + 1, dtype=inputs.dtype)[None, :, None]
        denom = att * counts + EPS_ATT
        attn_out = att[..., None] * cumv / denom[..., None]
        attn_out = attn_out.reshape(attn_out.shape[0], S, FINAL)
        op = attn_out @ operator + vector[:, None, :]
        concat = jnp.concatenate([inputs, op], axis=-1)
        res = jax.nn.relu(concat @ ff1 + ff1_bias)
        res = res @ ff2 + ff2_bias + inputs
        mu = jnp.mean(res, axis=-1, keepdims=True)
        var = jnp.mean(jnp.square(res - mu), axis=-1, keepdims=True)
        xhat = (res - mu) * jax.lax.rsqrt(var + EPS_LN)
        return xhat * ln_gamma + ln_beta

    def _L1_cond_ref(x, c, W_ada, b_ada, Wq, bq, Wk, bk, Wv, bv, Wo, bo, W1, b1, W2, b2):
        import jax, jax.numpy as jnp
        import numpy as np
        D_MODEL = 512
        NHEAD = 16
        HEAD_DIM = D_MODEL // NHEAD
        D_FF = 2048
        EPS = 1e-05

        def _layernorm(x):
            mu = jnp.mean(x, axis=-1, keepdims=True)
            var = jnp.var(x, axis=-1, keepdims=True)
            return (x - mu) * jax.lax.rsqrt(var + EPS)
        B, N, _ = x.shape
        ada = (c @ W_ada + b_ada)[:, None, :]
        shift1, scale1, gate1, shift2, scale2, gate2 = jnp.split(ada, 6, axis=-1)
        h = _layernorm(x) * (1.0 + scale1) + shift1
        Q = (h @ Wq + bq).reshape(B, N, NHEAD, HEAD_DIM)
        K = (h @ Wk + bk).reshape(B, N, NHEAD, HEAD_DIM)
        V = (h @ Wv + bv).reshape(B, N, NHEAD, HEAD_DIM)
        scores = jnp.einsum('bqhd,bkhd->bhqk', Q, K) / np.sqrt(HEAD_DIM).astype(np.float32)
        attn = jax.nn.softmax(scores, axis=-1)
        attn_out = jnp.einsum('bhqk,bkhd->bqhd', attn, V).reshape(B, N, D_MODEL)
        attn_out = attn_out @ Wo + bo
        x = x + gate1 * attn_out
        h = _layernorm(x) * (1.0 + scale2) + shift2
        ff = jax.nn.gelu(h @ W1 + b1, approximate=False) @ W2 + b2
        return x + gate2 * ff
    x = _L0_cond_ref(x, cond_1024, L0_cond_attention_weights, L0_cond_temperature, L0_cond_values, L0_cond_operator, L0_cond_ff1, L0_cond_ff1_bias, L0_cond_ff2, L0_cond_ff2_bias, L0_cond_ln_gamma, L0_cond_ln_beta)
    x = _L1_cond_ref(x, cond_1024, L1_cond_W_ada, L1_cond_b_ada, L1_cond_Wq, L1_cond_bq, L1_cond_Wk, L1_cond_bk, L1_cond_Wv, L1_cond_bv, L1_cond_Wo, L1_cond_bo, L1_cond_W1, L1_cond_b1, L1_cond_W2, L1_cond_b2)
    return x

_drawn_inputs = setup_inputs


def setup_inputs(seed=0):
    import zlib

    import numpy as np

    out = dict(_drawn_inputs(seed))
    spreads = {'L0_cond_temperature': (1.0, 0.6),
     'L0_cond_ff1_bias': (0.0, 0.1),
     'L0_cond_ff2_bias': (0.0, 0.1),
     'L0_cond_ln_gamma': (1.0, 0.2),
     'L0_cond_ln_beta': (0.0, 0.1),
     'L1_cond_b_ada': (0.0, 0.1),
     'L1_cond_bq': (0.0, 0.8),
     'L1_cond_bk': (0.0, 2.0),
     'L1_cond_bv': (0.0, 0.4),
     'L1_cond_bo': (0.0, 0.1),
     'L1_cond_b1': (0.0, 0.35),
     'L1_cond_b2': (0.0, 0.1)}
    factors = {'L0_cond_attention_weights': 64.0,
     'L0_cond_values': 8.0,
     'L0_cond_operator': 8.0,
     'L1_cond_Wq': 8.0,
     'L1_cond_Wk': 8.0}
    for name, (base, spread) in spreads.items():
        noise = np.random.default_rng([zlib.crc32(name.encode()), seed]).standard_normal(out[name].shape)
        drawn = base * np.exp(spread * noise) if base else spread * noise
        out[name] = jnp.asarray(drawn.astype(out[name].dtype))
    for name, factor in factors.items():
        out[name] = (out[name] * factor).astype(out[name].dtype)
    return out
```

```python
import numpy as np
from contextlib import ExitStack

import concourse.bass as bass
from concourse import mybir

F32 = mybir.dt.float32
F16 = mybir.dt.float16
ACT = mybir.ActivationFunctionType
ALU = mybir.AluOpType
AX = mybir.AxisListType
RMAX = bass.bass_isa.ReduceOp.max

P = 128
B, S, D = 2, 2048, 512
T = B * S
H0, K0 = 16, 64
HK = H0 * K0
H1, DH = 16, 32
FF = 2048
CH = 512
NCH = T // CH
CPB = S // CH
KD = D // P
KH = HK // P
TPC = CH // P
TPB = S // P
NADA = 6 * D
WS = 64.0
EPS_ATT, EPS_LN0, EPS_LN1 = 1e-30, 1e-6, 1e-5


class Memory:

    def __init__(self, nc, stack):
        self.nc, self.stack = nc, stack
        self.sems = []
        stack.callback(self.clear_sems)

    def sb(self, name, shape, dt=F32):
        return self.stack.enter_context(self.nc.sbuf_tensor(name, shape, dt))

    def ps(self, name, shape=(P, CH), dt=F32):
        return self.stack.enter_context(self.nc.psum_tensor(name, list(shape), dt))

    def sem(self, name):
        self.sems.append(self.nc.alloc_semaphore(name))
        return self.sems[-1]

    def clear_sems(self):
        if self.sems:
            self.nc.clear_and_free_semaphores(self.sems)
            self.nc.all_engine_barrier()


def split_weight_tiles(w, cols):
    v = w.rearrange("(k p) n -> p k n", p=P)
    return [v[:, :, c:c + cols] for c in range(0, w.shape[1], cols)]


def combine_moments(nc, dve, stats, mv, diff, stats_done, stats_before, mv_done, mv_before):
    halves = stats[:].rearrange("p t (h m) -> p t m h", h=2)
    dve.wait_ge(stats_done, stats_before + TPC)
    nc.vector.tensor_tensor(diff[:], halves[:, :, 1, 0], halves[:, :, 1, 1], ALU.subtract).then_inc(mv_done, 1)
    nc.vector.tensor_tensor(mv[:], halves[:, :, 1:3, 0], halves[:, :, 1:3, 1], ALU.add).then_inc(mv_done, 1)
    dve.wait_ge(mv_done, mv_before + 2)
    nc.vector.tensor_tensor(diff[:], diff[:], diff[:], ALU.mult).then_inc(mv_done, 1)
    dve.wait_ge(mv_done, mv_before + 3)
    nc.vector.scalar_tensor_tensor(mv[:, :, 1], diff[:], D / 4, mv[:, :, 1], ALU.mult, ALU.add).then_inc(mv_done, 1)


def bcast_rows(vec, n=P):
    return vec.partition_broadcast(n)


def phase_prepare(nc, a, s, w):
    with ExitStack() as stack:
        m = Memory(nc, stack)
        QT = 4
        NQ = TPB // QT
        ident = m.sb("p_ident", [P, P])
        inv_counts = m.sb("p_inv_counts", [P, S])
        counts = m.sb("p_counts", [P, TPB])
        ones = m.sb("p_ones", [P, 1])
        x_tok = m.sb("p_x_tok", [P, 2, TPB, P])
        xT = m.sb("p_xT", [P, 2, S])
        x_hi = m.sb("p_x_hi", [P, 2, S], F16)
        x_lo = m.sb("p_x_lo", [P, 2, S], F16)
        c32 = m.sb("p_c32", [P, S])
        c_hi = m.sb("p_c_hi", [P, 2, S], F16)
        c_lo = m.sb("p_c_lo", [P, 2, S], F16)
        aw = m.sb("p_aw", [P, KD, H0])
        aw_hi = m.sb("p_aw_hi", [P, KD, H0], F16)
        aw_lo = m.sb("p_aw_lo", [P, KD, H0], F16)
        temp = m.sb("p_temp", [P, H0])
        mx = m.sb("p_mx", [P, H0])
        mxa = m.sb("p_mxa", [P, H0])
        att = m.sb("p_att", [P, TPB, H0])
        atc = m.sb("p_atc", [P, TPB, H0])
        gate = m.sb("p_gate", [P, B, TPB, H0])
        gT = c32[0:H0, :]
        gT_hi = m.sb("p_gT_hi", [H0, S], F16)
        gT_lo = m.sb("p_gT_lo", [H0, S], F16)
        stage = m.sb("p_stage", [P, 2, 2048])
        oper = x_tok[:].rearrange("p r t f -> p (r t f)").rearrange("p (k n) -> p k n", n=D)
        operT = xT[:].rearrange("p r t -> p (r t)").rearrange("p (k n) -> p k n", n=HK)
        ff1b = m.sb("p_ff1b", [P, KD, D])
        of32 = m.sb("p_of32", [P, 2, D])
        condT = m.sb("p_condT", [P, KD, B])
        ff1_bias = m.sb("p_ff1_bias", [P, KD])
        ada = m.sb("p_ada", [B, 2, CH])
        b_ada = m.sb("p_b_ada", [B, 2, CH])

        psT = [m.ps(f"p_psT{i}") for i in range(2)]
        psA = m.ps("p_psA")
        psG = m.ps("p_psG")
        psW = [m.ps(f"p_psW{i}") for i in range(2)]
        psD = m.ps("p_psD")
        psB = m.ps("p_psB")

        consts_in = m.sem("p_consts_in")
        aw_in = m.sem("p_aw_in")
        x_in = [m.sem(f"p_x_in{i}") for i in range(2)]
        w_in = [m.sem(f"p_w_in{i}") for i in range(2)]
        oper_in = m.sem("p_oper_in")
        ada_in = [m.sem(f"p_ada_in{i}") for i in range(2)]
        b_ada_in = [m.sem(f"p_b_ada_in{i}") for i in range(2)]
        small_in = m.sem("p_small_in")
        aw_split = m.sem("p_aw_split")
        temp_scaled = m.sem("p_temp_scaled")
        x_turned = m.sem("p_x_turned")
        xT_written = m.sem("p_xT_written")
        x_lo_done = m.sem("p_x_lo_done")
        scanned = m.sem("p_scanned")
        meaned = m.sem("p_meaned")
        c_hi_done = m.sem("p_c_hi_done")
        c_lo_done = m.sem("p_c_lo_done")
        stored = [m.sem(f"p_stored{i}") for i in range(2)]
        att_done = m.sem("p_att_done")
        mx_done = m.sem("p_mx_done")
        mx_all = m.sem("p_mx_all")
        att_step = m.sem("p_att_step")
        att_arg = m.sem("p_att_arg")
        att_exp = m.sem("p_att_exp")
        gate_done = m.sem("p_gate_done")
        g_turned = m.sem("p_g_turned")
        gT_written = m.sem("p_gT_written")
        gT_lo_done = m.sem("p_gT_lo_done")
        g_stored = m.sem("p_g_stored")
        w64_done = m.sem("p_w64_done")
        w_hi_done = m.sem("p_w_hi_done")
        w_lo_done = m.sem("p_w_lo_done")
        oper_turned = m.sem("p_oper_turned")
        operT_written = m.sem("p_operT_written")
        of_mm = m.sem("p_of_mm")
        of_written = m.sem("p_of_written")
        of_lo_done = m.sem("p_of_lo_done")
        b1_mm = m.sem("p_b1_mm")
        b1_done = m.sem("p_b1_done")
        ada_mm = m.sem("p_ada_mm")
        ada_done = m.sem("p_ada_done")
        ada_stored = m.sem("p_ada_stored")

        x_v = a["x"].rearrange("b (t p) (k f) -> b k p t f", p=P, f=P)

        pieces = []
        for name, hi, lo in (("L0_cond_values", "val_hi", "val_lo"), ("L0_cond_ff1", "f1_hi", "f1_lo"),
                             ("L0_cond_ff2", "f2_hi", "f2_lo"), ("L1_cond_Wq", "wq_hi", "wq_lo"),
                             ("L1_cond_Wk", "wk_hi", "wk_lo"), ("L1_cond_Wv", "wv_hi", "wv_lo")):
            src = a[name]
            if name == "L0_cond_values":
                src = src.rearrange("i h k -> i (h k)")
            if name == "L0_cond_ff1":
                src = src[0:D, :]
            for c, part in enumerate(split_weight_tiles(src, CH)):
                pieces.append((part, w[hi][:, :, c * CH:(c + 1) * CH], w[lo][:, :, c * CH:(c + 1) * CH]))

        block = stack.enter_context(nc.Block())

        @block.sync
        def _(sp):
            sp.dma_start(ident[:], a["c_ident"]).then_inc(consts_in, 16)
            sp.dma_start(counts[:], a["c_counts"]).then_inc(consts_in, 16)
            sp.dma_start(inv_counts[:], bcast_rows(a["c_inv_counts"])).then_inc(consts_in, 16)
            sp.dma_start(aw[:], a["L0_cond_attention_weights"].rearrange("(k p) n -> p k n", p=P)).then_inc(aw_in, 16)
            sp.dma_start(temp[:], bcast_rows(a["L0_cond_temperature"].rearrange("a b h -> (a b h)"))).then_inc(aw_in, 16)

            def load_x(b, p):
                sp.dma_start(x_tok[:, p % 2], x_v[b, p]).then_inc(x_in[p % 2], 16)

            def store(b, p, n):
                r = p % 2
                cols = [x_hi, x_lo, c_hi, c_lo]
                sp.wait_ge(xT_written, (n + 1) * 2 * NQ)
                sp.wait_ge(x_lo_done, n + 1)
                sp.wait_ge(c_hi_done, (n + 1) * 2)
                sp.wait_ge(c_lo_done, (n + 1) * 2)
                for name, t in zip(("x_hi", "x_lo", "c_hi", "c_lo"), cols):
                    dst = s[name].rearrange("(b c) p k t -> b k p c t", b=B)[b, p]
                    sp.dma_start(dst, t[:, r].rearrange("p (c t) -> p c t", c=CPB)).then_inc(stored[r], 16)

            load_x(0, 0)
            load_x(0, 1)
            for p in range(2, KD):
                sp.wait_ge(x_turned, (p - 1) * NQ)
                load_x(0, p)
                store(0, p - 2, p - 2)
            for p in range(2):
                sp.wait_ge(x_turned, (KD + p - 1) * NQ)
                load_x(1, p)
                store(0, KD - 2 + p, KD - 2 + p)
            for p in range(2, KD):
                sp.wait_ge(x_turned, (KD + p - 1) * NQ)
                load_x(1, p)
                store(1, p - 2, KD + p - 2)
            for p in range(KD - 2, KD):
                store(1, p, KD + p)
            for i in range(2):
                sp.wait_ge(stored[i], 16 * 4 * KD)
            for b in range(B):
                sp.wait_ge(gT_written, 2 * NQ * (b + 1))
                sp.wait_ge(gT_lo_done, b + 1)
                for half, t in enumerate((gT_hi, gT_lo)):
                    sp.dma_start(s["g"][b * CPB:(b + 1) * CPB].rearrange("c h t -> h c t")[half * H0:(half + 1) * H0],
                                 t[:].rearrange("h (c t) -> h c t", c=CPB)).then_inc(g_stored, 16)
            sp.wait_ge(g_stored, 16 * 2 * B)
            for n in range(NADA // CH):
                sp.wait_ge(ada_done, n + 1)
                sp.dma_start(s["ada"][:, n * CH:(n + 1) * CH], ada[:, n % 2]).then_inc(ada_stored, 16)
                sp.wait_ge(ada_stored, 16 * (n + 1))

        @block.gpsimd
        def _(pool):
            pool.dma_start(ff1b[:], a["L0_cond_ff1"][D:2 * D, :].rearrange("(k p) n -> p k n", p=P)).then_inc(oper_in, 16)
            for b in range(B):
                pool.dma_start(condT[:, :, b], a["cond_1024"][b].rearrange("(k p) -> p k", p=P), allow_slow_non_contiguous=True).then_inc(small_in, 16)
            pool.dma_start(ff1_bias[:], a["L0_cond_ff1_bias"].rearrange("a b (k p) -> p (a b k)", p=P), allow_slow_non_contiguous=True).then_inc(small_in, 16)
            for n in range(2):
                pool.dma_start(stage[:, n].rearrange("p (k c) -> p k c", k=KD), pieces[n][0]).then_inc(w_in[n], 16)
            for b in range(B):
                pool.wait_ge(mx_done, b + 1)
                if b == B - 1:
                    pool.wait_ge(x_turned, B * KD * NQ)
                    pool.dma_start(oper, a["L0_cond_operator"].rearrange("(k p) n -> p k n", p=P)).then_inc(oper_in, 16)
                nc.gpsimd.partition_all_reduce(mxa[:], mx[:], P, RMAX).then_inc(mx_all, 1)
            for n, (_, hi, lo) in enumerate(pieces):
                pool.wait_ge(w_hi_done, n + 1)
                pool.wait_ge(w64_done, n + 1)
                nc.gpsimd.tensor_tensor(lo, stage[:, n % 2].rearrange("p (k c) -> p k c", k=KD), hi,
                                        ALU.subtract).then_inc(w_lo_done, 1)
                if n + 2 < len(pieces):
                    pool.wait_ge(w_lo_done, n + 1)
                    pool.dma_start(stage[:, n % 2].rearrange("p (k c) -> p k c", k=KD),
                                   pieces[n + 2][0]).then_inc(w_in[n % 2], 16)
            ada_v = split_weight_tiles(a["L1_cond_W_ada"], CH)
            for n in range(NADA // CH):
                r = n % 2
                if n >= 2:
                    pool.wait_ge(ada_mm, n - 1)
                    pool.wait_ge(ada_done, n - 1)
                else:
                    pool.wait_ge(w_lo_done, len(pieces))
                pool.dma_start(stage[:, r].rearrange("p (k c) -> p k c", k=KD), ada_v[n]).then_inc(ada_in[r], 16)
                pool.dma_start(b_ada[:, r], bcast_rows(a["L1_cond_b_ada"][n * CH:(n + 1) * CH], B)).then_inc(b_ada_in[r], 16)

        @block.scalar
        def _(act):
            act.wait_ge(aw_in, 32)
            nc.scalar.activation(aw_hi[:], aw[:], ACT.Identity, scale=WS).then_inc(aw_split, 1)
            nc.scalar.mul(temp[:], temp[:], 1.0 / WS).then_inc(temp_scaled, 1)

            def unit(b, p, n):
                r = p % 2
                for q in range(NQ):
                    act.wait_ge(x_turned, n * NQ + q + 1)
                    if q == 0:
                        if not (isinstance(b, int) and b == 0 and p < 2):
                            act.wait_ge(scanned, n - 1)
                            act.wait_ge(x_lo_done, n - 1)
                            act.wait_ge(att_done, n - 1)
                            act.wait_ge(stored[r], 16 * 4 * (2 * b + p // 2))
                    cols = slice(q * CH, (q + 1) * CH)
                    nc.scalar.copy(xT[:, r, cols], psT[q % 2][:]).then_inc(xT_written, 1)
                    nc.scalar.copy(x_hi[:, r, cols], psT[q % 2][:]).then_inc(xT_written, 1)
                for h in range(2):
                    act.wait_ge(meaned, 2 * n + h + 1)
                    half = slice(h * S // 2, (h + 1) * S // 2)
                    nc.scalar.copy(c_hi[:, r, half], c32[:, half]).then_inc(c_hi_done, 1)

            for b in range(B):
                for p in range(KD):
                    unit(b, p, b * KD + p)
                act.wait_ge(att_arg, b + 1)
                nc.scalar.activation(att[:], att[:], ACT.Exp).then_inc(att_exp, 1)
            for n, (_, hi, lo) in enumerate(pieces):
                v = stage[:, n % 2].rearrange("p (k c) -> p k c", k=KD)
                act.wait_ge(w_in[n % 2], 16 * (n // 2 + 1))
                nc.scalar.activation(hi, v, ACT.Identity, scale=WS).then_inc(w_hi_done, 1)
                act.wait_ge(w_hi_done, n + 1)
                nc.scalar.activation(v, v, ACT.Identity, scale=WS).then_inc(w64_done, 1)
                if n == 1:
                    act.wait_ge(scanned, B * KD)
                    act.wait_ge(x_lo_done, B * KD)
                    for i in range(2 * KD):
                        act.wait_ge(oper_turned, i + 1)
                        k, half = i // 2, i % 2
                        nc.scalar.copy(operT[:, k, half * CH:(half + 1) * CH], psT[i % 2][:]).then_inc(operT_written, 1)
                    for j in range(KH):
                        act.wait_ge(of_mm, j + 1)
                        if j >= 2:
                            act.wait_ge(of_lo_done, j - 1)
                        nc.scalar.activation(w["of_hi"][:, j], psW[j % 2][:], ACT.Identity, scale=WS).then_inc(of_written, 1)
                        nc.scalar.activation(of32[:, j % 2], psW[j % 2][:], ACT.Identity, scale=WS).then_inc(of_written, 1)
                    act.wait_ge(c_lo_done, 2 * B * KD)
                    for b in range(B):
                        for q in range(NQ):
                            act.wait_ge(g_turned, b * NQ + q + 1)
                            if b == 1 and q == 0:
                                act.wait_ge(gT_lo_done, 1)
                                act.wait_ge(g_stored, 32)
                            cols = slice(q * CH, (q + 1) * CH)
                            nc.scalar.copy(gT[:, cols], psG[0:H0, :]).then_inc(gT_written, 1)
                            nc.scalar.copy(gT_hi[:, cols], psG[0:H0, :]).then_inc(gT_written, 1)

        @block.vector
        def _(dve):
            nc.vector.memset(ones[:], 1.0).then_inc(att_step, 1)
            dve.wait_ge(aw_split, 1)
            nc.vector.scalar_tensor_tensor(aw_lo[:], aw[:], WS, aw_hi[:], ALU.mult, ALU.subtract).then_inc(aw_split, 1)
            dve.wait_ge(consts_in, 48)
            dve.wait_ge(att_step, 1)

            def unit(b, p, n):
                r = p % 2
                dve.wait_ge(xT_written, (n + 1) * 2 * NQ)
                nc.vector.tensor_tensor(x_lo[:, r], xT[:, r], x_hi[:, r], ALU.subtract).then_inc(x_lo_done, 1)
                if n >= 1:
                    dve.wait_ge(c_lo_done, 2 * n)
                    dve.wait_ge(c_hi_done, 2 * n)
                nc.vector.tensor_tensor_scan(c32[:], ones[:, 0:1].to_broadcast([P, S]), xT[:, r], 0.0,
                                             ALU.mult, ALU.add).then_inc(scanned, 1)
                dve.wait_ge(scanned, n + 1)
                for h in range(2):
                    half = slice(h * S // 2, (h + 1) * S // 2)
                    nc.vector.tensor_tensor(c32[:, half], c32[:, half], inv_counts[:, half],
                                            ALU.mult).then_inc(meaned, 1)
                for h in range(2):
                    half = slice(h * S // 2, (h + 1) * S // 2)
                    dve.wait_ge(meaned, 2 * n + h + 1)
                    dve.wait_ge(c_hi_done, 2 * n + h + 1)
                    nc.vector.tensor_tensor(c_lo[:, r, half], c32[:, half], c_hi[:, r, half],
                                            ALU.subtract).then_inc(c_lo_done, 1)

            for b in range(B):
                for p in range(KD):
                    unit(b, p, b * KD + p)
                step = 1 + 4 * b
                dve.wait_ge(att_done, KD * (b + 1))
                scores = psA[:, 0:TPB * H0].rearrange("p (t h) -> p t h", h=H0)
                if b >= 1:
                    dve.wait_ge(mx_all, b)
                nc.vector.tensor_reduce(mx[:], scores.rearrange("p t h -> p h t"), AX.X, ALU.max).then_inc(mx_done, 1)
                dve.wait_ge(mx_all, b + 1)
                if b >= 1:
                    dve.wait_ge(gate_done, b)
                nc.vector.tensor_tensor(att[:], scores, mxa[:].unsqueeze(1).to_broadcast([P, TPB, H0]),
                                        ALU.subtract).then_inc(att_step, 1)
                dve.wait_ge(att_step, step + 1)
                dve.wait_ge(temp_scaled, 1)
                nc.vector.tensor_tensor(att[:], att[:], temp[:].unsqueeze(1).to_broadcast([P, TPB, H0]),
                                        ALU.mult).then_inc(att_arg, 1)
                dve.wait_ge(att_exp, b + 1)
                nc.vector.tensor_tensor(atc[:], att[:], counts[:].unsqueeze(2).to_broadcast([P, TPB, H0]),
                                        ALU.mult).then_inc(att_step, 1)
                dve.wait_ge(att_step, step + 2)
                nc.vector.tensor_scalar_add(att[:], atc[:], EPS_ATT).then_inc(att_step, 1)
                dve.wait_ge(att_step, step + 3)
                nc.vector.reciprocal(att[:], att[:]).then_inc(att_step, 1)
                dve.wait_ge(att_step, step + 4)
                nc.vector.tensor_tensor(gate[:, b], atc[:], att[:], ALU.mult).then_inc(gate_done, 1)
            for j in range(KH):
                dve.wait_ge(of_written, 2 * (j + 1))
                nc.vector.tensor_tensor(w["of_lo"][:, j], of32[:, j % 2], w["of_hi"][:, j],
                                        ALU.subtract).then_inc(of_lo_done, 1)
            dve.wait_ge(b1_mm, 1)
            dve.wait_ge(small_in, 48)
            for b in range(B):
                nc.vector.tensor_tensor(w["b1"][:, :, b * CPB:(b + 1) * CPB],
                                        psB[:, b:KD * B:B].unsqueeze(2).to_broadcast([P, KD, CPB]),
                                        ff1_bias[:].unsqueeze(2).to_broadcast([P, KD, CPB]), ALU.add).then_inc(b1_done, 1)
            for b in range(B):
                dve.wait_ge(gT_written, 2 * NQ * (b + 1))
                if b == 1:
                    dve.wait_ge(g_stored, 32)
                nc.vector.tensor_tensor(gT_lo[:], gT, gT_hi[:], ALU.subtract).then_inc(gT_lo_done, 1)
            for n in range(NADA // CH):
                dve.wait_ge(ada_mm, n + 1)
                dve.wait_ge(b_ada_in[n % 2], 16 * (n // 2 + 1))
                if n >= 2:
                    dve.wait_ge(ada_stored, 16 * (n - 1))
                nc.vector.tensor_tensor(ada[:, n % 2], psD[0:B, :], b_ada[:, n % 2], ALU.add).then_inc(ada_done, 1)

        @block.tensor
        def _(pe):
            pe.wait_ge(consts_in, 48)

            def unit(b, p, n):
                r = p % 2
                pe.wait_ge(x_in[r], 16 * (2 * b + p // 2 + 1))
                for q in range(NQ):
                    if n > 0 or q >= 2:
                        pe.wait_ge(xT_written, 2 * (n * NQ + q - 1))
                    for k in range(QT):
                        last = nc.tensor.transpose(psT[q % 2][:, k * P:(k + 1) * P], x_tok[:, r, q * QT + k, :], ident[:])
                    last.then_inc(x_turned, 1)

            def scores(b, p, n):
                r = p % 2
                pe.wait_ge(xT_written, (n + 1) * 2 * NQ)
                pe.wait_ge(x_lo_done, n + 1)
                if n == 0:
                    pe.wait_ge(aw_split, 2)
                if b == 1 and p == 0:
                    pe.wait_ge(gate_done, 1)
                for t in range(TPB):
                    out = psA[:, t * H0:(t + 1) * H0]
                    cols = slice(t * P, (t + 1) * P)
                    for i, (l, rr) in enumerate(((x_hi, aw_hi), (x_hi, aw_lo), (x_lo, aw_hi))):
                        last = nc.tensor.matmul(out, l[:, r, cols], rr[:, p, :], start=(p == 0 and t == 0 and i == 0),
                                                stop=(p == KD - 1 and i == 2), skip_group_check=True)
                last.then_inc(att_done, 1)

            for b in range(B):
                for p in range(KD):
                    unit(b, p, b * KD + p)
                    if p >= 1:
                        scores(b, p - 1, b * KD + p - 1)
                scores(b, KD - 1, b * KD + KD - 1)
            pe.wait_ge(oper_in, 32)
            for i in range(2 * KD):
                k, half = i // 2, i % 2
                if i < 2:
                    pe.wait_ge(xT_written, 2 * B * KD * NQ)
                else:
                    pe.wait_ge(operT_written, i - 1)
                for j in range(4):
                    last = nc.tensor.transpose(psT[i % 2][:, j * P:(j + 1) * P], oper[:, half * 4 + j, k * P:(k + 1) * P], ident[:])
                last.then_inc(oper_turned, 1)
            pe.wait_ge(operT_written, 2 * KD)
            for j in range(KH):
                if j >= 2:
                    pe.wait_ge(of_written, 2 * (j - 1))
                for k in range(KD):
                    last = nc.tensor.matmul(psW[j % 2][:], operT[:, k, j * P:(j + 1) * P], ff1b[:, k, :],
                                            start=(k == 0), stop=(k == KD - 1))
                last.then_inc(of_mm, 1)
            pe.wait_ge(small_in, 48)
            for o in range(KD):
                for k in range(KD):
                    last = nc.tensor.matmul(psB[:, o * B:(o + 1) * B], ff1b[:, k, o * P:(o + 1) * P], condT[:, k, :],
                                            start=(o == 0 and k == 0), stop=(k == KD - 1), skip_group_check=True)
            last.then_inc(b1_mm, 1)
            for b in range(B):
                pe.wait_ge(gate_done, b + 1)
                for q in range(NQ):
                    if b > 0 or q > 0:
                        pe.wait_ge(gT_written, 2 * (b * NQ + q))
                    for k in range(QT):
                        last = nc.tensor.transpose(psG[0:H0, k * P:(k + 1) * P], gate[:, b, q * QT + k, :], ident[:])
                    last.then_inc(g_turned, 1)
            for n in range(NADA // CH):
                pe.wait_ge(ada_in[n % 2], 16 * (n // 2 + 1))
                if n >= 1:
                    pe.wait_ge(ada_done, n)
                for k in range(KD):
                    last = nc.tensor.matmul(psD[0:B, :], condT[:, k, :], stage[:, n % 2, k * CH:(k + 1) * CH], start=(k == 0), stop=(k == KD - 1))
                last.then_inc(ada_mm, 1)


def split_product(pe, out, terms):
    last = None
    for i, (l_hi, l_lo, r_hi, r_lo) in enumerate(terms):
        for j, (l, r) in enumerate(((l_hi, r_hi), (l_hi, r_lo), (l_lo, r_hi))):
            last = pe.matmul(out, l, r, start=(i == 0 and j == 0), stop=(i == len(terms) - 1 and j == 2))
    return last


def phase_layer0(nc, a, s, w):
    with ExitStack() as stack:
        m = Memory(nc, stack)
        c_hi = m.sb("l_c_hi", [P, 2, KD, CH], F16)
        c_lo = m.sb("l_c_lo", [P, 2, KD, CH], F16)
        x_hi = m.sb("l_x_hi", [P, 2, KD, CH], F16)
        x_lo = m.sb("l_x_lo", [P, 2, KD, CH], F16)
        g = m.sb("l_g", [P, 2, CH], F16)
        sel = m.sb("l_sel", [P, KH, P], F16)
        y = m.sb("l_y", [P, 2, TPC, D])
        gB = m.sb("l_gB", [P, 2, CH])
        a32 = m.sb("l_a32", [P, 2, CH])
        a_hi = m.sb("l_a_hi", [P, KH, CH], F16)
        a_lo = m.sb("l_a_lo", [P, KH, CH], F16)
        h32 = m.sb("l_h32", [P, 2, CH])
        h_hi = m.sb("l_h_hi", [P, KD, CH], F16)
        h_lo = m.sb("l_h_lo", [P, KD, CH], F16)
        b2 = m.sb("l_b2", [P, D])
        gamma = m.sb("l_gamma", [P, D])
        beta = m.sb("l_beta", [P, D])
        stats = m.sb("l_stats", [P, TPC, 6])
        mv = m.sb("l_mv", [P, TPC, 2])
        mean_diff = m.sb("l_mean_diff", [P, TPC])
        std = m.sb("l_std", [P, TPC])
        rstd = m.sb("l_rstd", [P, TPC])
        nmr = m.sb("l_nmr", [P, TPC])
        eps = m.sb("l_eps", [P, 1])
        psV = [m.ps(f"l_psV{i}") for i in range(2)]
        psG = [m.ps(f"l_psG{i}") for i in range(2)]
        psF = [m.ps(f"l_psF{i}") for i in range(2)]
        psR = [m.ps(f"l_psR{i}") for i in range(2)]

        rows_in = m.sem("l_rows_in")
        mats_in = [m.sem(f"l_mats_in{i}") for i in range(2)]
        x_in = [m.sem(f"l_x_in{i}") for i in range(2)]
        x1_out = [m.sem(f"l_x1_out{i}") for i in range(2)]
        init = m.sem("l_init")
        v_mm = m.sem("l_v_mm")
        gB_done = m.sem("l_gB_done")
        a32_done = m.sem("l_a32_done")
        a_hi_done = m.sem("l_a_hi_done")
        a_lo_done = m.sem("l_a_lo_done")
        f1_mm = m.sem("l_f1_mm")
        h32_done = m.sem("l_h32_done")
        h_hi_done = m.sem("l_h_hi_done")
        h_lo_done = m.sem("l_h_lo_done")
        f2_mm = m.sem("l_f2_mm")
        bias_added = m.sem("l_bias_added")
        res_done = m.sem("l_res_done")
        stats_done = m.sem("l_stats_done")
        mv_done = m.sem("l_mv_done")
        std_done = m.sem("l_std_done")
        rstd_done = m.sem("l_rstd_done")
        nmr_done = m.sem("l_nmr_done")
        norm_done = m.sem("l_norm_done")
        gamma_done = m.sem("l_gamma_done")
        beta_done = m.sem("l_beta_done")

        x_v = a["x"].rearrange("b (c t p) d -> (b c) p t d", p=P, t=TPC)

        block = stack.enter_context(nc.Block())

        @block.sync
        def _(sp):
            sp.dma_start(sel[:], a["c_sel"]).then_inc(rows_in, 16)

            def load_mats(c, r):
                for t, name in ((c_hi, "c_hi"), (c_lo, "c_lo"), (x_hi, "x_hi"), (x_lo, "x_lo")):
                    sp.dma_start(t[:, r], s[name][c]).then_inc(mats_in[r], 16)
                sp.dma_start(g[0:2 * H0, r, :], s["g"][c]).then_inc(mats_in[r], 16)

            def load_x(c, r):
                sp.dma_start(y[:, r], x_v[c]).then_inc(x_in[r], 16)

            def store(c, r):
                sp.wait_ge(beta_done, TPC * c + TPC)
                sp.dma_start(s["x1"][c], y[:, r]).then_inc(x1_out[r], 16)

            sp.wait_ge(init, 1)
            for r in range(2):
                load_mats(r, r)
            for r in range(2):
                load_x(r, r)
            for t, name in ((b2, "L0_cond_ff2_bias"), (gamma, "L0_cond_ln_gamma"), (beta, "L0_cond_ln_beta")):
                src = a[name] if name != "L0_cond_ff2_bias" else a[name].rearrange("a b n -> (a b n)")
                sp.dma_start(t[:], bcast_rows(src)).then_inc(rows_in, 16)
            with sp.Fori(0, NCH // 2 - 1) as i:
                for r in range(2):
                    c = 2 * i + r
                    sp.wait_ge(f1_mm, KD * c + KD)
                    load_mats(c + 2, r)
                    store(c, r)
                    sp.wait_ge(x1_out[r], 16 * i + 16)
                    load_x(2 * (i + 1) + r, r)
            for r in range(2):
                store(NCH - 2 + r, r)
            for r in range(2):
                sp.wait_ge(x1_out[r], 16 * NCH // 2)

        @block.gpsimd
        def _(pool):
            pool.wait_ge(rows_in, 64)

            def add_bias(r, i):
                pool.wait_ge(x_in[r], 16 * i + 16)
                nc.gpsimd.tensor_tensor(y[:, r], y[:, r], b2[:].unsqueeze(1).to_broadcast([P, TPC, D]),
                                        ALU.add).then_inc(bias_added, 1)

            def add_beta(c, r):
                for t in range(TPC):
                    pool.wait_ge(gamma_done, TPC * c + t + 1)
                    nc.gpsimd.tensor_tensor(y[:, r, t], y[:, r, t], beta[:], ALU.add).then_inc(beta_done, 1)

            add_bias(0, 0)
            add_bias(1, 0)
            with pool.Fori(0, NCH // 2 - 1) as i:
                for r in range(2):
                    add_beta(2 * i + r, r)
                    add_bias(r, i + 1)
            for r in range(2):
                add_beta(NCH - 2 + r, r)

        @block.scalar
        def _(act):
            def gates(c, j):
                act.wait_ge(v_mm, KH * c + j + 1)
                if not (isinstance(c, int) and c == 0 and j < 2):
                    act.wait_ge(a32_done, KH * c + j - 1)
                nc.scalar.activation(gB[:, j % 2], psG[j % 2][:], ACT.Copy, scale=1.0 / WS).then_inc(gB_done, 1)

            def values(c):
                for j in range(2):
                    gates(c, j)
                for j in range(KH):
                    act.wait_ge(a32_done, KH * c + j + 1)
                    nc.scalar.copy(a_hi[:, j], a32[:, j % 2]).then_inc(a_hi_done, 1)
                    if j + 2 < KH:
                        gates(c, j + 2)

            def hidden(c):
                for o in range(KD):
                    act.wait_ge(f1_mm, KD * c + o + 1)
                    if not (isinstance(c, int) and c == 0 and o < 2):
                        act.wait_ge(h_lo_done, KD * c + o - 1)
                    bias = w["b1"][:, o, bass.ds(c, 1)]
                    nc.scalar.activation(h32[:, o % 2], psF[o % 2][:], ACT.Relu, bias=bias, scale=1.0 / WS).then_inc(h32_done, 1)
                    nc.scalar.activation(h_hi[:, o], psF[o % 2][:], ACT.Relu, bias=bias, scale=1.0 / WS).then_inc(h_hi_done, 1)

            def norm(c, r):
                act.wait_ge(mv_done, TPC * c + TPC)
                nc.scalar.activation(std[:], mv[:, :, 1], ACT.Sqrt, bias=eps[:], scale=1.0 / D).then_inc(std_done, 1)
                act.wait_ge(nmr_done, c + 1)
                for t in range(TPC):
                    nc.scalar.activation(y[:, r, t], y[:, r, t], ACT.Identity, bias=nmr[:, t:t + 1],
                                         scale=rstd[:, t:t + 1]).then_inc(norm_done, 1)

            act.wait_ge(init, 2)
            values(0)
            hidden(0)
            with act.Fori(0, NCH // 2 - 1) as i:
                for u in range(2):
                    c = 2 * i + 1 + u
                    values(c)
                    norm(c - 1, u)
                    hidden(c)
            values(NCH - 1)
            norm(NCH - 2, 0)
            hidden(NCH - 1)
            norm(NCH - 1, 1)

        @block.vector
        def _(dve):
            nc.vector.memset(g[:], 0.0).then_inc(init, 1)
            nc.vector.memset(eps[:], EPS_LN0).then_inc(init, 1)

            def values(c):
                for j in range(KH):
                    dve.wait_ge(gB_done, KH * c + j + 1)
                    if not (isinstance(c, int) and c == 0 and j < 2):
                        dve.wait_ge(a_hi_done, KH * c + j - 1)
                        dve.wait_ge(a_lo_done, KH * c + j - 1)
                    nc.vector.tensor_tensor(a32[:, j % 2], psV[j % 2][:], gB[:, j % 2], ALU.mult).then_inc(a32_done, 1)
                    if j >= 1:
                        low(c, j - 1)
                low(c, KH - 1)

            def low(c, j):
                dve.wait_ge(a_hi_done, KH * c + j + 1)
                dve.wait_ge(a32_done, KH * c + j + 1)
                nc.vector.tensor_tensor(a_lo[:, j], a32[:, j % 2], a_hi[:, j], ALU.subtract).then_inc(a_lo_done, 1)

            def hidden(c):
                for o in range(KD):
                    dve.wait_ge(h_hi_done, KD * c + o + 1)
                    dve.wait_ge(h32_done, KD * c + o + 1)
                    nc.vector.tensor_tensor(h_lo[:, o], h32[:, o % 2], h_hi[:, o], ALU.subtract).then_inc(h_lo_done, 1)

            def norm(c, r):
                dve.wait_ge(bias_added, c + 1)
                for t in range(TPC):
                    dve.wait_ge(f2_mm, TPC * c + t + 1)
                    nc.vector.scalar_tensor_tensor(y[:, r, t], psR[t % 2][:], 1.0 / WS, y[:, r, t],
                                                   ALU.mult, ALU.add).then_inc(res_done, 1)
                    dve.wait_ge(res_done, TPC * c + t + 1)
                    nc.vector.bn_stats(stats[:, t], y[:, r, t]).then_inc(stats_done, 1)
                combine_moments(nc, dve, stats, mv, mean_diff, stats_done, TPC * c, mv_done, TPC * c)
                dve.wait_ge(std_done, c + 1)
                nc.vector.reciprocal(rstd[:], std[:]).then_inc(rstd_done, 1)
                dve.wait_ge(rstd_done, c + 1)
                dve.wait_ge(mv_done, TPC * c + TPC)
                nc.vector.scalar_tensor_tensor(nmr[:], mv[:, :, 0], -0.5, rstd[:], ALU.mult, ALU.mult).then_inc(nmr_done, 1)
                for t in range(TPC):
                    dve.wait_ge(norm_done, TPC * c + t + 1)
                    nc.vector.tensor_tensor(y[:, r, t], y[:, r, t], gamma[:], ALU.mult).then_inc(gamma_done, 1)

            dve.wait_ge(rows_in, 64)
            values(0)
            hidden(0)
            with dve.Fori(0, NCH // 2 - 1) as i:
                for u in range(2):
                    c = 2 * i + 1 + u
                    values(c)
                    norm(c - 1, u)
                    hidden(c)
            values(NCH - 1)
            norm(NCH - 2, 0)
            hidden(NCH - 1)
            norm(NCH - 1, 1)

        @block.tensor
        def _(pe):
            def values(c, r, i):
                pe.wait_ge(mats_in[r], 80 * i + 80)
                for j in range(KH):
                    if not (isinstance(c, int) and c == 0 and j < 2):
                        pe.wait_ge(gB_done, KH * c + j - 1)
                        pe.wait_ge(a32_done, KH * c + j - 1)
                    cols = slice(j * P, (j + 1) * P)
                    pe.matmul(psG[j % 2][:], sel[:, j, :], g[:, r, :], start=True, stop=True)
                    split_product(pe, psV[j % 2][:], [(w["val_hi"][:, k, cols], w["val_lo"][:, k, cols], c_hi[:, r, k, :], c_lo[:, r, k, :])
                                                      for k in range(KD)]).then_inc(v_mm, 1)

            def hidden(c, r):
                for o in range(KD):
                    cols = slice(o * P, (o + 1) * P)
                    if not (isinstance(c, int) and c == 0 and o < 2):
                        pe.wait_ge(h_hi_done, KD * c + o - 1)
                    if o == 0:
                        pe.wait_ge(a_hi_done, KH * c + KH)
                        pe.wait_ge(a_lo_done, KH * c + KH)
                    terms = [(w["f1_hi"][:, k, cols], w["f1_lo"][:, k, cols], x_hi[:, r, k, :], x_lo[:, r, k, :]) for k in range(KD)]
                    terms += [(w["of_hi"][:, k, cols], w["of_lo"][:, k, cols], a_hi[:, k, :], a_lo[:, k, :]) for k in range(KH)]
                    split_product(pe, psF[o % 2][:], terms).then_inc(f1_mm, 1)

            def output(c):
                pe.wait_ge(h_lo_done, KD * c + KD)
                for t in range(TPC):
                    if t >= 2:
                        pe.wait_ge(res_done, TPC * c + t - 1)
                    cols = slice(t * P, (t + 1) * P)
                    split_product(pe, psR[t % 2][:], [(h_hi[:, k, cols], h_lo[:, k, cols], w["f2_hi"][:, k, :], w["f2_lo"][:, k, :])
                                                      for k in range(KD)]).then_inc(f2_mm, 1)

            pe.wait_ge(rows_in, 16)
            values(0, 0, 0)
            hidden(0, 0)
            with pe.Fori(0, NCH // 2 - 1) as i:
                for u in range(2):
                    c = 2 * i + 1 + u
                    values(c, (1 + u) % 2, i + u)
                    output(c - 1)
                    hidden(c, (1 + u) % 2)
            values(NCH - 1, 1, NCH // 2 - 1)
            output(NCH - 2)
            hidden(NCH - 1, 1)
            output(NCH - 1)


def phase_qkv(nc, a, s, w):
    with ExitStack() as stack:
        m = Memory(nc, stack)
        ident = m.sb("q_ident", [P, P])
        x = m.sb("q_x", [P, 2, TPC, D])
        hT32 = m.sb("q_hT32", [P, 2, CH])
        h_hi = m.sb("q_h_hi", [P, 2, KD, CH], F16)
        h_lo = m.sb("q_h_lo", [P, 2, KD, CH], F16)
        p32 = m.sb("q_p32", [P, 2, CH])
        qk_hi = m.sb("q_qk_hi", [P, 2, 2, KD, CH], F16)
        qk_lo = m.sb("q_qk_lo", [P, 2, 2, KD, CH], F16)
        v = m.sb("q_v", [P, 2, TPC, D])
        bqk = m.sb("q_bqk", [P, 2, KD])
        mod = m.sb("q_mod", [P, 2, KD, B])
        mod_c = m.sb("q_mod_c", [P, 2, KD, NCH])
        stats = m.sb("q_stats", [P, TPC, 6])
        mv = m.sb("q_mv", [P, TPC, 2])
        mean_diff = m.sb("q_mean_diff", [P, TPC])
        std = m.sb("q_std", [P, TPC])
        rstd = m.sb("q_rstd", [P, TPC])
        nmr = m.sb("q_nmr", [P, TPC])
        eps = m.sb("q_eps", [P, 1])
        psT = [m.ps(f"q_psT{i}") for i in range(2)]
        psQ = [m.ps(f"q_psQ{i}") for i in range(4)]
        NT = 3 * KD

        rows_in = m.sem("q_rows_in")
        mod_done = m.sem("q_mod_done")
        x_in = [m.sem(f"q_x_in{i}") for i in range(2)]
        stats_done = m.sem("q_stats_done")
        mv_done = m.sem("q_mv_done")
        std_done = m.sem("q_std_done")
        rstd_done = m.sem("q_rstd_done")
        nmr_done = m.sem("q_nmr_done")
        norm_done = m.sem("q_norm_done")
        turned = m.sem("q_turned")
        h32_done = m.sem("q_h32_done")
        h_hi_done = m.sem("q_h_hi_done")
        h_lo_done = m.sem("q_h_lo_done")
        proj_mm = m.sem("q_proj_mm")
        p32_done = m.sem("q_p32_done")
        p_hi_done = m.sem("q_p_hi_done")
        p_lo_done = m.sem("q_p_lo_done")
        v_done = m.sem("q_v_done")
        stored = [m.sem(f"q_stored{i}") for i in range(2)]

        stage = m.sb("q_stage", [P, 2, KD, CH])
        stage_in = [m.sem(f"q_stage_in{i}") for i in range(2)]
        w64_done = m.sem("q_w64_done")
        w_hi_done = m.sem("q_w_hi_done")
        w_lo_done = m.sem("q_w_lo_done")
        pieces = [(a["L1_cond_Wo"].rearrange("(k p) n -> p k n", p=P), w["wo_hi"][:], w["wo_lo"][:])]
        for j in range(FF // CH):
            cols = slice(j * CH, (j + 1) * CH)
            pieces.append((a["L1_cond_W1"].rearrange("(k p) n -> p k n", p=P)[:, :, cols], w["w1_hi"][:, :, cols], w["w1_lo"][:, :, cols]))
        for j in range(FF // CH):
            rows = slice(j * KD, (j + 1) * KD)
            pieces.append((a["L1_cond_W2"].rearrange("(k p) n -> p k n", p=P)[:, rows, :], w["w2_hi"][:, rows, :], w["w2_lo"][:, rows, :]))

        block = stack.enter_context(nc.Block())

        @block.gpsimd
        def _(pool):
            for n in range(2):
                pool.dma_start(stage[:, n], pieces[n][0]).then_inc(stage_in[n], 16)
            for n, (_, hi, lo) in enumerate(pieces):
                pool.wait_ge(stage_in[n % 2], 16 * (n // 2 + 1))
                nc.gpsimd.tensor_scalar(stage[:, n % 2], stage[:, n % 2], WS, None, ALU.mult).then_inc(w64_done, 1)
                pool.wait_ge(w64_done, n + 1)
                nc.gpsimd.tensor_copy(hi, stage[:, n % 2]).then_inc(w_hi_done, 1)
                pool.wait_ge(w_hi_done, n + 1)
                nc.gpsimd.tensor_tensor(lo, stage[:, n % 2], hi, ALU.subtract).then_inc(w_lo_done, 1)
                if n + 2 < len(pieces):
                    pool.wait_ge(w_lo_done, n + 1)
                    pool.dma_start(stage[:, n % 2], pieces[n + 2][0]).then_inc(stage_in[n % 2], 16)

        @block.sync
        def _(sp):
            def load(c, r):
                sp.dma_start(x[:, r], s["x1"][c]).then_inc(x_in[r], 16)

            def store(i, r):
                c = 2 * i + r
                sp.wait_ge(p_hi_done, 2 * KD * c + 2 * KD)
                sp.wait_ge(p_lo_done, 2 * KD * c + 2 * KD)
                for j, name in enumerate("qk"):
                    for half, t in enumerate((qk_hi, qk_lo)):
                        sp.dma_start(s[name].rearrange("h (g c) p t -> h c p g t", g=KD)[half, c], t[:, r, j]).then_inc(stored[r], 16)
                sp.wait_ge(v_done, TPC * c + TPC)
                c = 2 * (i + 1) + r - 2
                for g in range(KD):
                    sp.dma_start(s["v"].rearrange("(g c) p t d -> g c p t d", g=KD)[g, c],
                                 v[:, r, :, g * P:(g + 1) * P]).then_inc(stored[r], 16)

            load(0, 0)
            sp.dma_start(ident[:], a["c_ident"]).then_inc(rows_in, 16)
            for i, name in enumerate(("bq", "bk")):
                sp.dma_start(bqk[:, i], a["L1_cond_" + name].rearrange("(k p) -> p k", p=P),
                             allow_slow_non_contiguous=True).then_inc(rows_in, 16)
                for b in range(B):
                    sp.dma_start(mod[:, i, :, b], s["ada"][b, i * D:(i + 1) * D].rearrange("(k p) -> p k", p=P),
                                 allow_slow_non_contiguous=True).then_inc(rows_in, 16)
            load(1, 1)
            with sp.Fori(0, NCH // 2 - 1) as i:
                for r in range(2):
                    c = 2 * i + r
                    sp.wait_ge(turned, KD * c + KD)
                    store(i, r)
                    sp.wait_ge(stored[r], 128 * i + 128)
                    load(c + 2, r)
            for r in range(2):
                store(NCH // 2 - 1, r)
            for r in range(2):
                sp.wait_ge(stored[r], 128 * (NCH // 2))

        @block.scalar
        def _(act):
            def norm(c, r):
                act.wait_ge(mv_done, TPC * c + TPC)
                if not (isinstance(c, int) and c == 0):
                    act.wait_ge(rstd_done, c)
                nc.scalar.activation(std[:], mv[:, :, 1], ACT.Sqrt, bias=eps[:], scale=1.0 / D).then_inc(std_done, 1)
                act.wait_ge(nmr_done, c + 1)
                for t in range(TPC):
                    nc.scalar.activation(x[:, r, t], x[:, r, t], ACT.Identity, bias=nmr[:, t:t + 1],
                                         scale=rstd[:, t:t + 1]).then_inc(norm_done, 1)

            def modulate(c, r):
                for k in range(KD):
                    act.wait_ge(turned, KD * c + k + 1)
                    if not (isinstance(c, int) and c == 0 and k < 2):
                        act.wait_ge(h_lo_done, KD * c + k - 1)
                    shift, scale = mod_c[:, 0, k, bass.ds(c, 1)], mod_c[:, 1, k, bass.ds(c, 1)]
                    nc.scalar.activation(hT32[:, k % 2], psT[k % 2][:], ACT.Identity, bias=shift, scale=scale).then_inc(h32_done, 1)
                    nc.scalar.activation(h_hi[:, r, k], psT[k % 2][:], ACT.Identity, bias=shift, scale=scale).then_inc(h_hi_done, 1)

            def queries_keys(c, r):
                for j in range(2 * KD):
                    act.wait_ge(proj_mm, NT * c + j + 1)
                    if not (isinstance(c, int) and c == 0 and j < 2):
                        act.wait_ge(p_lo_done, 2 * KD * c + j - 1)
                    which, o = j // KD, j % KD
                    bias = bqk[:, which, o:o + 1]
                    nc.scalar.activation(p32[:, j % 2], psQ[j % 4][:], ACT.Identity, bias=bias, scale=1.0 / WS).then_inc(p32_done, 1)
                    nc.scalar.activation(qk_hi[:, r, which, o], psQ[j % 4][:], ACT.Identity, bias=bias, scale=1.0 / WS).then_inc(p_hi_done, 1)

            def values(c, r):
                for t in range(TPC):
                    act.wait_ge(proj_mm, NT * c + 2 * KD + t + 1)
                    nc.scalar.activation(v[:, r, t], psQ[(2 * KD + t) % 4][:], ACT.Copy, scale=1.0 / WS).then_inc(v_done, 1)

            norm(0, 0)
            act.wait_ge(mod_done, 3)
            modulate(0, 0)
            norm(1, 1)
            queries_keys(0, 0)
            modulate(1, 1)
            values(0, 0)
            with act.Fori(0, NCH // 2 - 1) as i:
                for u in range(2):
                    c, r = 2 * i + 1 + u, (1 + u) % 2
                    norm(c + 1, 1 - r)
                    queries_keys(c, r)
                    modulate(c + 1, 1 - r)
                    values(c, r)
            queries_keys(NCH - 1, 1)
            values(NCH - 1, 1)

        @block.vector
        def _(dve):
            nc.vector.memset(eps[:], EPS_LN1).then_inc(mod_done, 1)
            dve.wait_ge(rows_in, 112)
            dve.wait_ge(mod_done, 1)
            for i, one in enumerate((0.0, 1.0)):
                nc.vector.tensor_scalar_add(mod_c[:, i].rearrange("p k (b c) -> p (k b) c", b=B),
                                            mod[:, i].rearrange("p k b -> p (k b)").unsqueeze(2).to_broadcast([P, KD * B, CPB]),
                                            one).then_inc(mod_done, 1)

            def norm(c, r, i):
                dve.wait_ge(x_in[r], 16 * i + 16)
                for t in range(TPC):
                    nc.vector.bn_stats(stats[:, t], x[:, r, t]).then_inc(stats_done, 1)
                if not (isinstance(c, int) and c == 0):
                    dve.wait_ge(std_done, c)
                combine_moments(nc, dve, stats, mv, mean_diff, stats_done, TPC * c, mv_done, TPC * c)
                dve.wait_ge(std_done, c + 1)
                if not (isinstance(c, int) and c == 0):
                    dve.wait_ge(norm_done, TPC * c)
                nc.vector.reciprocal(rstd[:], std[:]).then_inc(rstd_done, 1)
                dve.wait_ge(rstd_done, c + 1)
                nc.vector.scalar_tensor_tensor(nmr[:], mv[:, :, 0], -0.5, rstd[:], ALU.mult, ALU.mult).then_inc(nmr_done, 1)

            def modulate(c, r):
                for k in range(KD):
                    dve.wait_ge(h32_done, KD * c + k + 1)
                    dve.wait_ge(h_hi_done, KD * c + k + 1)
                    nc.vector.tensor_tensor(h_lo[:, r, k], hT32[:, k % 2], h_hi[:, r, k], ALU.subtract).then_inc(h_lo_done, 1)

            def queries_keys(c, r):
                for j in range(2 * KD):
                    dve.wait_ge(p32_done, 2 * KD * c + j + 1)
                    dve.wait_ge(p_hi_done, 2 * KD * c + j + 1)
                    which, o = j // KD, j % KD
                    nc.vector.tensor_tensor(qk_lo[:, r, which, o], p32[:, j % 2], qk_hi[:, r, which, o],
                                            ALU.subtract).then_inc(p_lo_done, 1)

            norm(0, 0, 0)
            modulate(0, 0)
            norm(1, 1, 0)
            queries_keys(0, 0)
            modulate(1, 1)
            with dve.Fori(0, NCH // 2 - 1) as i:
                for u in range(2):
                    c, r = 2 * i + 1 + u, (1 + u) % 2
                    norm(c + 1, 1 - r, i + 1)
                    queries_keys(c, r)
                    modulate(c + 1, 1 - r)
            queries_keys(NCH - 1, 1)

        @block.tensor
        def _(pe):
            def turn(c, r):
                for k in range(KD):
                    if k == 0:
                        pe.wait_ge(norm_done, TPC * c + TPC)
                    if not (isinstance(c, int) and c == 0 and k < 2):
                        pe.wait_ge(h_hi_done, KD * c + k - 1)
                    for t in range(TPC):
                        last = pe.transpose(psT[k % 2][:, t * P:(t + 1) * P], x[:, r, t, k * P:(k + 1) * P], ident[:])
                    last.then_inc(turned, 1)

            def queries_keys(c, r):
                pe.wait_ge(h_lo_done, KD * c + KD)
                for j in range(2 * KD):
                    name, cols = ("wq", "wk")[j // KD], slice(j % KD * P, (j % KD + 1) * P)
                    if not (isinstance(c, int) and c == 0 and j < 4):
                        if j < 4:
                            pe.wait_ge(v_done, TPC * c - TPC + j + 1)
                        else:
                            pe.wait_ge(p_hi_done, 2 * KD * c + j - 3)
                    split_product(pe, psQ[j % 4][:], [(w[name + "_hi"][:, k, cols], w[name + "_lo"][:, k, cols], h_hi[:, r, k, :], h_lo[:, r, k, :])
                                                      for k in range(KD)]).then_inc(proj_mm, 1)

            def values(c, r):
                for t in range(TPC):
                    pe.wait_ge(p_hi_done, 2 * KD * c + KD + t + 1)
                    cols = slice(t * P, (t + 1) * P)
                    split_product(pe, psQ[t % 4][:], [(h_hi[:, r, k, cols], h_lo[:, r, k, cols], w["wv_hi"][:, k, :], w["wv_lo"][:, k, :])
                                                      for k in range(KD)]).then_inc(proj_mm, 1)

            pe.wait_ge(rows_in, 112)
            turn(0, 0)
            queries_keys(0, 0)
            turn(1, 1)
            values(0, 0)
            with pe.Fori(0, NCH // 2 - 1) as i:
                for u in range(2):
                    c, r = 2 * i + 1 + u, (1 + u) % 2
                    queries_keys(c, r)
                    turn(c + 1, 1 - r)
                    values(c, r)
            queries_keys(NCH - 1, 1)
            values(NCH - 1, 1)


def phase_attention(nc, a, s, w):
    with ExitStack() as stack:
        m = Memory(nc, stack)
        NH = P // DH
        NI = KD * NCH
        NG = KD * B
        MU = NH * TPC * CPB
        ADDED = [kt for kt in range(TPB) if kt == 0 or kt % 3 != 0]
        ADDS = len(ADDED) - 1
        UNITS, first_unit = [], 0
        for kt in range(TPB):
            here = min(MU - first_unit, 0 if kt == TPB - 1 else 5 if kt < 2 or (kt - 1) not in ADDED else 4)
            UNITS.append(range(first_unit, first_unit + here))
            first_unit += here
        assert first_unit == MU
        R3 = 3 * DH
        SCALE = 1.0 / float(np.sqrt(np.float32(DH)))

        ident = m.sb("a_ident", [P, P])
        ident16 = m.sb("a_ident16", [P, P], F16)
        krows = m.sb("a_krows", [P, 1])
        ka = w["qkv"][0:R3, 0:NH]
        qa = m.sb("a_qa", [R3, NH, CH], F16)
        kb = m.sb("a_kb", [P, NH, S], F16)
        qb = w["qkv"][:, NH:NH + 2].rearrange("p s (h t) -> p s h t", h=NH)
        vb = m.sb("a_vb", [P, TPB, P])
        ones = m.sb("a_ones", [P, DH])
        probs = m.sb("a_probs", [P, 4, NH, CH])
        parts = m.sb("a_parts", [P, MU])
        m16 = m.sb("a_m16", [P, NH * TPC])
        mcols = m.sb("a_mcols", [P, NH * TPC, DH], F16)
        o32 = m.sb("a_o32", [P, CH])
        z32 = m.sb("a_z32", [P, CH])
        sums = m.sb("a_sums", [P, NH, CH])
        rz = m.sb("a_rz", [P, CH])
        att = m.sb("a_att", [P, CH])
        ob32 = m.sb("a_ob32", [P, CH])
        o_hi = m.sb("a_o_hi", [P, 2, CH], F16)
        o_lo = m.sb("a_o_lo", [P, 2, CH], F16)
        bv = m.sb("a_bv", [P, KD])
        psS = [m.ps(f"a_psS{i}", (P, 2 * CH)) for i in range(2)]
        psM = [m.ps(f"a_psM{i}") for i in range(2)]
        psO = m.ps("a_psO")
        psZ = m.ps("a_psZ")

        rows_in = m.sem("a_rows_in")
        qa_in = m.sem("a_qa_in")
        qb_in = m.sem("a_qb_in")
        ka_in = [m.sem(f"a_ka_in{i}") for i in range(NH)]
        kb_in = [m.sem(f"a_kb_in{i}") for i in range(4)]
        init = m.sem("a_init")
        ident16_done = m.sem("a_ident16_done")
        s_mm = m.sem("a_s_mm")
        m_mm = m.sem("a_m_mm")
        mx_part = m.sem("a_mx_part")
        m16_done = m.sem("a_m16_done")
        mh_done = m.sem("a_mh_done")
        ml_done = m.sem("a_ml_done")
        r_mm = m.sem("a_r_mm")
        rows_done = m.sem("a_rows_done")
        exp_done = m.sem("a_exp_done")
        pv_done = m.sem("a_pv_done")
        added = m.sem("a_added")
        z_mm = m.sem("a_z_mm")
        z_out = m.sem("a_z_out")
        o_out = m.sem("a_o_out")
        rz_done = m.sem("a_rz_done")
        att_done = m.sem("a_att_done")
        ob_done = m.sem("a_ob_done")
        o_hi_done = m.sem("a_o_hi_done")
        o_lo_done = m.sem("a_o_lo_done")
        o_stored = m.sem("a_o_stored")

        HI, LO = 0, 1
        RZ = TPC
        q_v = s["q"].rearrange("h n (j d) t -> h n d j t", d=DH)
        k_v = s["k"].rearrange("h (g c) (j d) t -> h g j d c t", c=CPB, d=DH)
        v_v = s["v"].rearrange("(g c) p t d -> g c p t d", c=CPB)

        block = stack.enter_context(nc.Block())

        @block.sync
        def _(sp):
            def load_qa(n):
                for i, half in enumerate((HI, LO, HI)):
                    sp.dma_start(qa[i * DH:(i + 1) * DH], q_v[half, n]).then_inc(qa_in, 16)

            def load_qb(n, slot):
                for i, half in enumerate((HI, LO, HI)):
                    sp.dma_start(qb[i * DH:(i + 1) * DH, slot], q_v[half, n]).then_inc(qb_in, 16)

            def load_ka(g, h):
                for i, half in enumerate((HI, HI, LO)):
                    sp.dma_start(ka[i * DH:(i + 1) * DH, h].rearrange("d (c t) -> d c t", c=CPB),
                                 k_v[half, g, h]).then_inc(ka_in[h], 16)

            def load_kb(g, c):
                for i, half in enumerate((HI, HI, LO)):
                    sp.dma_start(kb[i * DH:(i + 1) * DH, :, c * CH:(c + 1) * CH],
                                 k_v[half, g].rearrange("j d c t -> c d j t")[c]).then_inc(kb_in[c], 16)
                sp.dma_start(vb[:, c * TPC:(c + 1) * TPC, :], v_v[g, c]).then_inc(kb_in[c], 16)

            def store_o(n):
                if not (isinstance(n, int) and n == 0):
                    sp.wait_ge(o_stored, 32 * n)
                sp.wait_ge(o_hi_done, n + 1)
                sp.wait_ge(o_lo_done, n + 1)
                slot = n % 2
                for half, t in enumerate((o_hi, o_lo)):
                    src = t[:, slot, :] if isinstance(n, int) else t[:, bass.ds(slot, 1), :].rearrange("p a t -> p (a t)")
                    sp.dma_start(s["o"][half, n], src).then_inc(o_stored, 16)

            def item(n, g, cc, first=False, last_group=False):
                if not first:
                    store_o(n - 1)
                if not (last_group and cc == CPB - 1):
                    if not first:
                        sp.wait_ge(s_mm, 2 * TPB * n)
                    sp.wait_ge(qb_in, 48 * n + 48)
                    load_qb(n + 1, (cc + 1) % 2)
                if cc == CPB - 2 and not last_group:
                    for h in range(NH):
                        sp.wait_ge(m_mm, MU * (n + 1) + (h + 1) * MU // NH)
                        load_ka(g + 1, h)
                if cc == CPB - 1 and not last_group:
                    for c in range(CPB - 1):
                        sp.wait_ge(pv_done, TPB * n + TPC * (c + 1))
                        load_kb(g + 1, c)
                if not (last_group and cc >= CPB - 2):
                    sp.wait_ge(m_mm, MU * (n + 1) + MU)
                    load_qa(n + 2)
                if cc == CPB - 1 and not last_group:
                    sp.wait_ge(pv_done, TPB * n + TPB)
                    load_kb(g + 1, CPB - 1)

            load_qa(0)
            for h in range(NH):
                load_ka(0, h)
            load_qb(0, 0)
            sp.dma_start(krows[:], a["c_krows"]).then_inc(rows_in, 16)
            sp.dma_start(ident[:], a["c_ident"]).then_inc(rows_in, 16)
            sp.dma_start(bv[:], a["L1_cond_bv"].rearrange("(k p) -> p k", p=P), allow_slow_non_contiguous=True).then_inc(rows_in, 16)
            for c in range(CPB):
                load_kb(0, c)
            sp.wait_ge(m_mm, MU)
            load_qa(1)
            for cc in range(CPB):
                item(cc, 0, cc, first=cc == 0)
            with sp.Fori(1, NG - 1) as g:
                for cc in range(CPB):
                    item(CPB * g + cc, g, cc)
            for cc in range(CPB):
                item(CPB * (NG - 1) + cc, NG - 1, cc, last_group=True)
            store_o(NI - 1)
            sp.wait_ge(o_stored, 32 * NI)

        @block.gpsimd
        def _(pool):
            def item(n):
                for j, kt in enumerate(ADDED[1:]):
                    pool.wait_ge(exp_done, 2 * TPB * n + 2 * kt + 2)
                    if j == 0:
                        if not (isinstance(n, int) and n == 0):
                            pool.wait_ge(z_mm, n)
                        former = probs[:, ADDED[0] % 4]
                    else:
                        pool.wait_ge(added, ADDS * n + j)
                        former = sums[:]
                    nc.gpsimd.tensor_tensor(sums[:], former, probs[:, kt % 4], ALU.add).then_inc(added, 1)

            item(0)
            with pool.Fori(1, NI) as n:
                item(n)

        @block.scalar
        def _(act):
            def exps(n, kt):
                for pair in range(2):
                    act.wait_ge(s_mm, 2 * TPB * n + 2 * kt + pair + 1)
                    if pair == 0 and not (isinstance(n, int) and n == 0 and kt < 4):
                        act.wait_ge(pv_done, TPB * n + kt - 3)
                        act.wait_ge(added, ADDS * n + adds_until(kt - 4))
                    nc.scalar.activation(probs[:, kt % 4, 2 * pair:2 * pair + 2].rearrange("p h t -> p (h t)"), psS[pair][:],
                                         ACT.Exp, scale=SCALE).then_inc(exp_done, 1)

            def adds_until(kt):
                if kt < 0:
                    return adds_until(kt + TPB) - ADDS
                return max(1, sum(1 for s in ADDED[1:] if s <= kt))

            def values_out(n):
                act.wait_ge(pv_done, TPB * n + TPB)
                if not (isinstance(n, int) and n == 0):
                    act.wait_ge(att_done, n)
                nc.scalar.copy(o32[:], psO[:]).then_inc(o_out, 1)

            def sums_out(n):
                act.wait_ge(z_mm, n + 1)
                if not (isinstance(n, int) and n == 0):
                    act.wait_ge(rz_done, RZ * n)
                nc.scalar.copy(z32[:], psZ[:]).then_inc(z_out, 1)

            def result(n, slot):
                act.wait_ge(att_done, n + 1)
                group = n // NCH
                bias = bv[:, group:group + 1] if isinstance(n, int) else bv[:, bass.ds(group, 1)]
                hi = o_hi[:, slot] if isinstance(n, int) else o_hi[:, bass.ds(slot, 1)].rearrange("p a t -> p (a t)")
                nc.scalar.activation(ob32[:], att[:], ACT.Identity, bias=bias).then_inc(ob_done, 1)
                nc.scalar.activation(hi, att[:], ACT.Identity, bias=bias).then_inc(o_hi_done, 1)

            def rows(n):
                act.wait_ge(r_mm, n + 1)
                slot = n % 2
                for h in range(NH):
                    out = qb[R3:P, slot, h] if isinstance(n, int) else qb[R3:P, bass.ds(slot, 1), h].rearrange("p a t -> p (a t)")
                    nc.scalar.copy(out, psM[0][h * DH:(h + 1) * DH, :]).then_inc(rows_done, 1)

            def item(n, first=False, last=False):
                for kt in range(TPB):
                    if kt == 0 and not first:
                        values_out(n - 1)
                    exps(n, kt)
                    if kt == 2 and not first:
                        sums_out(n - 1)
                    if kt == 10 and not first:
                        result(n - 1, (n - 1) % 2)
                    if kt == TPB - 1 and not last:
                        rows(n + 1)

            act.wait_ge(rows_in, 48)
            nc.scalar.copy(ident16[:], ident[:]).then_inc(ident16_done, 1)
            rows(0)
            item(0, first=True)
            with act.Fori(1, NI - 1) as n:
                item(n)
            item(NI - 1, last=True)
            values_out(NI - 1)
            sums_out(NI - 1)
            result(NI - 1, (NI - 1) % 2)

        @block.vector
        def _(dve):
            nc.vector.memset(ones[:], 1.0).then_inc(init, 1)
            nc.vector.memset(mcols[:], 0.0).then_inc(init, 1)
            nc.vector.memset(kb[R3:P], 0.0).then_inc(init, 1)
            dve.wait_ge(init, 3)
            dve.wait_ge(rows_in, 48)
            nc.vector.tensor_scalar(kb[R3:P], kb[R3:P], krows[R3:P, 0:1], None, ALU.add).then_inc(init, 1)

            def maxima(n, units):
                for u in units:
                    dve.wait_ge(m_mm, MU * n + u + 1)
                    if u == 0 and not (isinstance(n, int) and n == 0):
                        dve.wait_ge(m16_done, n)
                    nc.vector.reduce_max(parts[:, u:u + 1], psM[u % 2][:], AX.X).then_inc(mx_part, 1)
                if units[-1] == MU - 1:
                    dve.wait_ge(mx_part, MU * n + MU)
                    if not (isinstance(n, int) and n == 0):
                        dve.wait_ge(ml_done, n)
                        dve.wait_ge(r_mm, n)
                    nc.vector.tensor_reduce(m16[:], parts[:].rearrange("p (u k) -> p u k", k=CPB), AX.X, ALU.max).then_inc(m16_done, 1)
                    dve.wait_ge(m16_done, n + 1)
                    nc.vector.tensor_scalar(mcols[:, :, 0], m16[:], -1.0 / WS, None, ALU.mult).then_inc(mh_done, 1)
                    dve.wait_ge(mh_done, n + 1)
                    nc.vector.scalar_tensor_tensor(mcols[:, :, 1], mcols[:, :, 0], -WS, m16[:],
                                                   ALU.mult, ALU.subtract).then_inc(ml_done, 1)

            def reciprocal(n, part):
                cols = slice(part * P, (part + 1) * P)
                dve.wait_ge(z_out, n + 1)
                nc.vector.reciprocal(rz[:, cols], z32[:, cols]).then_inc(rz_done, 1)

            def normalise(n):
                dve.wait_ge(rz_done, RZ * n + RZ)
                dve.wait_ge(o_out, n + 1)
                nc.vector.tensor_tensor(att[:], o32[:], rz[:], ALU.mult).then_inc(att_done, 1)
                dve.wait_ge(att_done, n + 1)

            def low(n, slot):
                dve.wait_ge(ob_done, n + 1)
                dve.wait_ge(o_hi_done, n + 1)
                hi, lo = ((t[:, slot] if isinstance(n, int) else t[:, bass.ds(slot, 1)].rearrange("p a t -> p (a t)")) for t in (o_hi, o_lo))
                nc.vector.tensor_tensor(lo, ob32[:], hi, ALU.subtract).then_inc(o_lo_done, 1)

            def item(n, first=False, last=False):
                for kt in range(TPB):
                    if kt < TPB - 1 and not last:
                        maxima(n + 1, UNITS[kt])
                    if 4 <= kt < 4 + RZ and not first:
                        reciprocal(n - 1, kt - 4)
                    if kt == 8 and not first:
                        normalise(n - 1)
                    if kt == 11 and not first:
                        low(n - 1, (n - 1) % 2)

            maxima(0, range(MU))
            item(0, first=True)
            with dve.Fori(1, NI - 1) as n:
                item(n)
            item(NI - 1, last=True)
            for part in range(RZ):
                reciprocal(NI - 1, part)
            normalise(NI - 1)
            low(NI - 1, (NI - 1) % 2)

        @block.tensor
        def _(pe):
            def scores(n, kt, pair):
                slot = n % 2
                if kt == 0 and pair == 0:
                    pe.wait_ge(qb_in, 48 * n + 48)
                    pe.wait_ge(rows_done, NH * n + NH)
                if kt % TPC == 0 and pair == 0:
                    pe.wait_ge(kb_in[kt // TPC], 64 * (n // CPB) + 64)
                if not (isinstance(n, int) and n == 0 and kt == 0):
                    pe.wait_ge(exp_done, 2 * TPB * n + 2 * kt + pair - 1)
                for h in (2 * pair, 2 * pair + 1):
                    q = qb[:, slot, h] if isinstance(n, int) else qb[:, bass.ds(slot, 1), h].rearrange("p a t -> p (a t)")
                    last = pe.matmul(psS[pair][:, h % 2 * CH:(h % 2 + 1) * CH], kb[:, h, kt * P:(kt + 1) * P], q,
                                     start=True, stop=True)
                last.then_inc(s_mm, 1)

            def maxima(n, units):
                for u in units:
                    h, qt, k = u // (TPC * CPB), u // CPB % TPC, u % CPB
                    if u == 0:
                        pe.wait_ge(qa_in, 48 * n + 48)
                        if not (isinstance(n, int) and n == 0):
                            pe.wait_ge(rows_done, NH * n)
                    if u % (TPC * CPB) == 0:
                        pe.wait_ge(ka_in[h], 48 * (n // CPB) + 48)
                    if not (isinstance(n, int) and n == 0 and u < 2):
                        pe.wait_ge(mx_part, MU * n + u - 1)
                    pe.matmul(psM[u % 2][:], qa[:, h, qt * P:(qt + 1) * P], ka[:, h, k * CH:(k + 1) * CH],
                              start=True, stop=True).then_inc(m_mm, 1)

            def rows(n):
                pe.wait_ge(ml_done, n + 1)
                for h in range(NH):
                    for qt in range(TPC):
                        last = pe.matmul(psM[0][h * DH:(h + 1) * DH, qt * P:(qt + 1) * P], mcols[:, h * TPC + qt, :], ident16[:],
                                         start=True, stop=True)
                last.then_inc(r_mm, 1)

            def values(n, kt):
                pe.wait_ge(exp_done, 2 * TPB * n + 2 * kt + 2)
                if kt == 0 and not (isinstance(n, int) and n == 0):
                    pe.wait_ge(o_out, n)
                for h in range(NH):
                    rows_h = slice(h * DH, (h + 1) * DH)
                    last = pe.matmul(psO[rows_h, :], vb[:, kt, rows_h], probs[:, kt % 4, h], start=kt == 0, stop=kt == TPB - 1)
                return last

            def sum_step(n, kt):
                if kt == DIRECT[0] and not (isinstance(n, int) and n == 0):
                    pe.wait_ge(z_out, n)
                for h in range(NH):
                    last = pe.matmul(psZ[h * DH:(h + 1) * DH, :], ones[:], probs[:, kt % 4, h], start=kt == DIRECT[0], stop=False)
                return last

            def sum_added(n):
                pe.wait_ge(added, ADDS * n + ADDS)
                for h in range(NH):
                    last = pe.matmul(psZ[h * DH:(h + 1) * DH, :], ones[:], sums[:, h], start=False, stop=True)
                last.then_inc(z_mm, 1)

            DIRECT = [kt for kt in range(TPB) if kt not in ADDED]

            def products(n, kt, between):
                last = values(n, kt)
                if kt in DIRECT:
                    between(1)
                    last = sum_step(n, kt)
                last.then_inc(pv_done, 1)

            def item(n, first=False, last=False):
                for kt in range(TPB):
                    left = list(UNITS[kt])

                    def between(count):
                        if not last:
                            maxima(n + 1, left[:count])
                            del left[:count]

                    if kt == 0:
                        if not first:
                            products(n - 1, TPB - 1, between)
                        between(1)
                    scores(n, kt, 0)
                    between(1)
                    scores(n, kt, 1)
                    between(1)
                    if kt == 1 and not first:
                        sum_added(n - 1)
                        between(1)
                    if kt > 0:
                        products(n, kt - 1, between)
                    between(len(left))
                    if kt == TPB - 1 and not last:
                        rows(n + 1)

            pe.wait_ge(init, 4)
            pe.wait_ge(ident16_done, 1)
            maxima(0, range(MU))
            rows(0)
            item(0, first=True)
            with pe.Fori(1, NI - 1) as n:
                item(n)
            item(NI - 1, last=True)
            products(NI - 1, TPB - 1, lambda count: None)
            sum_added(NI - 1)


def phase_feed_forward(nc, a, s, w, out):
    with ExitStack() as stack:
        m = Memory(nc, stack)
        KF = FF // P
        ident = m.sb("f_ident", [P, P])
        x = m.sb("f_x", [P, 2, TPC, D])
        xn = m.sb("f_xn", [P, TPC, D])
        o_hi = m.sb("f_o_hi", [P, 2, KD, CH], F16)
        o_lo = m.sb("f_o_lo", [P, 2, KD, CH], F16)
        hT32 = m.sb("f_hT32", [P, 2, CH])
        h_hi = m.sb("f_h_hi", [P, KD, CH], F16)
        h_lo = m.sb("f_h_lo", [P, KD, CH], F16)
        g32 = m.sb("f_g32", [P, 2, CH])
        g_hi = m.sb("f_g_hi", [P, KF, CH], F16)
        g_lo = m.sb("f_g_lo", [P, KF, CH], F16)
        scaled = m.sb("f_scaled", [P, 2, D])
        gates = m.sb("f_gates", [P, 2, B, D])
        gated_bias = m.sb("f_gated_bias", [P, 2, B, D])
        b1 = m.sb("f_b1", [P, KF])
        mod = m.sb("f_mod", [P, 2, KD, B])
        mod_c = m.sb("f_mod_c", [P, 2, KD, NCH])
        stats = m.sb("f_stats", [P, TPC, 6])
        mv = m.sb("f_mv", [P, TPC, 2])
        mean_diff = m.sb("f_mean_diff", [P, TPC])
        std = m.sb("f_std", [P, TPC])
        rstd = m.sb("f_rstd", [P, TPC])
        nmr = m.sb("f_nmr", [P, TPC])
        eps = m.sb("f_eps", [P, 1])
        psT = [m.ps(f"f_psT{i}") for i in range(2)]
        psW = [m.ps(f"f_psW{i}") for i in range(2)]
        psO = [m.ps(f"f_psO{i}") for i in range(2)]
        psY = [m.ps(f"f_psY{i}") for i in range(2)]

        rows_in = m.sem("f_rows_in")
        mod_done = m.sem("f_mod_done")
        bias_gated = m.sem("f_bias_gated")
        gates_scaled = m.sem("f_gates_scaled")
        x_in = [m.sem(f"f_x_in{i}") for i in range(2)]
        o_in = [m.sem(f"f_o_in{i}") for i in range(2)]
        stored = [m.sem(f"f_stored{i}") for i in range(2)]
        bo_added = m.sem("f_bo_added")
        b2_added = m.sem("f_b2_added")
        wo_mm = m.sem("f_wo_mm")
        scaled_done = m.sem("f_scaled_done")
        x2_done = m.sem("f_x2_done")
        stats_done = m.sem("f_stats_done")
        mv_done = m.sem("f_mv_done")
        std_done = m.sem("f_std_done")
        rstd_done = m.sem("f_rstd_done")
        nmr_done = m.sem("f_nmr_done")
        norm_done = m.sem("f_norm_done")
        turned = m.sem("f_turned")
        h32_done = m.sem("f_h32_done")
        h_hi_done = m.sem("f_h_hi_done")
        h_lo_done = m.sem("f_h_lo_done")
        w1_mm = m.sem("f_w1_mm")
        g32_done = m.sem("f_g32_done")
        g_hi_done = m.sem("f_g_hi_done")
        g_lo_done = m.sem("f_g_lo_done")
        w2_mm = m.sem("f_w2_mm")
        y_scaled = m.sem("f_y_scaled")
        y_done = m.sem("f_y_done")

        out_v = out.rearrange("b (c t p) d -> (b c) p t d", p=P, t=TPC)
        ADA = ("shift1", "scale1", "gate1", "shift2", "scale2", "gate2")

        def ada_part(b, name):
            i = ADA.index(name)
            return s["ada"][b, i * D:(i + 1) * D]

        block = stack.enter_context(nc.Block())

        @block.sync
        def _(sp):
            def load_o(c, r):
                for half, t in enumerate((o_hi, o_lo)):
                    sp.dma_start(t[:, r], s["o"].rearrange("h (g c) p t -> h c p g t", g=KD)[half, c]).then_inc(o_in[r], 16)

            def load_x(c, r):
                sp.dma_start(x[:, r], s["x1"][c]).then_inc(x_in[r], 16)

            def store(c, r):
                sp.wait_ge(y_done, TPC * c + TPC)
                sp.dma_start(out_v[c], x[:, r]).then_inc(stored[r], 16)

            load_o(0, 0)
            for b in range(B):
                for i, (gate, bias) in enumerate((("gate1", "L1_cond_bo"), ("gate2", "L1_cond_b2"))):
                    sp.dma_start(gates[:, i, b], bcast_rows(ada_part(b, gate))).then_inc(rows_in, 16)
                    sp.dma_start(gated_bias[:, i, b], bcast_rows(a[bias])).then_inc(rows_in, 16)
                for i, name in enumerate(("shift2", "scale2")):
                    sp.dma_start(mod[:, i, :, b], ada_part(b, name).rearrange("(k p) -> p k", p=P),
                                 allow_slow_non_contiguous=True).then_inc(rows_in, 16)
            load_x(0, 0)
            sp.dma_start(ident[:], a["c_ident"]).then_inc(rows_in, 16)
            sp.dma_start(b1[:], a["L1_cond_b1"].rearrange("(k p) -> p k", p=P), allow_slow_non_contiguous=True).then_inc(rows_in, 16)
            load_o(1, 1)
            load_x(1, 1)
            with sp.Fori(0, NCH // 2 - 1) as i:
                for r in range(2):
                    c = 2 * i + r
                    sp.wait_ge(wo_mm, TPC * c + TPC)
                    load_o(c + 2, r)
                    store(c, r)
                    sp.wait_ge(stored[r], 16 * i + 16)
                    load_x(c + 2, r)
            for r in range(2):
                store(NCH - 2 + r, r)
            for r in range(2):
                sp.wait_ge(stored[r], 16 * (NCH // 2))

        @block.gpsimd
        def _(pool):
            def batch(t, i, c):
                if isinstance(c, int):
                    return t[:, i, c // CPB:c // CPB + 1].to_broadcast([P, TPC, D])
                return t[:, i, bass.ds(c // CPB, 1)].to_broadcast([P, TPC, D])

            def add_bo(c, r, i):
                pool.wait_ge(x_in[r], 16 * i + 16)
                nc.gpsimd.tensor_tensor(x[:, r], x[:, r], batch(gated_bias, 0, c), ALU.add).then_inc(bo_added, 1)

            def add_b2(c, r):
                pool.wait_ge(norm_done, TPC * c + TPC)
                nc.gpsimd.tensor_tensor(x[:, r], x[:, r], batch(gated_bias, 1, c), ALU.add).then_inc(b2_added, 1)

            pool.wait_ge(rows_in, 224)
            nc.gpsimd.tensor_tensor(gated_bias[:], gated_bias[:], gates[:], ALU.mult).then_inc(bias_gated, 1)
            pool.wait_ge(bias_gated, 1)
            add_bo(0, 0, 0)
            add_b2(0, 0)
            add_bo(1, 1, 0)
            add_b2(1, 1)
            with pool.Fori(0, NCH // 2 - 1) as i:
                for r in range(2):
                    add_bo(2 * i + 2 + r, r, i + 1)
                    add_b2(2 * i + 2 + r, r)

        @block.scalar
        def _(act):
            def norm(c, r):
                act.wait_ge(mv_done, TPC * c + TPC)
                if not (isinstance(c, int) and c == 0):
                    act.wait_ge(rstd_done, c)
                    act.wait_ge(turned, KD * c)
                nc.scalar.activation(std[:], mv[:, :, 1], ACT.Sqrt, bias=eps[:], scale=1.0 / D).then_inc(std_done, 1)
                act.wait_ge(nmr_done, c + 1)
                for t in range(TPC):
                    nc.scalar.activation(xn[:, t], x[:, r, t], ACT.Identity, bias=nmr[:, t:t + 1],
                                         scale=rstd[:, t:t + 1]).then_inc(norm_done, 1)

            def modulate(c):
                for k in range(KD):
                    act.wait_ge(turned, KD * c + k + 1)
                    if not (isinstance(c, int) and c == 0 and k < 2):
                        act.wait_ge(h_lo_done, KD * c + k - 1)
                    shift, scale = mod_c[:, 0, k, bass.ds(c, 1)], mod_c[:, 1, k, bass.ds(c, 1)]
                    nc.scalar.activation(hT32[:, k % 2], psT[k % 2][:], ACT.Identity, bias=shift, scale=scale).then_inc(h32_done, 1)
                    nc.scalar.activation(h_hi[:, k], psT[k % 2][:], ACT.Identity, bias=shift, scale=scale).then_inc(h_hi_done, 1)

            def gelus(c):
                for j in range(KF):
                    act.wait_ge(w1_mm, KF * c + j + 1)
                    if not (isinstance(c, int) and c == 0 and j < 2):
                        act.wait_ge(g_lo_done, KF * c + j - 1)
                    nc.scalar.activation(g32[:, j % 2], psW[j % 2][:], ACT.Gelu, bias=b1[:, j:j + 1], scale=1.0 / WS).then_inc(g32_done, 1)
                    nc.scalar.activation(g_hi[:, j], psW[j % 2][:], ACT.Gelu, bias=b1[:, j:j + 1], scale=1.0 / WS).then_inc(g_hi_done, 1)

            norm(0, 0)
            act.wait_ge(mod_done, 3)
            modulate(0)
            gelus(0)
            norm(1, 1)
            modulate(1)
            with act.Fori(0, NCH // 2 - 1) as i:
                for u in range(2):
                    c = 2 * i + 1 + u
                    gelus(c)
                    norm(c + 1, u)
                    modulate(c + 1)
            gelus(NCH - 1)

        @block.vector
        def _(dve):
            def batch(t, i, c):
                if isinstance(c, int):
                    return t[:, i, c // CPB]
                return t[:, i, bass.ds(c // CPB, 1)].rearrange("p a d -> p (a d)")

            def attention_out(c, r):
                dve.wait_ge(bo_added, c + 1)
                for t in range(TPC):
                    dve.wait_ge(wo_mm, TPC * c + t + 1)
                    if not (isinstance(c, int) and c == 0 and t < 2):
                        dve.wait_ge(x2_done, TPC * c + t - 1)
                    if t < 2 and not (isinstance(c, int) and c < 2):
                        dve.wait_ge(y_done, TPC * c - TPC - 1)
                    nc.vector.tensor_tensor(scaled[:, t % 2], psO[t % 2][:], batch(gates, 0, c), ALU.mult).then_inc(scaled_done, 1)
                    dve.wait_ge(scaled_done, TPC * c + t + 1)
                    nc.vector.tensor_tensor(x[:, r, t], x[:, r, t], scaled[:, t % 2], ALU.add).then_inc(x2_done, 1)
                    dve.wait_ge(x2_done, TPC * c + t + 1)
                    nc.vector.bn_stats(stats[:, t], x[:, r, t]).then_inc(stats_done, 1)
                if not (isinstance(c, int) and c == 0):
                    dve.wait_ge(std_done, c)
                combine_moments(nc, dve, stats, mv, mean_diff, stats_done, TPC * c, mv_done, TPC * c)
                dve.wait_ge(std_done, c + 1)
                if not (isinstance(c, int) and c == 0):
                    dve.wait_ge(norm_done, TPC * c)
                nc.vector.reciprocal(rstd[:], std[:]).then_inc(rstd_done, 1)
                dve.wait_ge(rstd_done, c + 1)
                nc.vector.scalar_tensor_tensor(nmr[:], mv[:, :, 0], -0.5, rstd[:], ALU.mult, ALU.mult).then_inc(nmr_done, 1)

            def modulate(c):
                for k in range(KD):
                    dve.wait_ge(h32_done, KD * c + k + 1)
                    dve.wait_ge(h_hi_done, KD * c + k + 1)
                    nc.vector.tensor_tensor(h_lo[:, k], hT32[:, k % 2], h_hi[:, k], ALU.subtract).then_inc(h_lo_done, 1)

            def gelus(c):
                for j in range(KF):
                    dve.wait_ge(g32_done, KF * c + j + 1)
                    dve.wait_ge(g_hi_done, KF * c + j + 1)
                    nc.vector.tensor_tensor(g_lo[:, j], g32[:, j % 2], g_hi[:, j], ALU.subtract).then_inc(g_lo_done, 1)

            def outputs(c, r, tiles):
                dve.wait_ge(b2_added, c + 1)
                for t in tiles:
                    dve.wait_ge(w2_mm, TPC * c + t + 1)
                    if isinstance(c, int) and c == 0 and t < 2:
                        dve.wait_ge(x2_done, TPC)
                    else:
                        dve.wait_ge(y_done, TPC * c + t - 1)
                    nc.vector.tensor_tensor(scaled[:, t % 2], psY[t % 2][:], batch(gates, 1, c), ALU.mult).then_inc(y_scaled, 1)
                    dve.wait_ge(y_scaled, TPC * c + t + 1)
                    nc.vector.tensor_tensor(x[:, r, t], x[:, r, t], scaled[:, t % 2], ALU.add).then_inc(y_done, 1)

            nc.vector.memset(eps[:], EPS_LN1).then_inc(mod_done, 1)
            dve.wait_ge(rows_in, 224)
            dve.wait_ge(mod_done, 1)
            for i, one in enumerate((0.0, 1.0)):
                nc.vector.tensor_scalar_add(mod_c[:, i].rearrange("p k (b c) -> p (k b) c", b=B),
                                            mod[:, i].rearrange("p k b -> p (k b)").unsqueeze(2).to_broadcast([P, KD * B, CPB]),
                                            one).then_inc(mod_done, 1)
            dve.wait_ge(bias_gated, 1)
            nc.vector.tensor_scalar(gates[:], gates[:], 1.0 / WS, None, ALU.mult).then_inc(gates_scaled, 1)
            dve.wait_ge(gates_scaled, 1)
            attention_out(0, 0)
            modulate(0)
            gelus(0)
            attention_out(1, 1)
            outputs(0, 0, range(3))
            modulate(1)
            outputs(0, 0, range(3, 4))
            with dve.Fori(0, NCH // 2 - 1) as i:
                for u in range(2):
                    c = 2 * i + 1 + u
                    gelus(c)
                    attention_out(c + 1, u)
                    outputs(c, 1 - u, range(3))
                    modulate(c + 1)
                    outputs(c, 1 - u, range(3, 4))
            gelus(NCH - 1)
            outputs(NCH - 1, 1, range(4))

        @block.tensor
        def _(pe):
            def attention_out(c, r, i):
                pe.wait_ge(o_in[r], 32 * i + 32)
                for t in range(TPC):
                    if not (isinstance(c, int) and c == 0 and t < 2):
                        pe.wait_ge(scaled_done, TPC * c + t - 1)
                    cols = slice(t * P, (t + 1) * P)
                    split_product(pe, psO[t % 2][:], [(o_hi[:, r, k, cols], o_lo[:, r, k, cols], w["wo_hi"][:, k, :], w["wo_lo"][:, k, :])
                                                      for k in range(KD)]).then_inc(wo_mm, 1)

            def turn(c):
                pe.wait_ge(norm_done, TPC * c + TPC)
                for k in range(KD):
                    if not (isinstance(c, int) and c == 0 and k < 2):
                        pe.wait_ge(h_hi_done, KD * c + k - 1)
                    for t in range(TPC):
                        last = pe.transpose(psT[k % 2][:, t * P:(t + 1) * P], xn[:, t, k * P:(k + 1) * P], ident[:])
                    last.then_inc(turned, 1)

            def expand(c):
                pe.wait_ge(h_lo_done, KD * c + KD)
                for j in range(KF):
                    if not (isinstance(c, int) and c == 0 and j < 2):
                        pe.wait_ge(g_hi_done, KF * c + j - 1)
                    cols = slice(j * P, (j + 1) * P)
                    split_product(pe, psW[j % 2][:], [(w["w1_hi"][:, k, cols], w["w1_lo"][:, k, cols], h_hi[:, k, :], h_lo[:, k, :])
                                                      for k in range(KD)]).then_inc(w1_mm, 1)

            def contract(c, tiles):
                for t in tiles:
                    if t == 0:
                        pe.wait_ge(g_lo_done, KF * c + KF)
                    if not (isinstance(c, int) and c == 0 and t < 2):
                        pe.wait_ge(y_scaled, TPC * c + t - 1)
                    cols = slice(t * P, (t + 1) * P)
                    split_product(pe, psY[t % 2][:], [(g_hi[:, k, cols], g_lo[:, k, cols], w["w2_hi"][:, k, :], w["w2_lo"][:, k, :])
                                                      for k in range(KF)]).then_inc(w2_mm, 1)

            pe.wait_ge(rows_in, 224)
            attention_out(0, 0, 0)
            turn(0)
            expand(0)
            attention_out(1, 1, 0)
            contract(0, range(3))
            turn(1)
            contract(0, range(3, 4))
            with pe.Fori(0, NCH // 2 - 1) as i:
                for u in range(2):
                    c = 2 * i + 1 + u
                    expand(c)
                    attention_out(c + 1, u, i + 1)
                    contract(c, range(3))
                    turn(c + 1)
                    contract(c, range(3, 4))
            expand(NCH - 1)
            contract(NCH - 1, range(4))




def build(nc, a, out):
    s = {}
    for name in ("x_hi", "x_lo", "c_hi", "c_lo"):
        s[name] = nc.dram_tensor("scr_" + name, (NCH, P, KD, CH), F16, kind="Internal").ap()
    s["g"] = nc.dram_tensor("scr_g", (NCH, 2 * H0, CH), F16, kind="Internal").ap()
    s["x1"] = nc.dram_tensor("scr_x1", (NCH, P, TPC, D), F32, kind="Internal").ap()
    for name in "qk":
        s[name] = nc.dram_tensor("scr_" + name, (2, KD * NCH, P, CH), F16, kind="Internal").ap()
    s["o"] = nc.dram_tensor("scr_o", (2, KD * NCH, P, CH), F16, kind="Internal").ap()
    s["v"] = nc.dram_tensor("scr_v", (KD * NCH, P, TPC, P), F32, kind="Internal").ap()
    s["ada"] = nc.dram_tensor("scr_ada", (B, NADA), F32, kind="Internal").ap()
    with ExitStack() as stack:
        m = Memory(nc, stack)
        w = {}
        with ExitStack() as stack_qkv:
            m_qkv = Memory(nc, stack_qkv)
            w["qkv"] = m_qkv.sb("qkv_weights", [P, 6, KD * D], F16)
            for i, name in enumerate(("wq", "wk", "wv")):
                for j, half in enumerate(("hi", "lo")):
                    w[f"{name}_{half}"] = w["qkv"][:, 2 * i + j].rearrange("p (k n) -> p k n", n=D)
            with ExitStack() as stack_0:
                m_0 = Memory(nc, stack_0)
                for name, shape in (("val", [P, KD, HK]), ("f1", [P, KD, D]), ("f2", [P, KD, D]), ("of", [P, KH, D])):
                    for half in ("hi", "lo"):
                        w[f"{name}_{half}"] = m_0.sb(f"{name}_{half}", shape, F16)
                w["b1"] = m_0.sb("b1_columns", [P, KD, NCH])
                phase_prepare(nc, a, s, w)
                phase_layer0(nc, a, s, w)
            for name, shape in (("wo", [P, KD, D]), ("w1", [P, KD, FF]), ("w2", [P, FF // P, D])):
                for half in ("hi", "lo"):
                    w[f"{name}_{half}"] = m_qkv.sb(f"{name}_{half}", shape, F16)
            phase_qkv(nc, a, s, w)
            phase_attention(nc, a, s, w)
            phase_feed_forward(nc, a, s, w, out)


_IN = ['x', 'cond_1024', 'L0_cond_attention_weights', 'L0_cond_temperature', 'L0_cond_values', 'L0_cond_operator',
       'L0_cond_ff1', 'L0_cond_ff1_bias', 'L0_cond_ff2', 'L0_cond_ff2_bias', 'L0_cond_ln_gamma', 'L0_cond_ln_beta',
       'L1_cond_W_ada', 'L1_cond_b_ada', 'L1_cond_Wq', 'L1_cond_bq', 'L1_cond_Wk', 'L1_cond_bk', 'L1_cond_Wv',
       'L1_cond_bv', 'L1_cond_Wo', 'L1_cond_bo', 'L1_cond_W1', 'L1_cond_b1', 'L1_cond_W2', 'L1_cond_b2']


def constants():
    sel = np.zeros((P, KH, P), np.float16)
    for k in range(2 * H0):
        for j in range(KH):
            for c in range(P):
                sel[k, j, c] = (k % H0) == (j * P + c) // K0
    krows = np.zeros((P, 1), np.float32)
    krows[3 * DH:3 * DH + 2, 0] = (WS, 1.0)
    count = np.arange(1, S + 1, dtype=np.float32)
    return {"c_ident": np.eye(P, dtype=np.float32), "c_inv_counts": (1.0 / count).astype(np.float32),
            "c_krows": krows, "c_counts": np.ascontiguousarray(count.reshape(TPB, P).T), "c_sel": sel}


def kernel(**inputs):
    import concourse.bacc as bacc
    from concourse.bass_utils import run_bass_kernel_spmd

    nc = bacc.Bacc("TRN2", target_bir_lowering=False, num_devices=1)
    arrays = {name: np.ascontiguousarray(inputs[name]) for name in _IN}
    arrays.update(constants())
    aps = {}
    for name, v in arrays.items():
        aps[name] = nc.dram_tensor(name + "_in", v.shape, mybir.dt.from_np(v.dtype), kind="ExternalInput").ap()
    out = nc.dram_tensor("out", (B, S, D), F32, kind="ExternalOutput").ap()
    build(nc, aps, out)
    r = run_bass_kernel_spmd(nc, [{name + "_in": v for name, v in arrays.items()}], core_ids=[0])
    return r.results[0]["out"]
```

```python
import numpy as np
from contextlib import ExitStack

import concourse.bass as bass
from concourse import mybir

F32 = mybir.dt.float32
F16 = mybir.dt.float16
ACT = mybir.ActivationFunctionType
ALU = mybir.AluOpType
AX = mybir.AxisListType
RMAX = bass.bass_isa.ReduceOp.max

P = 128
B, S, D = 2, 2048, 512
T = B * S
H0, K0 = 16, 64
HK = H0 * K0
H1, DH = 16, 32
FF = 2048
CH = 512
NCH = T // CH
CPB = S // CH
KD = D // P
KH = HK // P
TPC = CH // P
TPB = S // P
NADA = 6 * D
WS = 64.0
HALVES = (range(0, 2), range(2, 4))
EPS_ATT, EPS_LN0, EPS_LN1 = 1e-30, 1e-6, 1e-5


class Memory:

    def __init__(self, nc, stack):
        self.nc, self.stack = nc, stack
        self.sems = []
        stack.callback(self.clear_sems)

    def sb(self, name, shape, dt=F32):
        return self.stack.enter_context(self.nc.sbuf_tensor(name, shape, dt))

    def ps(self, name, shape=(P, CH), dt=F32):
        return self.stack.enter_context(self.nc.psum_tensor(name, list(shape), dt))

    def sem(self, name):
        self.sems.append(self.nc.alloc_semaphore(name))
        return self.sems[-1]

    def clear_sems(self):
        if self.sems:
            self.nc.clear_and_free_semaphores(self.sems)
            self.nc.all_engine_barrier()


def split_weight_tiles(w, cols):
    v = w.rearrange("(k p) n -> p k n", p=P)
    return [v[:, :, c:c + cols] for c in range(0, w.shape[1], cols)]


def combine_moments(nc, dve, stats, mv, diff, stats_done, stats_before, mv_done, mv_before):
    halves = stats[:].rearrange("p t (h m) -> p t m h", h=2)
    dve.wait_ge(stats_done, stats_before + TPC)
    nc.vector.tensor_tensor(diff[:], halves[:, :, 1, 0], halves[:, :, 1, 1], ALU.subtract).then_inc(mv_done, 1)
    nc.vector.tensor_tensor(mv[:], halves[:, :, 1:3, 0], halves[:, :, 1:3, 1], ALU.add).then_inc(mv_done, 1)
    dve.wait_ge(mv_done, mv_before + 2)
    nc.vector.tensor_tensor(diff[:], diff[:], diff[:], ALU.mult).then_inc(mv_done, 1)
    dve.wait_ge(mv_done, mv_before + 3)
    nc.vector.scalar_tensor_tensor(mv[:, :, 1], diff[:], D / 4, mv[:, :, 1], ALU.mult, ALU.add).then_inc(mv_done, 1)


def bcast_rows(vec, n=P):
    return vec.partition_broadcast(n)


def phase_prepare(nc, a, s, w):
    with ExitStack() as stack:
        m = Memory(nc, stack)
        QT = 4
        NQ = TPB // QT
        NU = B * KD
        NA = NADA // CH
        ident = w["ident"]
        inv_counts = m.sb("p_inv_counts", [P, S])
        counts = m.sb("p_counts", [P, TPB])
        ones = m.sb("p_ones", [P, 1])
        x_tok = m.sb("p_x_tok", [P, 2, TPB, P])
        xT = m.sb("p_xT", [P, 2, S])
        x_hi = m.sb("p_x_hi", [P, 2, S], F16)
        x_lo = m.sb("p_x_lo", [P, 2, S], F16)
        c32 = m.sb("p_c32", [P, 2, S])
        c_hi = m.sb("p_c_hi", [P, 2, S], F16)
        c_lo = m.sb("p_c_lo", [P, 2, S], F16)
        aw = m.sb("p_aw", [P, KD, H0])
        aw_hi = m.sb("p_aw_hi", [P, KD, H0], F16)
        aw_lo = m.sb("p_aw_lo", [P, KD, H0], F16)
        temp = m.sb("p_temp", [P, H0])
        mx = m.sb("p_mx", [P, H0])
        mxa = m.sb("p_mxa", [P, H0])
        att = m.sb("p_att", [P, TPB, H0])
        atc = m.sb("p_atc", [P, TPB, H0])
        gate = m.sb("p_gate", [P, B, TPB, H0])
        stage = m.sb("p_stage", [P, 2, KD * CH])
        oper = x_tok[:].rearrange("p r t f -> p (r t f)").rearrange("p (k n) -> p k n", n=D)
        operT = xT[:].rearrange("p r t -> p (r t)").rearrange("p (k n) -> p k n", n=HK)
        gT_hi, gT_lo = x_hi[0:H0], x_lo[0:H0]
        ff1b = m.sb("p_ff1b", [P, KD, D])
        condT = m.sb("p_condT", [P, KD, B])
        ff1_bias = m.sb("p_ff1_bias", [P, KD])
        ada = m.sb("p_ada", [B, 2, CH])
        b_ada = m.sb("p_b_ada", [B, 2, CH])

        psT = [m.ps(f"p_psT{i}") for i in range(2)]
        psA = [m.ps(f"p_psA{i}") for i in range(B)]
        psG = m.ps("p_psG")
        psW = [m.ps(f"p_psW{i}") for i in range(2)]
        psD = m.ps("p_psD")

        consts_in = m.sem("p_consts_in")
        ident_in = m.sem("p_ident_in")
        aw_in = m.sem("p_aw_in")
        x_in = [m.sem(f"p_x_in{i}") for i in range(2)]
        w_in = [m.sem(f"p_w_in{i}") for i in range(2)]
        oper_in = m.sem("p_oper_in")
        ff1b_in = m.sem("p_ff1b_in")
        first_x_in = [m.sem(f"p_first_x_in{i}") for i in range(NQ)]
        ada_in = [m.sem(f"p_ada_in{i}") for i in range(2)]
        small_in = m.sem("p_small_in")
        aw_split = m.sem("p_aw_split")
        temp_scaled = m.sem("p_temp_scaled")
        x_turned = m.sem("p_x_turned")
        xT_written = m.sem("p_xT_written")
        x_lo_done = m.sem("p_x_lo_done")
        scanned = m.sem("p_scanned")
        meaned = m.sem("p_meaned")
        c_hi_done = m.sem("p_c_hi_done")
        c_lo_done = m.sem("p_c_lo_done")
        x_stored = [m.sem(f"p_x_stored{i}") for i in range(2)]
        c_stored = [m.sem(f"p_c_stored{i}") for i in range(2)]
        att_mm = m.sem("p_att_mm")
        mx_done = m.sem("p_mx_done")
        mx_all = m.sem("p_mx_all")
        att_step = m.sem("p_att_step")
        att_arg = m.sem("p_att_arg")
        att_exp = m.sem("p_att_exp")
        gate_done = m.sem("p_gate_done")
        g_turned = m.sem("p_g_turned")
        gT_hi_done = m.sem("p_gT_hi_done")
        gT_lo_done = m.sem("p_gT_lo_done")
        g_stored = m.sem("p_g_stored")
        w_hi_done = m.sem("p_w_hi_done")
        w_lo_done = m.sem("p_w_lo_done")
        oper_turned = m.sem("p_oper_turned")
        operT_written = m.sem("p_operT_written")
        of_mm = m.sem("p_of_mm")
        of_hi_done = m.sem("p_of_hi_done")
        of_lo_done = m.sem("p_of_lo_done")
        b1_mm = m.sem("p_b1_mm")
        b1_done = m.sem("p_b1_done")
        ada_mm = m.sem("p_ada_mm")
        ada_done = m.sem("p_ada_done")
        ada_stored = m.sem("p_ada_stored")

        x_v = a["x"].rearrange("b (t p) (k f) -> b k p t f", p=P, f=P)
        ada_v = split_weight_tiles(a["L1_cond_W_ada"], CH)

        pieces = []
        for name, hi, lo in (("L0_cond_values", "val_hi", "val_lo"), ("L0_cond_ff1", "f1_hi", "f1_lo"),
                             ("L0_cond_ff2", "f2_hi", "f2_lo"), ("L1_cond_Wq", "wq_hi", "wq_lo"),
                             ("L1_cond_Wk", "wk_hi", "wk_lo"), ("L1_cond_Wv", "wv_hi", "wv_lo")):
            src = a[name]
            if name == "L0_cond_values":
                src = src.rearrange("i h k -> i (h k)")
            if name == "L0_cond_ff1":
                src = src[0:D, :]
            for c, part in enumerate(split_weight_tiles(src, CH)):
                pieces.append((part, w[hi][:, :, c * CH:(c + 1) * CH], w[lo][:, :, c * CH:(c + 1) * CH]))

        def staged(n):
            return stage[:, n % 2].rearrange("p (k c) -> p k c", k=KD)

        block = stack.enter_context(nc.Block())

        @block.sync
        def _(sp):
            def load_x(n):
                sp.dma_start(x_tok[:, n % 2], x_v[n // KD, n % KD]).then_inc(x_in[n % 2], 16)

            def store_halves(n, names, tiles, sem):
                for name, t in zip(names, tiles):
                    dst = s[name].rearrange("(b c) p k t -> b k p c t", b=B)[n // KD, n % KD]
                    sp.dma_start(dst, t[:, n % 2].rearrange("p (c t) -> p c t", c=CPB)).then_inc(sem[n % 2], 16)

            def store_x(n):
                sp.wait_ge(xT_written, (n + 1) * 2 * NQ)
                sp.wait_ge(x_lo_done, n + 1)
                store_halves(n, ("x_hi", "x_lo"), (x_hi, x_lo), x_stored)

            def store_c(n):
                sp.wait_ge(c_hi_done, (n + 1) * 2)
                sp.wait_ge(c_lo_done, (n + 1) * 2)
                store_halves(n, ("c_hi", "c_lo"), (c_hi, c_lo), c_stored)

            def store_ada(n):
                sp.wait_ge(ada_done, n + 1)
                if n >= 1:
                    sp.wait_ge(ada_stored, 16 * n)
                sp.dma_start(s["ada"][:, n * CH:(n + 1) * CH], ada[:, n % 2]).then_inc(ada_stored, 16)

            for q in range(NQ):
                quarter = slice(q * QT, (q + 1) * QT)
                sp.dma_start(x_tok[:, 0, quarter], x_v[0, 0][:, quarter]).then_inc(first_x_in[q], 16)
                if q == 0:
                    sp.dma_start(ident[:], a["c_ident"]).then_inc(ident_in, 16)
            sp.dma_start(aw[:], a["L0_cond_attention_weights"].rearrange("(k p) n -> p k n", p=P)).then_inc(aw_in, 16)
            sp.dma_start(temp[:], bcast_rows(a["L0_cond_temperature"].rearrange("a b h -> (a b h)"))).then_inc(aw_in, 16)
            load_x(1)
            sp.dma_start(inv_counts[:], bcast_rows(a["c_inv_counts"])).then_inc(consts_in, 16)
            sp.dma_start(counts[:], a["c_counts"]).then_inc(consts_in, 16)
            sp.dma_start(w["sel"][:], a["c_sel"]).then_inc(consts_in, 16)
            for n in range(NU):
                if n + 2 < NU:
                    sp.wait_ge(x_turned, (n + 1) * NQ)
                    load_x(n + 2)
                store_x(n)
                if n >= 1:
                    store_c(n - 1)
                if n >= 3:
                    store_ada(n - 3)
            store_c(NU - 1)
            store_ada(NA - 1)
            sp.wait_ge(ada_stored, 16 * NA)
            for b in range(B):
                sp.wait_ge(gT_hi_done, NQ * (b + 1))
                sp.wait_ge(gT_lo_done, NQ * (b + 1))
                for half, t in enumerate((gT_hi, gT_lo)):
                    sp.dma_start(s["g"][b * CPB:(b + 1) * CPB].rearrange("c h t -> h c t")[half * H0:(half + 1) * H0],
                                 t[:, b].rearrange("h (c t) -> h c t", c=CPB)).then_inc(g_stored, 16)
            sp.wait_ge(g_stored, 16 * 2 * B)
            for i in range(2):
                sp.wait_ge(x_stored[i], 32 * NU // 2)
                sp.wait_ge(c_stored[i], 32 * NU // 2)

        @block.gpsimd
        def _(pool):
            def load_piece(n):
                pool.dma_start(staged(n), pieces[n][0]).then_inc(w_in[n % 2], 16)

            def load_ada(n):
                pool.dma_start(staged(n), ada_v[n]).then_inc(ada_in[n % 2], 16)
                pool.dma_start(b_ada[:, n % 2], bcast_rows(a["L1_cond_b_ada"][n * CH:(n + 1) * CH], B)).then_inc(ada_in[n % 2], 16)

            def largest(b):
                pool.wait_ge(mx_done, b + 1)
                nc.gpsimd.partition_all_reduce(mxa[:], mx[:], P, RMAX).then_inc(mx_all, 1)

            for b in range(B):
                pool.dma_start(condT[:, :, b], a["cond_1024"][b].rearrange("(k p) -> p k", p=P), allow_slow_non_contiguous=True).then_inc(small_in, 16)
            pool.dma_start(ff1_bias[:], a["L0_cond_ff1_bias"].rearrange("a b (k p) -> p (a b k)", p=P), allow_slow_non_contiguous=True).then_inc(small_in, 16)
            load_ada(0)
            for n in range(NU):
                if n == NU - 1:
                    pool.wait_ge(x_turned, NU * NQ)
                    pool.dma_start(oper, a["L0_cond_operator"].rearrange("(k p) n -> p k n", p=P)).then_inc(oper_in, 16)
                pool.wait_ge(xT_written, (n + 1) * 2 * NQ)
                if n >= 2:
                    pool.wait_ge(x_stored[n % 2], 32 * (n // 2))
                    pool.wait_ge(att_mm, n - 1)
                nc.gpsimd.tensor_tensor(x_lo[:, n % 2], xT[:, n % 2], x_hi[:, n % 2], ALU.subtract).then_inc(x_lo_done, 1)
                if n == 0:
                    load_ada(1)
                if n == KD:
                    pool.dma_start(ff1b[:], a["L0_cond_ff1"][D:2 * D, :].rearrange("(k p) n -> p k n", p=P)).then_inc(ff1b_in, 16)
                if n == KD + 1:
                    largest(0)
                if n >= 2:
                    pool.wait_ge(ada_mm, n - 1)
                    pool.wait_ge(ada_done, n - 1)
                    if n < NA:
                        load_ada(n)
                    else:
                        load_piece(n - NA)
            largest(1)
            for n in range(2, len(pieces)):
                pool.wait_ge(w_lo_done, n - 1)
                load_piece(n)

        @block.scalar
        def _(act):
            act.wait_ge(aw_in, 32)
            nc.scalar.activation(aw_hi[:], aw[:], ACT.Identity, scale=WS).then_inc(aw_split, 1)
            nc.scalar.mul(temp[:], temp[:], 1.0 / WS).then_inc(temp_scaled, 1)

            def copies(n):
                for q in range(NQ):
                    act.wait_ge(x_turned, n * NQ + q + 1)
                    if q == 0 and n >= 2:
                        act.wait_ge(scanned, n - 1)
                        act.wait_ge(x_lo_done, n - 1)
                        act.wait_ge(att_mm, n - 1)
                        act.wait_ge(x_stored[n % 2], 32 * (n // 2))
                    cols = slice(q * CH, (q + 1) * CH)
                    nc.scalar.copy(xT[:, n % 2, cols], psT[q % 2][:]).then_inc(xT_written, 1)
                    nc.scalar.copy(x_hi[:, n % 2, cols], psT[q % 2][:]).then_inc(xT_written, 1)

            def mean_hi(n):
                for h in range(2):
                    act.wait_ge(meaned, 2 * n + h + 1)
                    if n >= 2:
                        act.wait_ge(c_stored[n % 2], 32 * (n // 2))
                    half = slice(h * S // 2, (h + 1) * S // 2)
                    nc.scalar.copy(c_hi[:, n % 2, half], c32[:, n % 2, half]).then_inc(c_hi_done, 1)

            def exp(b):
                act.wait_ge(att_arg, b + 1)
                nc.scalar.activation(att[:], att[:], ACT.Exp).then_inc(att_exp, 1)

            def piece_hi(n):
                act.wait_ge(w_in[n % 2], 16 * (n // 2 + 1))
                nc.scalar.activation(pieces[n][1], staged(n), ACT.Identity, scale=WS).then_inc(w_hi_done, 1)

            copies(0)
            for n in range(NU):
                if n + 1 < NU:
                    copies(n + 1)
                mean_hi(n)
                if n == KD + 1:
                    exp(0)
            exp(1)
            piece_hi(0)
            act.wait_ge(scanned, NU)
            act.wait_ge(x_lo_done, NU)
            for i in range(2 * KD):
                act.wait_ge(oper_turned, i + 1)
                k, half = i // 2, i % 2
                nc.scalar.copy(operT[:, k, half * CH:(half + 1) * CH], psT[i % 2][:]).then_inc(operT_written, 1)
            piece_hi(1)
            for i in range(2):
                act.wait_ge(x_stored[i], 32 * NU // 2)
            for j in range(KH):
                act.wait_ge(of_mm, j + 1)
                nc.scalar.activation(w["of_hi"][:, j], psW[j % 2][:], ACT.Identity, scale=WS).then_inc(of_hi_done, 1)
                act.wait_ge(g_turned, j + 1)
                nc.scalar.copy(gT_hi[:, j // NQ, j % NQ * CH:(j % NQ + 1) * CH], psG[0:H0, :]).then_inc(gT_hi_done, 1)
                if j % 2 == 0:
                    piece_hi(2 + j // 2)
            for n in range(2 + KH // 2, len(pieces)):
                piece_hi(n)

        @block.vector
        def _(dve):
            nc.vector.memset(ones[:], 1.0).then_inc(att_step, 1)
            dve.wait_ge(aw_split, 1)
            nc.vector.scalar_tensor_tensor(aw_lo[:], aw[:], WS, aw_hi[:], ALU.mult, ALU.subtract).then_inc(aw_split, 1)
            dve.wait_ge(att_step, 1)

            def mean(n):
                r = n % 2
                dve.wait_ge(xT_written, (n + 1) * 2 * NQ)
                if n >= 2:
                    dve.wait_ge(c_lo_done, 2 * (n - 1))
                    dve.wait_ge(c_hi_done, 2 * (n - 1))
                nc.vector.tensor_tensor_scan(c32[:, r], ones[:, 0:1].to_broadcast([P, S]), xT[:, r], 0.0,
                                             ALU.mult, ALU.add).then_inc(scanned, 1)
                dve.wait_ge(scanned, n + 1)
                if n == 0:
                    dve.wait_ge(consts_in, 48)
                for h in range(2):
                    half = slice(h * S // 2, (h + 1) * S // 2)
                    nc.vector.tensor_tensor(c32[:, r, half], c32[:, r, half], inv_counts[:, half],
                                            ALU.mult).then_inc(meaned, 1)

            def mean_lo(n):
                for h in range(2):
                    half = slice(h * S // 2, (h + 1) * S // 2)
                    dve.wait_ge(meaned, 2 * n + h + 1)
                    dve.wait_ge(c_hi_done, 2 * n + h + 1)
                    nc.vector.tensor_tensor(c_lo[:, n % 2, half], c32[:, n % 2, half], c_hi[:, n % 2, half],
                                            ALU.subtract).then_inc(c_lo_done, 1)

            def scores_of(b):
                return psA[b][:, 0:TPB * H0].rearrange("p (t h) -> p t h", h=H0)

            def largest(b):
                dve.wait_ge(att_mm, KD * (b + 1))
                if b >= 1:
                    dve.wait_ge(mx_all, b)
                nc.vector.tensor_reduce(mx[:], scores_of(b).rearrange("p t h -> p h t"), AX.X, ALU.max).then_inc(mx_done, 1)

            def exponents(b):
                step = 1 + 4 * b
                dve.wait_ge(mx_all, b + 1)
                if b >= 1:
                    dve.wait_ge(gate_done, b)
                nc.vector.tensor_tensor(att[:], scores_of(b), mxa[:].unsqueeze(1).to_broadcast([P, TPB, H0]),
                                        ALU.subtract).then_inc(att_step, 1)
                dve.wait_ge(att_step, step + 1)
                dve.wait_ge(temp_scaled, 1)
                nc.vector.tensor_tensor(att[:], att[:], temp[:].unsqueeze(1).to_broadcast([P, TPB, H0]),
                                        ALU.mult).then_inc(att_arg, 1)

            def gates(b):
                step = 1 + 4 * b
                dve.wait_ge(att_exp, b + 1)
                nc.vector.tensor_tensor(atc[:], att[:], counts[:].unsqueeze(2).to_broadcast([P, TPB, H0]),
                                        ALU.mult).then_inc(att_step, 1)
                dve.wait_ge(att_step, step + 2)
                nc.vector.tensor_scalar_add(att[:], atc[:], EPS_ATT).then_inc(att_step, 1)
                dve.wait_ge(att_step, step + 3)
                nc.vector.reciprocal(att[:], att[:]).then_inc(att_step, 1)
                dve.wait_ge(att_step, step + 4)
                nc.vector.tensor_tensor(gate[:, b], atc[:], att[:], ALU.mult).then_inc(gate_done, 1)

            def piece_lo(n):
                dve.wait_ge(w_hi_done, n + 1)
                nc.vector.scalar_tensor_tensor(pieces[n][2], staged(n), WS, pieces[n][1],
                                               ALU.mult, ALU.subtract).then_inc(w_lo_done, 1)

            for n in range(NU):
                mean(n)
                if n >= 1:
                    mean_lo(n - 1)
                if n >= 2:
                    dve.wait_ge(ada_mm, n - 1)
                    if n >= 4:
                        dve.wait_ge(ada_stored, 16 * (n - 3))
                    nc.vector.tensor_tensor(ada[:, n % 2], psD[0:B, :], b_ada[:, n % 2], ALU.add).then_inc(ada_done, 1)
                if n == KD:
                    largest(0)
                if n == KD + 1:
                    exponents(0)
                if n == KD + 2:
                    gates(0)
            largest(1)
            mean_lo(NU - 1)
            exponents(1)
            gates(1)
            piece_lo(0)
            piece_lo(1)
            for i in range(2):
                dve.wait_ge(x_stored[i], 32 * NU // 2)
            for j in range(KH):
                dve.wait_ge(of_hi_done, j + 1)
                nc.vector.scalar_tensor_tensor(w["of_lo"][:, j], psW[j % 2][:], WS, w["of_hi"][:, j],
                                               ALU.mult, ALU.subtract).then_inc(of_lo_done, 1)
                dve.wait_ge(gT_hi_done, j + 1)
                cols = slice(j % NQ * CH, (j % NQ + 1) * CH)
                nc.vector.tensor_tensor(gT_lo[:, j // NQ, cols], psG[0:H0, :], gT_hi[:, j // NQ, cols],
                                        ALU.subtract).then_inc(gT_lo_done, 1)
                if j % 2 == 0:
                    piece_lo(2 + j // 2)
            for n in range(2 + KH // 2, len(pieces)):
                piece_lo(n)
            dve.wait_ge(b1_mm, 1)
            dve.wait_ge(small_in, 48)
            for b in range(B):
                nc.vector.tensor_tensor(w["b1"][:, :, b * CPB:(b + 1) * CPB],
                                        psD[:, b:KD * B:B].unsqueeze(2).to_broadcast([P, KD, CPB]),
                                        ff1_bias[:].unsqueeze(2).to_broadcast([P, KD, CPB]), ALU.add).then_inc(b1_done, 1)

        @block.tensor
        def _(pe):
            pe.wait_ge(ident_in, 16)

            def turn(n):
                if n > 0:
                    pe.wait_ge(x_in[n % 2], 16 * ((n + 1) // 2))
                for q in range(NQ):
                    if n == 0:
                        pe.wait_ge(first_x_in[q], 16)
                    if n > 0 or q >= 2:
                        pe.wait_ge(xT_written, 2 * (n * NQ + q - 1))
                    for k in range(QT):
                        last = nc.tensor.transpose(psT[q % 2][:, k * P:(k + 1) * P], x_tok[:, n % 2, q * QT + k, :], ident[:])
                    last.then_inc(x_turned, 1)

            def scores(n):
                b, p = n // KD, n % KD
                pe.wait_ge(xT_written, (n + 1) * 2 * NQ)
                pe.wait_ge(x_lo_done, n + 1)
                if n == 0:
                    pe.wait_ge(aw_split, 2)
                for t in range(TPB):
                    out = psA[b][:, t * H0:(t + 1) * H0]
                    cols = slice(t * P, (t + 1) * P)
                    for i, (l, rr) in enumerate(((x_hi, aw_hi), (x_hi, aw_lo), (x_lo, aw_hi))):
                        last = nc.tensor.matmul(out, l[:, n % 2, cols], rr[:, p, :], start=(p == 0 and t == 0 and i == 0),
                                                stop=(p == KD - 1 and i == 2), skip_group_check=True)
                last.then_inc(att_mm, 1)

            def modulation(n):
                if n == 0:
                    pe.wait_ge(small_in, 48)
                pe.wait_ge(ada_in[n % 2], 32 * (n // 2 + 1))
                if n >= 1:
                    pe.wait_ge(ada_done, n)
                for k in range(KD):
                    last = nc.tensor.matmul(psD[0:B, :], condT[:, k, :], staged(n)[:, k, :], start=(k == 0), stop=(k == KD - 1))
                last.then_inc(ada_mm, 1)

            for n in range(NU):
                turn(n)
                if n >= 1:
                    scores(n - 1)
                if n >= 2:
                    modulation(n - 2)
            scores(NU - 1)
            pe.wait_ge(ada_done, NA)
            pe.wait_ge(ff1b_in, 16)
            for o in range(KD):
                for k in range(KD):
                    last = nc.tensor.matmul(psD[:, o * B:(o + 1) * B], ff1b[:, k, o * P:(o + 1) * P], condT[:, k, :],
                                            start=(o == 0 and k == 0), stop=(k == KD - 1), skip_group_check=True)
            last.then_inc(b1_mm, 1)
            pe.wait_ge(oper_in, 16)
            for i in range(2 * KD):
                k, half = i // 2, i % 2
                if i < 2:
                    pe.wait_ge(xT_written, 2 * NU * NQ)
                else:
                    pe.wait_ge(operT_written, i - 1)
                for j in range(4):
                    last = nc.tensor.transpose(psT[i % 2][:, j * P:(j + 1) * P], oper[:, half * 4 + j, k * P:(k + 1) * P], ident[:])
                last.then_inc(oper_turned, 1)
            pe.wait_ge(operT_written, 2 * KD)
            for j in range(KH):
                if j >= 2:
                    pe.wait_ge(of_lo_done, j - 1)
                for k in range(KD):
                    last = nc.tensor.matmul(psW[j % 2][:], operT[:, k, j * P:(j + 1) * P], ff1b[:, k, :],
                                            start=(k == 0), stop=(k == KD - 1))
                last.then_inc(of_mm, 1)
                pe.wait_ge(gate_done, j // NQ + 1)
                if j > 0:
                    pe.wait_ge(gT_lo_done, j)
                for k in range(QT):
                    last = nc.tensor.transpose(psG[0:H0, k * P:(k + 1) * P], gate[:, j // NQ, j % NQ * QT + k, :], ident[:])
                last.then_inc(g_turned, 1)


def split_product(pe, out, terms):
    last = None
    for i, (l_hi, l_lo, r_hi, r_lo) in enumerate(terms):
        for j, (l, r) in enumerate(((l_hi, r_hi), (l_hi, r_lo), (l_lo, r_hi))):
            last = pe.matmul(out, l, r, start=(i == 0 and j == 0), stop=(i == len(terms) - 1 and j == 2))
    return last


COLUMN_LOADS = 4 * B + 5


def load_columns(sp, a, s, w, columns_in):
    def column(dst, src):
        sp.dma_start(dst, src.rearrange("(k p) -> p k", p=P), allow_slow_non_contiguous=True).then_inc(columns_in, 16)

    for b in range(B):
        for name, first in (("mod1", 0), ("mod2", 3)):
            for i in range(2):
                column(w[name][:, i, :, b], s["ada"][b, (first + i) * D:(first + i + 1) * D])
    column(w["bqk"][:, 0], a["L1_cond_bq"])
    column(w["bqk"][:, 1], a["L1_cond_bk"])
    column(w["bv"][:], a["L1_cond_bv"])
    column(w["b1_ff"][:], a["L1_cond_b1"])
    sp.dma_start(w["krows"][:], a["c_krows"]).then_inc(columns_in, 16)


def phase_layer0(nc, a, s, w):
    with ExitStack() as stack:
        m = Memory(nc, stack)
        c_hi = m.sb("l_c_hi", [P, 2, KD, CH], F16)
        c_lo = m.sb("l_c_lo", [P, 2, KD, CH], F16)
        x_hi = m.sb("l_x_hi", [P, 2, KD, CH], F16)
        x_lo = m.sb("l_x_lo", [P, 2, KD, CH], F16)
        g = m.sb("l_g", [P, 2, CH], F16)
        y = m.sb("l_y", [P, 2, TPC, D])
        gB = m.sb("l_gB", [P, 2, CH])
        a32 = m.sb("l_a32", [P, 2, CH])
        a_hi = m.sb("l_a_hi", [P, KH, CH], F16)
        a_lo = m.sb("l_a_lo", [P, KH, CH], F16)
        h32 = m.sb("l_h32", [P, 2, CH])
        h_hi = m.sb("l_h_hi", [P, KD, CH], F16)
        h_lo = m.sb("l_h_lo", [P, KD, CH], F16)
        b2 = m.sb("l_b2", [P, D])
        gamma = m.sb("l_gamma", [P, D])
        beta = m.sb("l_beta", [P, D])
        stats = m.sb("l_stats", [P, TPC, 6])
        mv = m.sb("l_mv", [P, TPC, 2])
        mean_diff = m.sb("l_mean_diff", [P, TPC])
        std = m.sb("l_std", [P, TPC])
        rstd = m.sb("l_rstd", [P, TPC])
        nmr = m.sb("l_nmr", [P, TPC])
        eps = m.sb("l_eps", [P, 1])
        sel = w["sel"]
        psV = [m.ps(f"l_psV{i}") for i in range(2)]
        psG = [m.ps(f"l_psG{i}") for i in range(2)]
        psF = [m.ps(f"l_psF{i}") for i in range(2)]
        psR = [m.ps(f"l_psR{i}") for i in range(2)]

        rows_in = m.sem("l_rows_in")
        columns_in = m.sem("l_columns_in")
        mats_in = [m.sem(f"l_mats_in{i}") for i in range(2)]
        x_in = [m.sem(f"l_x_in{i}") for i in range(2)]
        x1_out = [m.sem(f"l_x1_out{i}") for i in range(2)]
        init = m.sem("l_init")
        v_mm = m.sem("l_v_mm")
        gB_done = m.sem("l_gB_done")
        a32_done = m.sem("l_a32_done")
        a_hi_done = m.sem("l_a_hi_done")
        a_lo_done = m.sem("l_a_lo_done")
        f1_mm = m.sem("l_f1_mm")
        h32_done = m.sem("l_h32_done")
        h_hi_done = m.sem("l_h_hi_done")
        h_lo_done = m.sem("l_h_lo_done")
        f2_mm = m.sem("l_f2_mm")
        bias_added = m.sem("l_bias_added")
        res_done = m.sem("l_res_done")
        stats_done = m.sem("l_stats_done")
        mv_done = m.sem("l_mv_done")
        std_done = m.sem("l_std_done")
        rstd_done = m.sem("l_rstd_done")
        nmr_done = m.sem("l_nmr_done")
        norm_done = m.sem("l_norm_done")
        gamma_done = m.sem("l_gamma_done")
        beta_done = m.sem("l_beta_done")

        x_v = a["x"].rearrange("b (c t p) d -> (b c) p t d", p=P, t=TPC)

        block = stack.enter_context(nc.Block())

        @block.sync
        def _(sp):
            def load_mats(c, r):
                for t, name in ((c_hi, "c_hi"), (c_lo, "c_lo"), (x_hi, "x_hi"), (x_lo, "x_lo")):
                    sp.dma_start(t[:, r], s[name][c]).then_inc(mats_in[r], 16)
                sp.dma_start(g[0:2 * H0, r, :], s["g"][c]).then_inc(mats_in[r], 16)

            def load_x(c, r):
                sp.dma_start(y[:, r], x_v[c]).then_inc(x_in[r], 16)

            def store(c, r):
                sp.wait_ge(beta_done, TPC * c + TPC)
                sp.dma_start(s["x1"][c], y[:, r]).then_inc(x1_out[r], 16)

            sp.wait_ge(init, 1)
            for r in range(2):
                load_mats(r, r)
            for r in range(2):
                load_x(r, r)
            for t, name in ((b2, "L0_cond_ff2_bias"), (gamma, "L0_cond_ln_gamma"), (beta, "L0_cond_ln_beta")):
                src = a[name] if name != "L0_cond_ff2_bias" else a[name].rearrange("a b n -> (a b n)")
                sp.dma_start(t[:], bcast_rows(src)).then_inc(rows_in, 16)
            load_columns(sp, a, s, w, columns_in)
            with sp.Fori(0, NCH // 2 - 1) as i:
                for r in range(2):
                    c = 2 * i + r
                    sp.wait_ge(f1_mm, KD * c + KD)
                    load_mats(c + 2, r)
                    store(c, r)
                    sp.wait_ge(x1_out[r], 16 * i + 16)
                    load_x(2 * (i + 1) + r, r)
            for r in range(2):
                store(NCH - 2 + r, r)
            for r in range(2):
                sp.wait_ge(x1_out[r], 16 * NCH // 2)
            sp.wait_ge(columns_in, 16 * COLUMN_LOADS)

        @block.gpsimd
        def _(pool):
            pool.wait_ge(rows_in, 48)

            def add_bias(r, i):
                pool.wait_ge(x_in[r], 16 * i + 16)
                nc.gpsimd.tensor_tensor(y[:, r], y[:, r], b2[:].unsqueeze(1).to_broadcast([P, TPC, D]),
                                        ALU.add).then_inc(bias_added, 1)

            def add_beta(c, r):
                for t in range(TPC):
                    pool.wait_ge(gamma_done, TPC * c + t + 1)
                    nc.gpsimd.tensor_tensor(y[:, r, t], y[:, r, t], beta[:], ALU.add).then_inc(beta_done, 1)

            add_bias(0, 0)
            add_bias(1, 0)
            with pool.Fori(0, NCH // 2 - 1) as i:
                for r in range(2):
                    add_beta(2 * i + r, r)
                    add_bias(r, i + 1)
            for r in range(2):
                add_beta(NCH - 2 + r, r)

        @block.scalar
        def _(act):
            def gates(c, j):
                act.wait_ge(v_mm, KH * c + j + 1)
                if not (isinstance(c, int) and c == 0 and j < 2):
                    act.wait_ge(a32_done, KH * c + j - 1)
                nc.scalar.activation(gB[:, j % 2], psG[j % 2][:], ACT.Copy, scale=1.0 / WS).then_inc(gB_done, 1)

            def values(c):
                for j in range(2):
                    gates(c, j)
                for j in range(KH):
                    act.wait_ge(a32_done, KH * c + j + 1)
                    nc.scalar.copy(a_hi[:, j], a32[:, j % 2]).then_inc(a_hi_done, 1)
                    if j + 2 < KH:
                        gates(c, j + 2)

            def hidden(c):
                for o in range(KD):
                    act.wait_ge(f1_mm, KD * c + o + 1)
                    if not (isinstance(c, int) and c == 0 and o < 2):
                        act.wait_ge(h_lo_done, KD * c + o - 1)
                    bias = w["b1"][:, o, bass.ds(c, 1)]
                    nc.scalar.activation(h32[:, o % 2], psF[o % 2][:], ACT.Relu, bias=bias, scale=1.0 / WS).then_inc(h32_done, 1)
                    nc.scalar.activation(h_hi[:, o], psF[o % 2][:], ACT.Relu, bias=bias, scale=1.0 / WS).then_inc(h_hi_done, 1)

            def norm(c, r):
                act.wait_ge(mv_done, TPC * c + TPC)
                nc.scalar.activation(std[:], mv[:, :, 1], ACT.Sqrt, bias=eps[:], scale=1.0 / D).then_inc(std_done, 1)
                act.wait_ge(nmr_done, c + 1)
                for t in range(TPC):
                    nc.scalar.activation(y[:, r, t], y[:, r, t], ACT.Identity, bias=nmr[:, t:t + 1],
                                         scale=rstd[:, t:t + 1]).then_inc(norm_done, 1)

            act.wait_ge(init, 2)
            values(0)
            hidden(0)
            with act.Fori(0, NCH // 2 - 1) as i:
                for u in range(2):
                    c = 2 * i + 1 + u
                    values(c)
                    norm(c - 1, u)
                    hidden(c)
            values(NCH - 1)
            norm(NCH - 2, 0)
            hidden(NCH - 1)
            norm(NCH - 1, 1)

        @block.vector
        def _(dve):
            nc.vector.memset(g[:], 0.0).then_inc(init, 1)
            nc.vector.memset(eps[:], EPS_LN0).then_inc(init, 1)

            def values(c):
                for j in range(KH):
                    dve.wait_ge(gB_done, KH * c + j + 1)
                    if not (isinstance(c, int) and c == 0 and j < 2):
                        dve.wait_ge(a_hi_done, KH * c + j - 1)
                        dve.wait_ge(a_lo_done, KH * c + j - 1)
                    nc.vector.tensor_tensor(a32[:, j % 2], psV[j % 2][:], gB[:, j % 2], ALU.mult).then_inc(a32_done, 1)
                    if j >= 1:
                        low(c, j - 1)
                low(c, KH - 1)

            def low(c, j):
                dve.wait_ge(a_hi_done, KH * c + j + 1)
                dve.wait_ge(a32_done, KH * c + j + 1)
                nc.vector.tensor_tensor(a_lo[:, j], a32[:, j % 2], a_hi[:, j], ALU.subtract).then_inc(a_lo_done, 1)

            def hidden(c):
                for o in range(KD):
                    dve.wait_ge(h_hi_done, KD * c + o + 1)
                    dve.wait_ge(h32_done, KD * c + o + 1)
                    nc.vector.tensor_tensor(h_lo[:, o], h32[:, o % 2], h_hi[:, o], ALU.subtract).then_inc(h_lo_done, 1)

            def norm(c, r):
                dve.wait_ge(bias_added, c + 1)
                for t in range(TPC):
                    dve.wait_ge(f2_mm, TPC * c + t + 1)
                    nc.vector.scalar_tensor_tensor(y[:, r, t], psR[t % 2][:], 1.0 / WS, y[:, r, t],
                                                   ALU.mult, ALU.add).then_inc(res_done, 1)
                    dve.wait_ge(res_done, TPC * c + t + 1)
                    nc.vector.bn_stats(stats[:, t], y[:, r, t]).then_inc(stats_done, 1)
                combine_moments(nc, dve, stats, mv, mean_diff, stats_done, TPC * c, mv_done, TPC * c)
                dve.wait_ge(std_done, c + 1)
                nc.vector.reciprocal(rstd[:], std[:]).then_inc(rstd_done, 1)
                dve.wait_ge(rstd_done, c + 1)
                dve.wait_ge(mv_done, TPC * c + TPC)
                nc.vector.scalar_tensor_tensor(nmr[:], mv[:, :, 0], -0.5, rstd[:], ALU.mult, ALU.mult).then_inc(nmr_done, 1)
                for t in range(TPC):
                    dve.wait_ge(norm_done, TPC * c + t + 1)
                    nc.vector.tensor_tensor(y[:, r, t], y[:, r, t], gamma[:], ALU.mult).then_inc(gamma_done, 1)

            dve.wait_ge(rows_in, 48)
            values(0)
            hidden(0)
            with dve.Fori(0, NCH // 2 - 1) as i:
                for u in range(2):
                    c = 2 * i + 1 + u
                    values(c)
                    norm(c - 1, u)
                    hidden(c)
            values(NCH - 1)
            norm(NCH - 2, 0)
            hidden(NCH - 1)
            norm(NCH - 1, 1)

        @block.tensor
        def _(pe):
            def values(c, r, i):
                pe.wait_ge(mats_in[r], 80 * i + 80)
                for j in range(KH):
                    if not (isinstance(c, int) and c == 0 and j < 2):
                        pe.wait_ge(gB_done, KH * c + j - 1)
                        pe.wait_ge(a32_done, KH * c + j - 1)
                    cols = slice(j * P, (j + 1) * P)
                    pe.matmul(psG[j % 2][:], sel[:, j, :], g[:, r, :], start=True, stop=True)
                    split_product(pe, psV[j % 2][:], [(w["val_hi"][:, k, cols], w["val_lo"][:, k, cols], c_hi[:, r, k, :], c_lo[:, r, k, :])
                                                      for k in range(KD)]).then_inc(v_mm, 1)

            def hidden(c, r):
                for o in range(KD):
                    cols = slice(o * P, (o + 1) * P)
                    if not (isinstance(c, int) and c == 0 and o < 2):
                        pe.wait_ge(h_hi_done, KD * c + o - 1)
                    if o == 0:
                        pe.wait_ge(a_hi_done, KH * c + KH)
                        pe.wait_ge(a_lo_done, KH * c + KH)
                    terms = [(w["f1_hi"][:, k, cols], w["f1_lo"][:, k, cols], x_hi[:, r, k, :], x_lo[:, r, k, :]) for k in range(KD)]
                    terms += [(w["of_hi"][:, k, cols], w["of_lo"][:, k, cols], a_hi[:, k, :], a_lo[:, k, :]) for k in range(KH)]
                    split_product(pe, psF[o % 2][:], terms).then_inc(f1_mm, 1)

            def output(c):
                pe.wait_ge(h_lo_done, KD * c + KD)
                for t in range(TPC):
                    if t >= 2:
                        pe.wait_ge(res_done, TPC * c + t - 1)
                    cols = slice(t * P, (t + 1) * P)
                    split_product(pe, psR[t % 2][:], [(h_hi[:, k, cols], h_lo[:, k, cols], w["f2_hi"][:, k, :], w["f2_lo"][:, k, :])
                                                      for k in range(KD)]).then_inc(f2_mm, 1)

            values(0, 0, 0)
            hidden(0, 0)
            with pe.Fori(0, NCH // 2 - 1) as i:
                for u in range(2):
                    c = 2 * i + 1 + u
                    values(c, (1 + u) % 2, i + u)
                    output(c - 1)
                    hidden(c, (1 + u) % 2)
            values(NCH - 1, 1, NCH // 2 - 1)
            output(NCH - 2)
            hidden(NCH - 1, 1)
            output(NCH - 1)


def phase_qkv(nc, a, s, w):
    with ExitStack() as stack:
        m = Memory(nc, stack)
        ident = w["ident"]
        x = m.sb("q_x", [P, 2, TPC, D])
        hT32 = m.sb("q_hT32", [P, 2, CH])
        h_hi = m.sb("q_h_hi", [P, 2, KD, CH], F16)
        h_lo = m.sb("q_h_lo", [P, 2, KD, CH], F16)
        p32 = m.sb("q_p32", [P, 2, CH])
        qk_hi = m.sb("q_qk_hi", [P, 2, 2, KD, CH], F16)
        qk_lo = m.sb("q_qk_lo", [P, 2, 2, KD, CH], F16)
        v = m.sb("q_v", [P, 2, TPC, D])
        bqk = w["bqk"]
        mod = w["mod1"]
        mod_c = m.sb("q_mod_c", [P, 2, KD, NCH])
        stats = m.sb("q_stats", [P, TPC, 6])
        mv = m.sb("q_mv", [P, TPC, 2])
        mean_diff = m.sb("q_mean_diff", [P, TPC])
        std = m.sb("q_std", [P, TPC])
        rstd = m.sb("q_rstd", [P, TPC])
        nmr = m.sb("q_nmr", [P, TPC])
        eps = m.sb("q_eps", [P, 1])
        psT = [m.ps(f"q_psT{i}") for i in range(2)]
        psQ = [m.ps(f"q_psQ{i}") for i in range(4)]
        NT = 3 * KD

        mod_done = m.sem("q_mod_done")
        x_in = [m.sem(f"q_x_in{i}") for i in range(2)]
        stats_done = m.sem("q_stats_done")
        mv_done = m.sem("q_mv_done")
        std_done = m.sem("q_std_done")
        rstd_done = m.sem("q_rstd_done")
        nmr_done = m.sem("q_nmr_done")
        norm_done = m.sem("q_norm_done")
        turned = m.sem("q_turned")
        h32_done = m.sem("q_h32_done")
        h_hi_done = m.sem("q_h_hi_done")
        h_lo_done = m.sem("q_h_lo_done")
        proj_mm = m.sem("q_proj_mm")
        p32_done = m.sem("q_p32_done")
        p_hi_done = m.sem("q_p_hi_done")
        p_lo_done = m.sem("q_p_lo_done")
        v_done = m.sem("q_v_done")
        stored = [m.sem(f"q_stored{i}") for i in range(2)]

        stage = m.sb("q_stage", [P, 2, KD, CH])
        stage_in = [m.sem(f"q_stage_in{i}") for i in range(2)]
        w64_done = m.sem("q_w64_done")
        w_hi_done = m.sem("q_w_hi_done")
        w_lo_done = m.sem("q_w_lo_done")
        pieces = [(a["L1_cond_Wo"].rearrange("(k p) n -> p k n", p=P), w["wo_hi"][:], w["wo_lo"][:])]
        for j in range(FF // CH):
            cols = slice(j * CH, (j + 1) * CH)
            pieces.append((a["L1_cond_W1"].rearrange("(k p) n -> p k n", p=P)[:, :, cols], w["w1_hi"][:, :, cols], w["w1_lo"][:, :, cols]))
        for j in range(FF // CH):
            rows = slice(j * KD, (j + 1) * KD)
            pieces.append((a["L1_cond_W2"].rearrange("(k p) n -> p k n", p=P)[:, rows, :], w["w2_hi"][:, rows, :], w["w2_lo"][:, rows, :]))

        block = stack.enter_context(nc.Block())

        @block.gpsimd
        def _(pool):
            for n in range(2):
                pool.dma_start(stage[:, n], pieces[n][0]).then_inc(stage_in[n], 16)
            for n, (_, hi, lo) in enumerate(pieces):
                pool.wait_ge(stage_in[n % 2], 16 * (n // 2 + 1))
                nc.gpsimd.tensor_scalar(stage[:, n % 2], stage[:, n % 2], WS, None, ALU.mult).then_inc(w64_done, 1)
                pool.wait_ge(w64_done, n + 1)
                nc.gpsimd.tensor_copy(hi, stage[:, n % 2]).then_inc(w_hi_done, 1)
                pool.wait_ge(w_hi_done, n + 1)
                nc.gpsimd.tensor_tensor(lo, stage[:, n % 2], hi, ALU.subtract).then_inc(w_lo_done, 1)
                if n + 2 < len(pieces):
                    pool.wait_ge(w_lo_done, n + 1)
                    pool.dma_start(stage[:, n % 2], pieces[n + 2][0]).then_inc(stage_in[n % 2], 16)

        @block.sync
        def _(sp):
            def load(c, r):
                sp.dma_start(x[:, r], s["x1"][c]).then_inc(x_in[r], 16)

            def store(i, r):
                c = 2 * i + r
                sp.wait_ge(p_hi_done, 2 * KD * c + 2 * KD)
                sp.wait_ge(p_lo_done, 2 * KD * c + 2 * KD)
                for j, name in enumerate("qk"):
                    for half, t in enumerate((qk_hi, qk_lo)):
                        sp.dma_start(s[name].rearrange("h (g c) p t -> h c p g t", g=KD)[half, c], t[:, r, j]).then_inc(stored[r], 16)
                sp.wait_ge(v_done, TPC * c + TPC)
                c = 2 * (i + 1) + r - 2
                for g in range(KD):
                    sp.dma_start(s["v"].rearrange("(g c) p t d -> g c p t d", g=KD)[g, c],
                                 v[:, r, :, g * P:(g + 1) * P]).then_inc(stored[r], 16)

            load(0, 0)
            load(1, 1)

            def step(c, i, r, former=None, load_next=True):
                sp.wait_ge(turned, KD * c + KD)
                if former is not None:
                    sp.wait_ge(stored[1 - r], 128 * former)
                if load_next:
                    load(2 * (i + 1) + r, r)
                store(i, r)

            step(0, 0, 0)
            with sp.Fori(0, NCH // 2 - 2) as i:
                step(2 * i + 1, i, 1, i + 1)
                step(2 * i + 2, i + 1, 0, i + 1)
            i = NCH // 2 - 2
            step(2 * i + 1, i, 1, i + 1)
            for r in range(2):
                step(NCH - 2 + r, NCH // 2 - 1, r, load_next=False)
            for r in range(2):
                sp.wait_ge(stored[r], 128 * (NCH // 2))

        @block.scalar
        def _(act):
            def norm(c, r):
                act.wait_ge(mv_done, TPC * c + TPC)
                if not (isinstance(c, int) and c == 0):
                    act.wait_ge(rstd_done, c)
                nc.scalar.activation(std[:], mv[:, :, 1], ACT.Sqrt, bias=eps[:], scale=1.0 / D).then_inc(std_done, 1)
                act.wait_ge(nmr_done, c + 1)
                for t in range(TPC):
                    nc.scalar.activation(x[:, r, t], x[:, r, t], ACT.Identity, bias=nmr[:, t:t + 1],
                                         scale=rstd[:, t:t + 1]).then_inc(norm_done, 1)

            def modulate(c, r, tiles):
                for k in tiles:
                    act.wait_ge(turned, KD * c + k + 1)
                    if not (isinstance(c, int) and c == 0 and k < 2):
                        act.wait_ge(h_lo_done, KD * c + k - 1)
                    shift, scale = mod_c[:, 0, k, bass.ds(c, 1)], mod_c[:, 1, k, bass.ds(c, 1)]
                    nc.scalar.activation(hT32[:, k % 2], psT[k % 2][:], ACT.Identity, bias=shift, scale=scale).then_inc(h32_done, 1)
                    nc.scalar.activation(h_hi[:, r, k], psT[k % 2][:], ACT.Identity, bias=shift, scale=scale).then_inc(h_hi_done, 1)

            def queries_keys(c, r):
                for j in range(2 * KD):
                    act.wait_ge(proj_mm, NT * c + j + 1)
                    if not (isinstance(c, int) and c == 0 and j < 2):
                        act.wait_ge(p_lo_done, 2 * KD * c + j - 1)
                    which, o = j // KD, j % KD
                    bias = bqk[:, which, o:o + 1]
                    nc.scalar.activation(p32[:, j % 2], psQ[j % 4][:], ACT.Identity, bias=bias, scale=1.0 / WS).then_inc(p32_done, 1)
                    nc.scalar.activation(qk_hi[:, r, which, o], psQ[j % 4][:], ACT.Identity, bias=bias, scale=1.0 / WS).then_inc(p_hi_done, 1)

            def values(c, r, tiles):
                for t in tiles:
                    act.wait_ge(proj_mm, NT * c + 2 * KD + t + 1)
                    nc.scalar.activation(v[:, r, t], psQ[(2 * KD + t) % 4][:], ACT.Copy, scale=1.0 / WS).then_inc(v_done, 1)

            norm(0, 0)
            act.wait_ge(mod_done, 3)
            modulate(0, 0, range(KD))
            norm(1, 1)
            queries_keys(0, 0)
            for tiles in HALVES:
                modulate(1, 1, tiles)
                values(0, 0, tiles)
            with act.Fori(0, NCH // 2 - 1) as i:
                for u in range(2):
                    c, r = 2 * i + 1 + u, (1 + u) % 2
                    norm(c + 1, 1 - r)
                    queries_keys(c, r)
                    for tiles in HALVES:
                        modulate(c + 1, 1 - r, tiles)
                        values(c, r, tiles)
            act.wait_ge(stored[1], 128 * (NCH // 2 - 1))
            queries_keys(NCH - 1, 1)
            values(NCH - 1, 1, range(TPC))

        @block.vector
        def _(dve):
            nc.vector.memset(eps[:], EPS_LN1).then_inc(mod_done, 1)
            dve.wait_ge(mod_done, 1)
            for i, one in enumerate((0.0, 1.0)):
                nc.vector.tensor_scalar_add(mod_c[:, i].rearrange("p k (b c) -> p (k b) c", b=B),
                                            mod[:, i].rearrange("p k b -> p (k b)").unsqueeze(2).to_broadcast([P, KD * B, CPB]),
                                            one).then_inc(mod_done, 1)

            def norm(c, r, i):
                dve.wait_ge(x_in[r], 16 * i + 16)
                for t in range(TPC):
                    nc.vector.bn_stats(stats[:, t], x[:, r, t]).then_inc(stats_done, 1)
                if not (isinstance(c, int) and c == 0):
                    dve.wait_ge(std_done, c)
                combine_moments(nc, dve, stats, mv, mean_diff, stats_done, TPC * c, mv_done, TPC * c)
                dve.wait_ge(std_done, c + 1)
                if not (isinstance(c, int) and c == 0):
                    dve.wait_ge(norm_done, TPC * c)
                nc.vector.reciprocal(rstd[:], std[:]).then_inc(rstd_done, 1)
                dve.wait_ge(rstd_done, c + 1)
                nc.vector.scalar_tensor_tensor(nmr[:], mv[:, :, 0], -0.5, rstd[:], ALU.mult, ALU.mult).then_inc(nmr_done, 1)

            def modulate(c, r):
                for k in range(KD):
                    dve.wait_ge(h32_done, KD * c + k + 1)
                    dve.wait_ge(h_hi_done, KD * c + k + 1)
                    nc.vector.tensor_tensor(h_lo[:, r, k], hT32[:, k % 2], h_hi[:, r, k], ALU.subtract).then_inc(h_lo_done, 1)

            def queries_keys(c, r):
                for j in range(2 * KD):
                    dve.wait_ge(p32_done, 2 * KD * c + j + 1)
                    dve.wait_ge(p_hi_done, 2 * KD * c + j + 1)
                    which, o = j // KD, j % KD
                    nc.vector.tensor_tensor(qk_lo[:, r, which, o], p32[:, j % 2], qk_hi[:, r, which, o],
                                            ALU.subtract).then_inc(p_lo_done, 1)

            norm(0, 0, 0)
            modulate(0, 0)
            norm(1, 1, 0)
            queries_keys(0, 0)
            modulate(1, 1)
            with dve.Fori(0, NCH // 2 - 1) as i:
                for u in range(2):
                    c, r = 2 * i + 1 + u, (1 + u) % 2
                    norm(c + 1, 1 - r, i + 1)
                    queries_keys(c, r)
                    modulate(c + 1, 1 - r)
            queries_keys(NCH - 1, 1)

        @block.tensor
        def _(pe):
            def turn(c, r, tiles):
                for k in tiles:
                    if k == 0:
                        pe.wait_ge(norm_done, TPC * c + TPC)
                    if not (isinstance(c, int) and c == 0 and k < 2):
                        pe.wait_ge(h_hi_done, KD * c + k - 1)
                    for t in range(TPC):
                        last = pe.transpose(psT[k % 2][:, t * P:(t + 1) * P], x[:, r, t, k * P:(k + 1) * P], ident[:])
                    last.then_inc(turned, 1)

            def queries_keys(c, r):
                pe.wait_ge(h_lo_done, KD * c + KD)
                for j in range(2 * KD):
                    name, cols = ("wq", "wk")[j // KD], slice(j % KD * P, (j % KD + 1) * P)
                    if not (isinstance(c, int) and c == 0 and j < 4):
                        if j < 4:
                            pe.wait_ge(v_done, TPC * c - TPC + j + 1)
                        else:
                            pe.wait_ge(p_hi_done, 2 * KD * c + j - 3)
                    split_product(pe, psQ[j % 4][:], [(w[name + "_hi"][:, k, cols], w[name + "_lo"][:, k, cols], h_hi[:, r, k, :], h_lo[:, r, k, :])
                                                      for k in range(KD)]).then_inc(proj_mm, 1)

            def values(c, r, tiles):
                for t in tiles:
                    pe.wait_ge(p_hi_done, 2 * KD * c + KD + t + 1)
                    cols = slice(t * P, (t + 1) * P)
                    split_product(pe, psQ[t % 4][:], [(h_hi[:, r, k, cols], h_lo[:, r, k, cols], w["wv_hi"][:, k, :], w["wv_lo"][:, k, :])
                                                      for k in range(KD)]).then_inc(proj_mm, 1)

            turn(0, 0, range(KD))
            queries_keys(0, 0)
            for tiles in HALVES:
                turn(1, 1, tiles)
                values(0, 0, tiles)
            with pe.Fori(0, NCH // 2 - 1) as i:
                for u in range(2):
                    c, r = 2 * i + 1 + u, (1 + u) % 2
                    queries_keys(c, r)
                    for tiles in HALVES:
                        turn(c + 1, 1 - r, tiles)
                        values(c, r, tiles)
            queries_keys(NCH - 1, 1)
            values(NCH - 1, 1, range(TPC))


def phase_attention(nc, a, s, w):
    with ExitStack() as stack:
        m = Memory(nc, stack)
        NH = P // DH
        NI = KD * NCH
        NG = KD * B
        MU = NH * TPC * CPB
        ADDED = [kt for kt in range(TPB) if kt % 3 != 2]
        ADDS = len(ADDED) - 1
        UNITS, first_unit = [], 0
        for kt in range(TPB):
            here = min(MU - first_unit, 0 if kt == TPB - 1 else 5 if kt == 2 or kt > 0 and (kt - 1) not in ADDED else 4)
            UNITS.append(range(first_unit, first_unit + here))
            first_unit += here
        assert first_unit == MU
        R3 = 3 * DH
        RING = 3
        SCALE = 1.0 / float(np.sqrt(np.float32(DH)))

        ident = w["ident"]
        ident16 = m.sb("a_ident16", [P, P], F16)
        krows = w["krows"]
        ka = w["qkv"][0:R3, 0:NH]
        qa = m.sb("a_qa", [R3, NH, CH], F16)
        kb = m.sb("a_kb", [P, NH, S], F16)
        qb = w["qkv"][:, NH:NH + 2].rearrange("p s (h t) -> p s h t", h=NH)
        vb = m.sb("a_vb", [P, TPB, P])
        ones = m.sb("a_ones", [P, DH])
        probs = m.sb("a_probs", [P, 4, NH, CH])
        parts = m.sb("a_parts", [P, MU])
        m16 = m.sb("a_m16", [P, NH * TPC])
        mcols = m.sb("a_mcols", [P, NH * TPC, DH], F16)
        o32 = m.sb("a_o32", [P, CH])
        z32 = m.sb("a_z32", [P, CH])
        sums = m.sb("a_sums", [P, NH, CH])
        rz = m.sb("a_rz", [P, CH])
        att = m.sb("a_att", [P, CH])
        ob32 = m.sb("a_ob32", [P, CH])
        o_hi = m.sb("a_o_hi", [P, 2, CH], F16)
        o_lo = m.sb("a_o_lo", [P, 2, CH], F16)
        bv = w["bv"]
        psS = [m.ps(f"a_psS{i}") for i in range(RING)]
        psM = [m.ps(f"a_psM{i}") for i in range(RING)]
        psO = m.ps("a_psO")
        psZ = m.ps("a_psZ")

        qa_in = [m.sem(f"a_qa_in{i}") for i in range(2)]
        qb_in = m.sem("a_qb_in")
        ka_in = [m.sem(f"a_ka_in{i}") for i in range(NH)]
        kb_in = [m.sem(f"a_kb_in{i}") for i in range(4)]
        rows_in = m.sem("a_rows_in")
        bias_gated = m.sem("a_bias_gated")
        gates_scaled = m.sem("a_gates_scaled")
        init = m.sem("a_init")
        ident16_done = m.sem("a_ident16_done")
        kb_rows = m.sem("a_kb_rows")
        s_mm = m.sem("a_s_mm")
        m_mm = m.sem("a_m_mm")
        mx_part = m.sem("a_mx_part")
        m16_done = m.sem("a_m16_done")
        mh_done = m.sem("a_mh_done")
        ml_done = m.sem("a_ml_done")
        r_mm = m.sem("a_r_mm")
        rows_done = m.sem("a_rows_done")
        exp_done = m.sem("a_exp_done")
        pv_done = m.sem("a_pv_done")
        added = m.sem("a_added")
        z_mm = m.sem("a_z_mm")
        z_out = m.sem("a_z_out")
        o_out = m.sem("a_o_out")
        rz_done = m.sem("a_rz_done")
        att_done = m.sem("a_att_done")
        ob_done = m.sem("a_ob_done")
        o_hi_done = m.sem("a_o_hi_done")
        o_lo_done = m.sem("a_o_lo_done")
        o_stored = m.sem("a_o_stored")

        HI, LO = 0, 1
        RZ = 2 * TPC
        q_v = s["q"].rearrange("h n (j d) t -> h n d j t", d=DH)
        k_v = s["k"].rearrange("h (g c) (j d) t -> h g j d c t", c=CPB, d=DH)
        v_v = s["v"].rearrange("(g c) p t d -> g c p t d", c=CPB)

        def add_step(eng, ops, n, j):
            kt = ADDED[j + 1]
            eng.wait_ge(exp_done, NH * (TPB * n + kt + 1))
            if j > 0:
                eng.wait_ge(added, ADDS * n + j)
            elif not (isinstance(n, int) and n == 0):
                eng.wait_ge(z_mm, n)
            former = sums[:] if j > 0 else probs[:, ADDED[0] % 4]
            ops.tensor_tensor(sums[:], former, probs[:, kt % 4], ALU.add).then_inc(added, 1)

        block = stack.enter_context(nc.Block())

        @block.sync
        def _(sp):
            def load_qa(n, pair):
                heads = slice(2 * pair, 2 * pair + 2)
                for i, half in enumerate((HI, LO, HI)):
                    sp.dma_start(qa[i * DH:(i + 1) * DH, heads], q_v[half, n][:, heads]).then_inc(qa_in[pair], 16)

            def next_qa(n, pair):
                sp.wait_ge(m_mm, MU * (n + 1) + (pair + 1) * MU // 2)
                load_qa(n + 2, pair)

            def load_qb(n, slot):
                for i, half in enumerate((HI, LO, HI)):
                    sp.dma_start(qb[i * DH:(i + 1) * DH, slot], q_v[half, n]).then_inc(qb_in, 16)

            def load_ka(g, h):
                for i, half in enumerate((HI, HI, LO)):
                    sp.dma_start(ka[i * DH:(i + 1) * DH, h].rearrange("d (c t) -> d c t", c=CPB),
                                 k_v[half, g, h]).then_inc(ka_in[h], 16)

            def load_kb(g, c):
                for i, half in enumerate((HI, HI, LO)):
                    sp.dma_start(kb[i * DH:(i + 1) * DH, :, c * CH:(c + 1) * CH],
                                 k_v[half, g].rearrange("j d c t -> c d j t")[c]).then_inc(kb_in[c], 16)
                sp.dma_start(vb[:, c * TPC:(c + 1) * TPC, :], v_v[g, c]).then_inc(kb_in[c], 16)

            def store_o(n):
                if not (isinstance(n, int) and n == 0):
                    sp.wait_ge(o_stored, 32 * n)
                sp.wait_ge(o_hi_done, n + 1)
                sp.wait_ge(o_lo_done, n + 1)
                slot = n % 2
                for half, t in enumerate((o_hi, o_lo)):
                    src = t[:, slot, :] if isinstance(n, int) else t[:, bass.ds(slot, 1), :].rearrange("p a t -> p (a t)")
                    sp.dma_start(s["o"][half, n], src).then_inc(o_stored, 16)

            def item(n, g, cc, first=False, last_group=False):
                if not (last_group and cc == CPB - 1):
                    if not first:
                        sp.wait_ge(s_mm, NH * TPB * n)
                    sp.wait_ge(qb_in, 48 * n + 48)
                    load_qb(n + 1, (cc + 1) % 2)
                if cc == CPB - 2 and not last_group:
                    for h in range(NH):
                        sp.wait_ge(m_mm, MU * (n + 1) + (h + 1) * MU // NH)
                        load_ka(g + 1, h)
                        if h % 2 == 1:
                            next_qa(n, h // 2)
                        if h == 1:
                            store_o(n - 1)
                elif cc == CPB - 1 and not last_group:
                    for c in range(CPB):
                        sp.wait_ge(pv_done, TPB * n + TPC * (c + 1))
                        load_kb(g + 1, c)
                        if c in (1, 2):
                            next_qa(n, c - 1)
                        if c == 1:
                            store_o(n - 1)
                elif not (last_group and cc >= CPB - 2):
                    next_qa(n, 0)
                    if not first:
                        store_o(n - 1)
                    next_qa(n, 1)
                else:
                    store_o(n - 1)

            for pair in range(2):
                load_qa(0, pair)
            for h in range(NH):
                load_ka(0, h)
            load_qb(0, 0)
            for c in range(CPB):
                load_kb(0, c)
            for b in range(B):
                for i, (part, bias) in enumerate(((2, "L1_cond_bo"), (5, "L1_cond_b2"))):
                    sp.dma_start(w["gates"][:, i, b], bcast_rows(s["ada"][b, part * D:(part + 1) * D])).then_inc(rows_in, 16)
                    sp.dma_start(w["gated_bias"][:, i, b], bcast_rows(a[bias])).then_inc(rows_in, 16)
            for pair in range(2):
                next_qa(-1, pair)
            for cc in range(CPB):
                item(cc, 0, cc, first=cc == 0)
            with sp.Fori(1, NG - 1) as g:
                for cc in range(CPB):
                    item(CPB * g + cc, g, cc)
            for cc in range(CPB):
                item(CPB * (NG - 1) + cc, NG - 1, cc, last_group=True)
            store_o(NI - 1)
            sp.wait_ge(o_stored, 32 * NI)

        @block.gpsimd
        def _(pool):
            def item(n):
                for j in range(ADDS):
                    add_step(pool, nc.gpsimd, n, j)

            pool.wait_ge(rows_in, 16 * 4 * B)
            nc.gpsimd.tensor_tensor(w["gated_bias"][:], w["gated_bias"][:], w["gates"][:], ALU.mult).then_inc(bias_gated, 1)
            pool.wait_ge(bias_gated, 1)
            nc.gpsimd.tensor_scalar(w["gates"][:], w["gates"][:], 1.0 / WS, None, ALU.mult).then_inc(gates_scaled, 1)
            item(0)
            with pool.Fori(1, NI - 1) as n:
                item(n)

        @block.scalar
        def _(act):
            def exps(n, kt):
                for h in range(NH):
                    act.wait_ge(s_mm, NH * (TPB * n + kt) + h + 1)
                    if h == 0 and not (isinstance(n, int) and n == 0 and kt < 4):
                        act.wait_ge(pv_done, TPB * n + kt - 3)
                        act.wait_ge(added, ADDS * n + adds_until(kt - 4))
                    nc.scalar.activation(probs[:, kt % 4, h], psS[(NH * kt + h) % RING][:], ACT.Exp,
                                         scale=SCALE).then_inc(exp_done, 1)

            def adds_until(kt):
                if kt < 0:
                    return adds_until(kt + TPB) - ADDS
                return max(1, sum(1 for s in ADDED[1:] if s <= kt))

            def values_out(n):
                act.wait_ge(pv_done, TPB * n + TPB)
                if not (isinstance(n, int) and n == 0):
                    act.wait_ge(att_done, n)
                nc.scalar.copy(o32[:], psO[:]).then_inc(o_out, 1)

            def sums_out(n):
                act.wait_ge(z_mm, n + 1)
                if not (isinstance(n, int) and n == 0):
                    act.wait_ge(rz_done, RZ * n)
                nc.scalar.copy(z32[:], psZ[:]).then_inc(z_out, 1)

            def result(n, slot):
                act.wait_ge(att_done, n + 1)
                if not (isinstance(n, int) and n < 2):
                    act.wait_ge(o_stored, 32 * (n - 1))
                group = n // NCH
                bias = bv[:, group:group + 1] if isinstance(n, int) else bv[:, bass.ds(group, 1)]
                hi = o_hi[:, slot] if isinstance(n, int) else o_hi[:, bass.ds(slot, 1)].rearrange("p a t -> p (a t)")
                nc.scalar.activation(ob32[:], att[:], ACT.Identity, bias=bias).then_inc(ob_done, 1)
                nc.scalar.activation(hi, att[:], ACT.Identity, bias=bias).then_inc(o_hi_done, 1)

            def rows(n):
                act.wait_ge(r_mm, n + 1)
                slot = n % 2
                for h in range(NH):
                    out = qb[R3:P, slot, h] if isinstance(n, int) else qb[R3:P, bass.ds(slot, 1), h].rearrange("p a t -> p (a t)")
                    nc.scalar.copy(out, psM[RING - 1][h * DH:(h + 1) * DH, :]).then_inc(rows_done, 1)

            def item(n, first=False, last=False):
                for kt in range(TPB):
                    if kt == 0 and not first:
                        values_out(n - 1)
                    exps(n, kt)
                    if kt == 2 and not first:
                        sums_out(n - 1)
                    if kt == 4 + RZ and not first:
                        result(n - 1, (n - 1) % 2)
                    if kt == TPB - 1 and not last:
                        rows(n + 1)

            nc.scalar.copy(ident16[:], ident[:]).then_inc(ident16_done, 1)
            nc.scalar.activation(kb[R3:P].rearrange("p h t -> p (h t)"), ident[R3:P, 0:1].to_broadcast([DH, NH * S]),
                                 ACT.Identity, bias=krows[R3:P, 0:1], scale=0.0).then_inc(kb_rows, 1)
            rows(0)
            item(0, first=True)
            for n in (1, 2):
                item(n)
            with act.Fori(3, NI - 1) as n:
                item(n)
            item(NI - 1, last=True)
            values_out(NI - 1)
            sums_out(NI - 1)
            result(NI - 1, (NI - 1) % 2)

        @block.vector
        def _(dve):
            nc.vector.memset(ones[:], 1.0).then_inc(init, 1)
            nc.vector.memset(mcols[:], 0.0).then_inc(init, 1)

            def maxima(n, units):
                for u in units:
                    dve.wait_ge(m_mm, MU * n + u + 1)
                    if u == 0 and not (isinstance(n, int) and n == 0):
                        dve.wait_ge(m16_done, n)
                    nc.vector.reduce_max(parts[:, u:u + 1], psM[u % RING][:], AX.X).then_inc(mx_part, 1)
                if MU - 1 in units:
                    dve.wait_ge(mx_part, MU * n + MU)
                    if not (isinstance(n, int) and n == 0):
                        dve.wait_ge(ml_done, n)
                        dve.wait_ge(r_mm, n)
                    nc.vector.tensor_reduce(m16[:], parts[:].rearrange("p (u k) -> p u k", k=CPB), AX.X, ALU.max).then_inc(m16_done, 1)
                    dve.wait_ge(m16_done, n + 1)
                    nc.vector.tensor_scalar(mcols[:, :, 0], m16[:], -1.0 / WS, None, ALU.mult).then_inc(mh_done, 1)
                    dve.wait_ge(mh_done, n + 1)
                    nc.vector.scalar_tensor_tensor(mcols[:, :, 1], mcols[:, :, 0], -WS, m16[:],
                                                   ALU.mult, ALU.subtract).then_inc(ml_done, 1)

            def reciprocal(n, part):
                cols = slice(part * CH // RZ, (part + 1) * CH // RZ)
                dve.wait_ge(z_out, n + 1)
                nc.vector.reciprocal(rz[:, cols], z32[:, cols]).then_inc(rz_done, 1)

            def normalise(n):
                dve.wait_ge(rz_done, RZ * n + RZ)
                dve.wait_ge(o_out, n + 1)
                nc.vector.tensor_tensor(att[:], o32[:], rz[:], ALU.mult).then_inc(att_done, 1)
                dve.wait_ge(att_done, n + 1)

            def low(n, slot):
                dve.wait_ge(ob_done, n + 1)
                dve.wait_ge(o_hi_done, n + 1)
                hi, lo = ((t[:, slot] if isinstance(n, int) else t[:, bass.ds(slot, 1)].rearrange("p a t -> p (a t)")) for t in (o_hi, o_lo))
                nc.vector.tensor_tensor(lo, ob32[:], hi, ALU.subtract).then_inc(o_lo_done, 1)

            def item(n, first=False, last=False):
                for kt in range(TPB):
                    if not last:
                        maxima(n + 1, UNITS[kt])
                    if 3 <= kt < 3 + RZ and not first:
                        reciprocal(n - 1, kt - 3)
                    if kt == 3 + RZ and not first:
                        normalise(n - 1)
                    if kt == 5 + RZ and not first:
                        low(n - 1, (n - 1) % 2)
                    if last and kt in ADDED[1:]:
                        add_step(dve, nc.vector, n, ADDED.index(kt) - 1)

            maxima(0, range(MU))
            item(0, first=True)
            with dve.Fori(1, NI - 1) as n:
                item(n)
            item(NI - 1, last=True)
            for part in range(RZ):
                reciprocal(NI - 1, part)
            normalise(NI - 1)
            low(NI - 1, (NI - 1) % 2)

        @block.tensor
        def _(pe):
            def scores(n, kt, h):
                slot, unit = n % 2, NH * kt + h
                if kt == 0 and h == 0:
                    pe.wait_ge(qb_in, 48 * n + 48)
                if kt == 0:
                    pe.wait_ge(rows_done, NH * n + h + 1)
                if kt % TPC == 0 and h == 0:
                    pe.wait_ge(kb_in[kt // TPC], 64 * (n // CPB) + 64)
                if unit >= RING:
                    pe.wait_ge(exp_done, NH * TPB * n + unit - RING + 1)
                elif unit == 0 and not (isinstance(n, int) and n == 0):
                    pe.wait_ge(exp_done, NH * TPB * n)
                q = qb[:, slot, h] if isinstance(n, int) else qb[:, bass.ds(slot, 1), h].rearrange("p a t -> p (a t)")
                pe.matmul(psS[unit % RING][:], kb[:, h, kt * P:(kt + 1) * P], q, start=True, stop=True).then_inc(s_mm, 1)

            def maxima(n, units):
                for u in units:
                    h, qt, k = u // (TPC * CPB), u // CPB % TPC, u % CPB
                    if u % (MU // 2) == 0:
                        pe.wait_ge(qa_in[u // (MU // 2)], 48 * n + 48)
                    if u == RING - 1 and not (isinstance(n, int) and n == 0):
                        pe.wait_ge(rows_done, NH * n)
                    if u % (TPC * CPB) == 0:
                        pe.wait_ge(ka_in[h], 48 * (n // CPB) + 48)
                    if u >= RING:
                        pe.wait_ge(mx_part, MU * n + u - RING + 1)
                    pe.matmul(psM[u % RING][:], qa[:, h, qt * P:(qt + 1) * P], ka[:, h, k * CH:(k + 1) * CH],
                              start=True, stop=True).then_inc(m_mm, 1)

            def rows(n):
                pe.wait_ge(ml_done, n + 1)
                for h in range(NH):
                    for qt in range(TPC):
                        last = pe.matmul(psM[RING - 1][h * DH:(h + 1) * DH, qt * P:(qt + 1) * P], mcols[:, h * TPC + qt, :], ident16[:],
                                         start=True, stop=True)
                last.then_inc(r_mm, 1)

            def values(n, kt):
                pe.wait_ge(exp_done, NH * (TPB * n + kt + 1))
                if kt == 0 and not (isinstance(n, int) and n == 0):
                    pe.wait_ge(o_out, n)
                for h in range(NH):
                    rows_h = slice(h * DH, (h + 1) * DH)
                    last = pe.matmul(psO[rows_h, :], vb[:, kt, rows_h], probs[:, kt % 4, h], start=kt == 0, stop=kt == TPB - 1)
                return last

            def sum_step(n, kt):
                if kt == DIRECT[0] and not (isinstance(n, int) and n == 0):
                    pe.wait_ge(z_out, n)
                for h in range(NH):
                    last = pe.matmul(psZ[h * DH:(h + 1) * DH, :], ones[:], probs[:, kt % 4, h], start=kt == DIRECT[0], stop=False)
                return last

            def sum_added(n):
                pe.wait_ge(added, ADDS * n + ADDS)
                for h in range(NH):
                    last = pe.matmul(psZ[h * DH:(h + 1) * DH, :], ones[:], sums[:, h], start=False, stop=True)
                last.then_inc(z_mm, 1)

            DIRECT = [kt for kt in range(TPB) if kt not in ADDED]

            def products(n, kt, between):
                last = values(n, kt)
                if kt in DIRECT:
                    between(1)
                    last = sum_step(n, kt)
                last.then_inc(pv_done, 1)

            def item(n, first=False, last=False):
                for kt in range(TPB):
                    left = list(UNITS[kt])

                    def between(count):
                        if not last:
                            maxima(n + 1, left[:count])
                            del left[:count]

                    if kt == 0:
                        if not first:
                            products(n - 1, TPB - 1, between)
                        between(1)
                    scores(n, kt, 0)
                    between(1)
                    scores(n, kt, 1)
                    between(1)
                    scores(n, kt, 2)
                    between(1)
                    scores(n, kt, 3)
                    if kt == TPB - 1 and not last:
                        rows(n + 1)
                    if kt == 2 and not first:
                        sum_added(n - 1)
                        between(1)
                    if kt > 0:
                        products(n, kt - 1, between)
                    between(len(left))

            maxima(0, range(MU))
            pe.wait_ge(init, 2)
            pe.wait_ge(ident16_done, 1)
            rows(0)
            pe.wait_ge(kb_rows, 1)
            item(0, first=True)
            with pe.Fori(1, NI - 1) as n:
                item(n)
            item(NI - 1, last=True)
            products(NI - 1, TPB - 1, lambda count: None)
            sum_added(NI - 1)


def phase_feed_forward(nc, a, s, w, out):
    with ExitStack() as stack:
        m = Memory(nc, stack)
        KF = FF // P
        ident = w["ident"]
        x = m.sb("f_x", [P, 2, TPC, D])
        xn = m.sb("f_xn", [P, TPC, D])
        o_hi = m.sb("f_o_hi", [P, 2, KD, CH], F16)
        o_lo = m.sb("f_o_lo", [P, 2, KD, CH], F16)
        hT32 = m.sb("f_hT32", [P, 2, CH])
        h_hi = m.sb("f_h_hi", [P, KD, CH], F16)
        h_lo = m.sb("f_h_lo", [P, KD, CH], F16)
        g32 = m.sb("f_g32", [P, 2, CH])
        g_hi = m.sb("f_g_hi", [P, KF, CH], F16)
        g_lo = m.sb("f_g_lo", [P, KF, CH], F16)
        scaled = m.sb("f_scaled", [P, 2, D])
        gates, gated_bias = w["gates"], w["gated_bias"]
        b1 = w["b1_ff"]
        mod = w["mod2"]
        mod_c = m.sb("f_mod_c", [P, 2, KD, NCH])
        stats = m.sb("f_stats", [P, TPC, 6])
        mv = m.sb("f_mv", [P, TPC, 2])
        mean_diff = m.sb("f_mean_diff", [P, TPC])
        std = m.sb("f_std", [P, TPC])
        rstd = m.sb("f_rstd", [P, TPC])
        nmr = m.sb("f_nmr", [P, TPC])
        eps = m.sb("f_eps", [P, 1])
        psT = [m.ps(f"f_psT{i}") for i in range(2)]
        psW = [m.ps(f"f_psW{i}") for i in range(2)]
        psO = [m.ps(f"f_psO{i}") for i in range(2)]
        psY = [m.ps(f"f_psY{i}") for i in range(2)]

        mod_done = m.sem("f_mod_done")
        x_in = [m.sem(f"f_x_in{i}") for i in range(2)]
        o_in = [m.sem(f"f_o_in{i}") for i in range(2)]
        stored = [m.sem(f"f_stored{i}") for i in range(2)]
        bo_added = m.sem("f_bo_added")
        b2_added = m.sem("f_b2_added")
        wo_mm = m.sem("f_wo_mm")
        scaled_done = m.sem("f_scaled_done")
        x2_done = m.sem("f_x2_done")
        stats_done = m.sem("f_stats_done")
        mv_done = m.sem("f_mv_done")
        std_done = m.sem("f_std_done")
        rstd_done = m.sem("f_rstd_done")
        nmr_done = m.sem("f_nmr_done")
        norm_done = m.sem("f_norm_done")
        turned = m.sem("f_turned")
        h32_done = m.sem("f_h32_done")
        h_hi_done = m.sem("f_h_hi_done")
        h_lo_done = m.sem("f_h_lo_done")
        w1_mm = m.sem("f_w1_mm")
        g32_done = m.sem("f_g32_done")
        g_hi_done = m.sem("f_g_hi_done")
        g_lo_done = m.sem("f_g_lo_done")
        w2_mm = m.sem("f_w2_mm")
        y_scaled = m.sem("f_y_scaled")
        y_done = m.sem("f_y_done")

        out_v = out.rearrange("b (c t p) d -> (b c) p t d", p=P, t=TPC)
        ADA = ("shift1", "scale1", "gate1", "shift2", "scale2", "gate2")

        block = stack.enter_context(nc.Block())

        @block.sync
        def _(sp):
            def load_o(c, r):
                for half, t in enumerate((o_hi, o_lo)):
                    sp.dma_start(t[:, r], s["o"].rearrange("h (g c) p t -> h c p g t", g=KD)[half, c]).then_inc(o_in[r], 16)

            def load_x(c, r):
                sp.dma_start(x[:, r], s["x1"][c]).then_inc(x_in[r], 16)

            def store(c, r):
                sp.wait_ge(y_done, TPC * c + TPC)
                sp.dma_start(out_v[c], x[:, r]).then_inc(stored[r], 16)

            load_o(0, 0)
            load_x(0, 0)
            load_o(1, 1)
            load_x(1, 1)
            with sp.Fori(0, NCH // 2 - 1) as i:
                for r in range(2):
                    c = 2 * i + r
                    sp.wait_ge(wo_mm, TPC * c + TPC)
                    load_o(c + 2, r)
                    store(c, r)
                    sp.wait_ge(stored[r], 16 * i + 16)
                    load_x(c + 2, r)
            for r in range(2):
                store(NCH - 2 + r, r)
            for r in range(2):
                sp.wait_ge(stored[r], 16 * (NCH // 2))

        @block.gpsimd
        def _(pool):
            def batch(t, i, c):
                if isinstance(c, int):
                    return t[:, i, c // CPB:c // CPB + 1].to_broadcast([P, TPC, D])
                return t[:, i, bass.ds(c // CPB, 1)].to_broadcast([P, TPC, D])

            def add_bo(c, r, i):
                pool.wait_ge(x_in[r], 16 * i + 16)
                nc.gpsimd.tensor_tensor(x[:, r], x[:, r], batch(gated_bias, 0, c), ALU.add).then_inc(bo_added, 1)

            def add_b2(c, r):
                pool.wait_ge(norm_done, TPC * c + TPC)
                nc.gpsimd.tensor_tensor(x[:, r], x[:, r], batch(gated_bias, 1, c), ALU.add).then_inc(b2_added, 1)

            add_bo(0, 0, 0)
            add_b2(0, 0)
            add_bo(1, 1, 0)
            add_b2(1, 1)
            with pool.Fori(0, NCH // 2 - 1) as i:
                for r in range(2):
                    add_bo(2 * i + 2 + r, r, i + 1)
                    add_b2(2 * i + 2 + r, r)

        @block.scalar
        def _(act):
            def norm(c, r):
                act.wait_ge(mv_done, TPC * c + TPC)
                if not (isinstance(c, int) and c == 0):
                    act.wait_ge(rstd_done, c)
                    act.wait_ge(turned, KD * c)
                nc.scalar.activation(std[:], mv[:, :, 1], ACT.Sqrt, bias=eps[:], scale=1.0 / D).then_inc(std_done, 1)
                act.wait_ge(nmr_done, c + 1)
                for t in range(TPC):
                    nc.scalar.activation(xn[:, t], x[:, r, t], ACT.Identity, bias=nmr[:, t:t + 1],
                                         scale=rstd[:, t:t + 1]).then_inc(norm_done, 1)

            def modulate(c):
                for k in range(KD):
                    act.wait_ge(turned, KD * c + k + 1)
                    if not (isinstance(c, int) and c == 0 and k < 2):
                        act.wait_ge(h_lo_done, KD * c + k - 1)
                    shift, scale = mod_c[:, 0, k, bass.ds(c, 1)], mod_c[:, 1, k, bass.ds(c, 1)]
                    nc.scalar.activation(hT32[:, k % 2], psT[k % 2][:], ACT.Identity, bias=shift, scale=scale).then_inc(h32_done, 1)
                    nc.scalar.activation(h_hi[:, k], psT[k % 2][:], ACT.Identity, bias=shift, scale=scale).then_inc(h_hi_done, 1)

            def gelus(c):
                for j in range(KF):
                    act.wait_ge(w1_mm, KF * c + j + 1)
                    if not (isinstance(c, int) and c == 0 and j < 2):
                        act.wait_ge(g_lo_done, KF * c + j - 1)
                    nc.scalar.activation(g32[:, j % 2], psW[j % 2][:], ACT.Gelu, bias=b1[:, j:j + 1], scale=1.0 / WS).then_inc(g32_done, 1)
                    nc.scalar.activation(g_hi[:, j], psW[j % 2][:], ACT.Gelu, bias=b1[:, j:j + 1], scale=1.0 / WS).then_inc(g_hi_done, 1)

            norm(0, 0)
            act.wait_ge(mod_done, 3)
            modulate(0)
            gelus(0)
            norm(1, 1)
            modulate(1)
            with act.Fori(0, NCH // 2 - 1) as i:
                for u in range(2):
                    c = 2 * i + 1 + u
                    gelus(c)
                    norm(c + 1, u)
                    modulate(c + 1)
            gelus(NCH - 1)

        @block.vector
        def _(dve):
            def batch(t, i, c):
                if isinstance(c, int):
                    return t[:, i, c // CPB]
                return t[:, i, bass.ds(c // CPB, 1)].rearrange("p a d -> p (a d)")

            def attention_out(c, r):
                dve.wait_ge(bo_added, c + 1)
                for t in range(TPC):
                    dve.wait_ge(wo_mm, TPC * c + t + 1)
                    if not (isinstance(c, int) and c == 0 and t < 2):
                        dve.wait_ge(x2_done, TPC * c + t - 1)
                    if t < 2 and not (isinstance(c, int) and c < 2):
                        dve.wait_ge(y_done, TPC * c - TPC - 1)
                    nc.vector.tensor_tensor(scaled[:, t % 2], psO[t % 2][:], batch(gates, 0, c), ALU.mult).then_inc(scaled_done, 1)
                    dve.wait_ge(scaled_done, TPC * c + t + 1)
                    nc.vector.tensor_tensor(x[:, r, t], x[:, r, t], scaled[:, t % 2], ALU.add).then_inc(x2_done, 1)
                    dve.wait_ge(x2_done, TPC * c + t + 1)
                    nc.vector.bn_stats(stats[:, t], x[:, r, t]).then_inc(stats_done, 1)
                if not (isinstance(c, int) and c == 0):
                    dve.wait_ge(std_done, c)
                combine_moments(nc, dve, stats, mv, mean_diff, stats_done, TPC * c, mv_done, TPC * c)
                dve.wait_ge(std_done, c + 1)
                if not (isinstance(c, int) and c == 0):
                    dve.wait_ge(norm_done, TPC * c)
                nc.vector.reciprocal(rstd[:], std[:]).then_inc(rstd_done, 1)
                dve.wait_ge(rstd_done, c + 1)
                nc.vector.scalar_tensor_tensor(nmr[:], mv[:, :, 0], -0.5, rstd[:], ALU.mult, ALU.mult).then_inc(nmr_done, 1)

            def modulate(c, tiles):
                for k in tiles:
                    dve.wait_ge(h32_done, KD * c + k + 1)
                    dve.wait_ge(h_hi_done, KD * c + k + 1)
                    nc.vector.tensor_tensor(h_lo[:, k], hT32[:, k % 2], h_hi[:, k], ALU.subtract).then_inc(h_lo_done, 1)

            def gelus(c):
                for j in range(KF):
                    dve.wait_ge(g32_done, KF * c + j + 1)
                    dve.wait_ge(g_hi_done, KF * c + j + 1)
                    nc.vector.tensor_tensor(g_lo[:, j], g32[:, j % 2], g_hi[:, j], ALU.subtract).then_inc(g_lo_done, 1)

            def outputs(c, r, tiles):
                dve.wait_ge(b2_added, c + 1)
                for t in tiles:
                    dve.wait_ge(w2_mm, TPC * c + t + 1)
                    if isinstance(c, int) and c == 0 and t < 2:
                        dve.wait_ge(x2_done, TPC)
                    else:
                        dve.wait_ge(y_done, TPC * c + t - 1)
                    nc.vector.tensor_tensor(scaled[:, t % 2], psY[t % 2][:], batch(gates, 1, c), ALU.mult).then_inc(y_scaled, 1)
                    dve.wait_ge(y_scaled, TPC * c + t + 1)
                    nc.vector.tensor_tensor(x[:, r, t], x[:, r, t], scaled[:, t % 2], ALU.add).then_inc(y_done, 1)

            nc.vector.memset(eps[:], EPS_LN1).then_inc(mod_done, 1)
            dve.wait_ge(mod_done, 1)
            for i, one in enumerate((0.0, 1.0)):
                nc.vector.tensor_scalar_add(mod_c[:, i].rearrange("p k (b c) -> p (k b) c", b=B),
                                            mod[:, i].rearrange("p k b -> p (k b)").unsqueeze(2).to_broadcast([P, KD * B, CPB]),
                                            one).then_inc(mod_done, 1)
            attention_out(0, 0)
            modulate(0, range(KD))
            gelus(0)
            attention_out(1, 1)
            outputs(0, 0, range(2))
            modulate(1, HALVES[0])
            outputs(0, 0, range(2, 3))
            modulate(1, HALVES[1])
            outputs(0, 0, range(3, 4))
            with dve.Fori(0, NCH // 2 - 1) as i:
                for u in range(2):
                    c = 2 * i + 1 + u
                    gelus(c)
                    attention_out(c + 1, u)
                    outputs(c, 1 - u, range(2))
                    modulate(c + 1, HALVES[0])
                    outputs(c, 1 - u, range(2, 3))
                    modulate(c + 1, HALVES[1])
                    outputs(c, 1 - u, range(3, 4))
            gelus(NCH - 1)
            outputs(NCH - 1, 1, range(4))

        @block.tensor
        def _(pe):
            def attention_out(c, r, i, tiles=range(TPC)):
                pe.wait_ge(o_in[r], 32 * i + 32)
                for t in tiles:
                    if not (isinstance(c, int) and c == 0 and t < 2):
                        pe.wait_ge(scaled_done, TPC * c + t - 1)
                    cols = slice(t * P, (t + 1) * P)
                    split_product(pe, psO[t % 2][:], [(o_hi[:, r, k, cols], o_lo[:, r, k, cols], w["wo_hi"][:, k, :], w["wo_lo"][:, k, :])
                                                      for k in range(KD)]).then_inc(wo_mm, 1)

            def turn(c, tiles):
                for k in tiles:
                    if k == 0:
                        pe.wait_ge(norm_done, TPC * c + TPC)
                    if not (isinstance(c, int) and c == 0 and k < 2):
                        pe.wait_ge(h_hi_done, KD * c + k - 1)
                    for t in range(TPC):
                        last = pe.transpose(psT[k % 2][:, t * P:(t + 1) * P], xn[:, t, k * P:(k + 1) * P], ident[:])
                    last.then_inc(turned, 1)

            def expand(c):
                pe.wait_ge(h_lo_done, KD * c + KD)
                for j in range(KF):
                    if not (isinstance(c, int) and c == 0 and j < 2):
                        pe.wait_ge(g_hi_done, KF * c + j - 1)
                    cols = slice(j * P, (j + 1) * P)
                    split_product(pe, psW[j % 2][:], [(w["w1_hi"][:, k, cols], w["w1_lo"][:, k, cols], h_hi[:, k, :], h_lo[:, k, :])
                                                      for k in range(KD)]).then_inc(w1_mm, 1)

            def contract(c, tiles):
                for t in tiles:
                    if t == 0:
                        pe.wait_ge(g_lo_done, KF * c + KF)
                    if not (isinstance(c, int) and c == 0 and t < 2):
                        pe.wait_ge(y_scaled, TPC * c + t - 1)
                    cols = slice(t * P, (t + 1) * P)
                    split_product(pe, psY[t % 2][:], [(g_hi[:, k, cols], g_lo[:, k, cols], w["w2_hi"][:, k, :], w["w2_lo"][:, k, :])
                                                      for k in range(KF)]).then_inc(w2_mm, 1)

            attention_out(0, 0, 0)
            attention_out(1, 1, 0, HALVES[0])
            turn(0, range(KD))
            expand(0)
            attention_out(1, 1, 0, HALVES[1])
            contract(0, range(2))
            turn(1, HALVES[0])
            contract(0, range(2, 3))
            turn(1, HALVES[1])
            contract(0, range(3, 4))
            with pe.Fori(0, NCH // 2 - 1) as i:
                for u in range(2):
                    c = 2 * i + 1 + u
                    expand(c)
                    attention_out(c + 1, u, i + 1)
                    contract(c, range(2))
                    turn(c + 1, HALVES[0])
                    contract(c, range(2, 3))
                    turn(c + 1, HALVES[1])
                    contract(c, range(3, 4))
            expand(NCH - 1)
            contract(NCH - 1, range(4))




def build(nc, a, out):
    s = {}
    for name in ("x_hi", "x_lo", "c_hi", "c_lo"):
        s[name] = nc.dram_tensor("scr_" + name, (NCH, P, KD, CH), F16, kind="Internal").ap()
    s["g"] = nc.dram_tensor("scr_g", (NCH, 2 * H0, CH), F16, kind="Internal").ap()
    s["x1"] = nc.dram_tensor("scr_x1", (NCH, P, TPC, D), F32, kind="Internal").ap()
    for name in "qk":
        s[name] = nc.dram_tensor("scr_" + name, (2, KD * NCH, P, CH), F16, kind="Internal").ap()
    s["o"] = nc.dram_tensor("scr_o", (2, KD * NCH, P, CH), F16, kind="Internal").ap()
    s["v"] = nc.dram_tensor("scr_v", (KD * NCH, P, TPC, P), F32, kind="Internal").ap()
    s["ada"] = nc.dram_tensor("scr_ada", (B, NADA), F32, kind="Internal").ap()
    with ExitStack() as stack:
        m = Memory(nc, stack)
        w = {"ident": m.sb("ident", [P, P])}
        for name, shape in (("mod1", [P, 2, KD, B]), ("mod2", [P, 2, KD, B]), ("bqk", [P, 2, KD]), ("bv", [P, KD]),
                            ("b1_ff", [P, FF // P]), ("krows", [P, 1])):
            w[name] = m.sb("col_" + name, shape)
        with ExitStack() as stack_qkv:
            m_qkv = Memory(nc, stack_qkv)
            w["qkv"] = m_qkv.sb("qkv_weights", [P, 6, KD * D], F16)
            for i, name in enumerate(("wq", "wk", "wv")):
                for j, half in enumerate(("hi", "lo")):
                    w[f"{name}_{half}"] = w["qkv"][:, 2 * i + j].rearrange("p (k n) -> p k n", n=D)
            with ExitStack() as stack_0:
                m_0 = Memory(nc, stack_0)
                for name, shape in (("val", [P, KD, HK]), ("f1", [P, KD, D]), ("f2", [P, KD, D]), ("of", [P, KH, D])):
                    for half in ("hi", "lo"):
                        w[f"{name}_{half}"] = m_0.sb(f"{name}_{half}", shape, F16)
                w["sel"] = m_0.sb("sel", [P, KH, P], F16)
                w["b1"] = m_0.sb("b1_columns", [P, KD, NCH])
                phase_prepare(nc, a, s, w)
                phase_layer0(nc, a, s, w)
            for name, shape in (("wo", [P, KD, D]), ("w1", [P, KD, FF]), ("w2", [P, FF // P, D])):
                for half in ("hi", "lo"):
                    w[f"{name}_{half}"] = m_qkv.sb(f"{name}_{half}", shape, F16)
            phase_qkv(nc, a, s, w)
            with ExitStack() as stack_ff:
                m_ff = Memory(nc, stack_ff)
                w["gates"] = m_ff.sb("gates", [P, 2, B, D])
                w["gated_bias"] = m_ff.sb("gated_bias", [P, 2, B, D])
                phase_attention(nc, a, s, w)
                phase_feed_forward(nc, a, s, w, out)


_IN = ['x', 'cond_1024', 'L0_cond_attention_weights', 'L0_cond_temperature', 'L0_cond_values', 'L0_cond_operator',
       'L0_cond_ff1', 'L0_cond_ff1_bias', 'L0_cond_ff2', 'L0_cond_ff2_bias', 'L0_cond_ln_gamma', 'L0_cond_ln_beta',
       'L1_cond_W_ada', 'L1_cond_b_ada', 'L1_cond_Wq', 'L1_cond_bq', 'L1_cond_Wk', 'L1_cond_bk', 'L1_cond_Wv',
       'L1_cond_bv', 'L1_cond_Wo', 'L1_cond_bo', 'L1_cond_W1', 'L1_cond_b1', 'L1_cond_W2', 'L1_cond_b2']


def constants():
    sel = np.zeros((P, KH, P), np.float16)
    for k in range(2 * H0):
        for j in range(KH):
            for c in range(P):
                sel[k, j, c] = (k % H0) == (j * P + c) // K0
    krows = np.zeros((P, 1), np.float32)
    krows[3 * DH:3 * DH + 2, 0] = (WS, 1.0)
    count = np.arange(1, S + 1, dtype=np.float32)
    return {"c_ident": np.eye(P, dtype=np.float32), "c_inv_counts": (1.0 / count).astype(np.float32),
            "c_krows": krows, "c_counts": np.ascontiguousarray(count.reshape(TPB, P).T), "c_sel": sel}


def kernel(**inputs):
    import concourse.bacc as bacc
    from concourse.bass_utils import run_bass_kernel_spmd

    nc = bacc.Bacc("TRN2", target_bir_lowering=False, num_devices=1)
    arrays = {name: np.ascontiguousarray(inputs[name]) for name in _IN}
    arrays.update(constants())
    aps = {}
    for name, v in arrays.items():
        aps[name] = nc.dram_tensor(name + "_in", v.shape, mybir.dt.from_np(v.dtype), kind="ExternalInput").ap()
    out = nc.dram_tensor("out", (B, S, D), F32, kind="ExternalOutput").ap()
    build(nc, aps, out)
    r = run_bass_kernel_spmd(nc, [{name + "_in": v for name, v in arrays.items()}], core_ids=[0])
    return r.results[0]["out"]
```
